# Optimizing a Trainium2 kernel written in Bass

```python
import numpy as np
import jax
import jax.numpy as jnp

def _softmax(x, axis=-1):
    return jax.nn.softmax(x, axis=axis)

def _gelu(x):
    return jax.nn.gelu(x, approximate=True)

def _silu(x):
    return jax.nn.silu(x)

def _sigmoid(x):
    return jax.nn.sigmoid(x)

def _layernorm(x, axis=-1, eps=1e-05):
    m = jnp.mean(x, axis=axis, keepdims=True)
    v = jnp.var(x, axis=axis, keepdims=True)
    return (x - m) / jnp.sqrt(v + eps)

def _scatter_add(tgt, idx, src, axis=0):
    return tgt.at[idx].add(src)

def _segment_sum(src, seg, n):
    return jax.ops.segment_sum(src, seg, n)
kernel_name = 'mk_gnn_resnorm_d4_gnn_r64_21f854'

def setup_inputs(seed: int=0):
    np.random.seed(seed)
    _w = jnp.asarray

    def _rec_inputs():
        import jax
        import jax.numpy as jnp
        _gk = jax.random.key(seed)
        x = -0.000202 + 1 * jax.random.normal(jax.random.fold_in(_gk, 1), (100000, 64), jnp.float32)
        src = jax.random.randint(jax.random.fold_in(_gk, 2), (50000,), 0, 100000, jnp.int32)
        dst = jnp.minimum((100000 * jax.random.uniform(jax.random.fold_in(_gk, 3), (50000,)) ** 2.0).astype(jnp.int32), 99999)
        _o = jnp.argsort(dst, stable=True)
        src = src[_o]
        dst = dst[_o]
        edge_attr_16 = 5.96457e-05 + 0.999887 * jax.random.normal(jax.random.fold_in(_gk, 12), (50000, 16), jnp.float32)
        edge_type_32 = jax.random.randint(jax.random.fold_in(_gk, 14), (50000,), 0, 32, jnp.int32)
        edge_weight = jax.random.uniform(jax.random.fold_in(_gk, 15), (50000,), jnp.float32, 0.0, 1)
        edge_weight_n2 = jax.random.uniform(jax.random.fold_in(_gk, 16), (50000,), jnp.float32, 0.0, 1)
        return (x, src, dst, edge_attr_16, edge_type_32, edge_weight, edge_weight_n2)
    x, src, dst, edge_attr_16, edge_type_32, edge_weight, edge_weight_n2 = _rec_inputs()

    def _L0_gnn_setup():
        import jax, jax.numpy as jnp
        import numpy as np
        from jax.ops import segment_sum
        N = 100000
        P = 25000
        F = 64
        H = 4
        FH = F // H
        key = jax.random.key(seed)
        ks = jax.random.split(key, 8)
        x = jax.random.normal(ks[0], (N, F), dtype=jnp.float32)
        phi_r_cut = jax.random.uniform(ks[1], (P,), dtype=jnp.float32)
        idx_i = jnp.sort(jax.random.randint(ks[2], (P,), 0, N))
        idx_j = jax.random.randint(ks[3], (P,), 0, N)
        pair_mask = jnp.ones((P,), dtype=jnp.float32)
        s = 1.0 / np.sqrt(FH)
        Wq = jax.random.uniform(ks[4], (H, FH, FH), jnp.float32, -s, s)
        Wk = jax.random.uniform(ks[5], (H, FH, FH), jnp.float32, -s, s)
        Wv = jax.random.uniform(ks[6], (H, FH, FH), jnp.float32, -s, s)
        return {'x': x, 'phi_r_cut': phi_r_cut, 'idx_i': idx_i, 'idx_j': idx_j, 'pair_mask': pair_mask, 'Wq': Wq, 'Wk': Wk, 'Wv': Wv}
    _L0_gnn_all = _L0_gnn_setup()
    _L0_gnn_in = {k: v for k, v in _L0_gnn_all.items() if k in ('Wq', 'Wk', 'Wv')}
    del _L0_gnn_all

    def _L1_gnn_setup():
        import jax, jax.numpy as jnp
        import numpy as np
        N, E, D, H, C = (50000, 12500, 64, 2, 64)

        def _transformer_conv(x, src, dst, wq, bq, wk, bk, wv, bv, ws, bs):
            n = x.shape[0]
            q = (x @ wq + bq).reshape(n, H, C)
            k = (x @ wk + bk).reshape(n, H, C)
            v = (x @ wv + bv).reshape(n, H, C)
            qi = q[dst]
            kj = k[src]
            vj = v[src]
            alpha = jnp.einsum('ehc,ehc->eh', qi, kj) / jnp.sqrt(jnp.asarray(C, x.dtype))
            amax = jax.ops.segment_max(alpha, dst, num_segments=n)
            amax = jnp.where(jnp.isfinite(amax), amax, 0.0)
            ex = jnp.exp(alpha - amax[dst])
            denom = jax.ops.segment_sum(ex, dst, num_segments=n)
            a = ex / (denom[dst] + 1e-16)
            out = jax.ops.segment_sum(a[:, :, None] * vj, dst, num_segments=n)
            out = out.mean(axis=1)
            return out + x @ ws + bs
        key = jax.random.key(seed)
        ks = jax.random.split(key, 20)
        x = jax.random.normal(ks[0], (N, D), dtype=jnp.float32)
        edge_index = jax.random.randint(ks[1], (2, E), 0, N, dtype=jnp.int64)
        s = 1.0 / np.sqrt(D)

        def lin(k, din, dout):
            return jax.random.uniform(k, (din, dout), jnp.float32, -s, s)
        inp = {'x': x, 'edge_index': edge_index}
        i = 2
        for l, din in ((1, D), (2, C)):
            for nm, dout in (('wq', H * C), ('wk', H * C), ('wv', H * C), ('ws', C)):
                inp[f'l{l}_{nm}'] = lin(ks[i], din, dout)
                i += 1
                inp[f"l{l}_{nm.replace('w', 'b')}"] = jnp.zeros((dout,), jnp.float32)
        return inp
    _L1_gnn_all = _L1_gnn_setup()
    _L1_gnn_in = {k: v for k, v in _L1_gnn_all.items() if k in ('l1_wq', 'l1_bq', 'l1_wk', 'l1_bk', 'l1_wv', 'l1_bv', 'l1_ws', 'l1_bs', 'l2_wq', 'l2_bq', 'l2_wk', 'l2_bk', 'l2_wv', 'l2_bv', 'l2_ws', 'l2_bs')}
    del _L1_gnn_all

    def _L2_gnn_setup():
        import jax, jax.numpy as jnp
        import numpy as np
        N_NODES = 50000
        N_EDGES = 12500
        IN_F = 64
        OUT_F = 64
        N_REL = 32
        N_BASES = 30
        key = jax.random.key(seed)
        ks = jax.random.split(key, 6)
        x = jax.random.normal(ks[0], (N_NODES, IN_F), dtype=jnp.float32)
        edge_index = jax.random.randint(ks[1], (2, N_EDGES), 0, N_NODES, dtype=jnp.int64)
        edge_type = jax.random.randint(ks[2], (N_EDGES,), 0, N_REL, dtype=jnp.int64)
        basis = jax.random.normal(ks[3], (N_BASES, IN_F, OUT_F), dtype=jnp.float32) * 0.01
        coeff = jax.random.normal(ks[4], (N_REL, N_BASES), dtype=jnp.float32) * 0.01
        self_weight = jax.random.normal(ks[5], (IN_F, OUT_F), dtype=jnp.float32) * 0.01
        bias = jnp.zeros((OUT_F,), dtype=jnp.float32)
        return {'x': x, 'edge_index': edge_index, 'edge_type': edge_type, 'num_nodes': N_NODES, 'basis': basis, 'coeff': coeff, 'self_weight': self_weight, 'bias': bias}
    _L2_gnn_all = _L2_gnn_setup()
    _L2_gnn_in = {k: v for k, v in _L2_gnn_all.items() if k in ('basis', 'coeff', 'self_weight', 'bias')}
    del _L2_gnn_all

    def _L3_gnn_setup():
        import jax, jax.numpy as jnp
        import numpy as np
        N_NODES = 20000
        N_EDGES = 10000
        H = 64
        E_FEAT = 16
        T = 2

        def _gru_cell(a, h, W_ih, W_hh, b_ih, b_hh):
            gi = a @ W_ih.T + b_ih
            gh = h @ W_hh.T + b_hh
            i_r, i_z, i_n = jnp.split(gi, 3, axis=1)
            h_r, h_z, h_n = jnp.split(gh, 3, axis=1)
            r = jax.nn.sigmoid(i_r + h_r)
            z = jax.nn.sigmoid(i_z + h_z)
            n = jnp.tanh(i_n + r * h_n)
            return (1.0 - z) * n + z * h
        key = jax.random.key(seed)
        ks = jax.random.split(key, 10)
        hv = jax.random.normal(ks[0], (N_NODES, H), dtype=jnp.float32)
        e = jax.random.normal(ks[1], (N_EDGES, E_FEAT), dtype=jnp.float32)
        src = jax.random.randint(ks[2], (N_EDGES,), 0, N_NODES, dtype=jnp.int32)
        dst = jax.random.randint(ks[3], (N_EDGES,), 0, N_NODES, dtype=jnp.int32)
        s = 0.1
        W_msg = jax.random.normal(ks[4], (T, 2 * H + E_FEAT, 2 * H), dtype=jnp.float32) * s
        b_msg = jax.random.normal(ks[5], (T, 2 * H), dtype=jnp.float32) * s
        W_ih = jax.random.normal(ks[6], (T, 3 * H, 2 * H), dtype=jnp.float32) * s
        W_hh = jax.random.normal(ks[7], (T, 3 * H, H), dtype=jnp.float32) * s
        b_ih = jax.random.normal(ks[8], (T, 3 * H), dtype=jnp.float32) * s
        b_hh = jax.random.normal(ks[9], (T, 3 * H), dtype=jnp.float32) * s
        return {'hv': hv, 'e': e, 'src': src, 'dst': dst, 'W_msg': W_msg, 'b_msg': b_msg, 'W_ih': W_ih, 'W_hh': W_hh, 'b_ih': b_ih, 'b_hh': b_hh}
    _L3_gnn_all = _L3_gnn_setup()
    _L3_gnn_in = {k: v for k, v in _L3_gnn_all.items() if k in ('W_msg', 'b_msg', 'W_ih', 'W_hh', 'b_ih', 'b_hh')}
    del _L3_gnn_all
    return {'x': x, 'src': src, 'dst': dst, 'edge_attr_16': edge_attr_16, 'edge_type_32': edge_type_32, 'edge_weight': edge_weight, 'edge_weight_n2': edge_weight_n2, 'L0_gnn_Wq': _L0_gnn_in['Wq'], 'L0_gnn_Wk': _L0_gnn_in['Wk'], 'L0_gnn_Wv': _L0_gnn_in['Wv'], 'L1_gnn_l1_wq': _L1_gnn_in['l1_wq'], 'L1_gnn_l1_bq': _L1_gnn_in['l1_bq'], 'L1_gnn_l1_wk': _L1_gnn_in['l1_wk'], 'L1_gnn_l1_bk': _L1_gnn_in['l1_bk'], 'L1_gnn_l1_wv': _L1_gnn_in['l1_wv'], 'L1_gnn_l1_bv': _L1_gnn_in['l1_bv'], 'L1_gnn_l1_ws': _L1_gnn_in['l1_ws'], 'L1_gnn_l1_bs': _L1_gnn_in['l1_bs'], 'L1_gnn_l2_wq': _L1_gnn_in['l2_wq'], 'L1_gnn_l2_bq': _L1_gnn_in['l2_bq'], 'L1_gnn_l2_wk': _L1_gnn_in['l2_wk'], 'L1_gnn_l2_bk': _L1_gnn_in['l2_bk'], 'L1_gnn_l2_wv': _L1_gnn_in['l2_wv'], 'L1_gnn_l2_bv': _L1_gnn_in['l2_bv'], 'L1_gnn_l2_ws': _L1_gnn_in['l2_ws'], 'L1_gnn_l2_bs': _L1_gnn_in['l2_bs'], 'L2_gnn_basis': _L2_gnn_in['basis'], 'L2_gnn_coeff': _L2_gnn_in['coeff'], 'L2_gnn_self_weight': _L2_gnn_in['self_weight'], 'L2_gnn_bias': _L2_gnn_in['bias'], 'L3_gnn_W_msg': _L3_gnn_in['W_msg'], 'L3_gnn_b_msg': _L3_gnn_in['b_msg'], 'L3_gnn_W_ih': _L3_gnn_in['W_ih'], 'L3_gnn_W_hh': _L3_gnn_in['W_hh'], 'L3_gnn_b_ih': _L3_gnn_in['b_ih'], 'L3_gnn_b_hh': _L3_gnn_in['b_hh']}

def reference(x, src, dst, edge_attr_16, edge_type_32, edge_weight, edge_weight_n2, L0_gnn_Wq, L0_gnn_Wk, L0_gnn_Wv, L1_gnn_l1_wq, L1_gnn_l1_bq, L1_gnn_l1_wk, L1_gnn_l1_bk, L1_gnn_l1_wv, L1_gnn_l1_bv, L1_gnn_l1_ws, L1_gnn_l1_bs, L1_gnn_l2_wq, L1_gnn_l2_bq, L1_gnn_l2_wk, L1_gnn_l2_bk, L1_gnn_l2_wv, L1_gnn_l2_bv, L1_gnn_l2_ws, L1_gnn_l2_bs, L2_gnn_basis, L2_gnn_coeff, L2_gnn_self_weight, L2_gnn_bias, L3_gnn_W_msg, L3_gnn_b_msg, L3_gnn_W_ih, L3_gnn_W_hh, L3_gnn_b_ih, L3_gnn_b_hh):
    import jax
    import jax.numpy as jnp

    def _L0_gnn_ref(x, phi_r_cut, idx_i, idx_j, pair_mask, Wq, Wk, Wv):
        import jax, jax.numpy as jnp
        import numpy as np
        from jax.ops import segment_sum
        N = 100000
        P = 25000
        F = 64
        H = 4
        FH = F // H
        n, f = x.shape
        x_heads = x.reshape(n, H, FH)
        q = jnp.einsum('nhf,hfg->nhg', x_heads, Wq)
        k = jnp.einsum('nhf,hfg->nhg', x_heads, Wk)
        v = jnp.einsum('nhf,hfg->nhg', x_heads, Wv)
        alpha = (q[idx_j] * k[idx_j]).sum(axis=-1) / jnp.sqrt(jnp.asarray(FH, x.dtype))
        alpha = alpha * (pair_mask * phi_r_cut)[:, None]
        msg = alpha[:, :, None] * v[idx_j]
        out = segment_sum(msg, segment_ids=idx_i, num_segments=n)
        return out.reshape(n, f)

    def _L1_gnn_ref(x, edge_index, l1_wq, l1_bq, l1_wk, l1_bk, l1_wv, l1_bv, l1_ws, l1_bs, l2_wq, l2_bq, l2_wk, l2_bk, l2_wv, l2_bv, l2_ws, l2_bs):
        import jax, jax.numpy as jnp
        import numpy as np
        N, E, D, H, C = (50000, 12500, 64, 2, 64)

        def _transformer_conv(x, src, dst, wq, bq, wk, bk, wv, bv, ws, bs):
            n = x.shape[0]
            q = (x @ wq + bq).reshape(n, H, C)
            k = (x @ wk + bk).reshape(n, H, C)
            v = (x @ wv + bv).reshape(n, H, C)
            qi = q[dst]
            kj = k[src]
            vj = v[src]
            alpha = jnp.einsum('ehc,ehc->eh', qi, kj) / jnp.sqrt(jnp.asarray(C, x.dtype))
            amax = jax.ops.segment_max(alpha, dst, num_segments=n)
            amax = jnp.where(jnp.isfinite(amax), amax, 0.0)
            ex = jnp.exp(alpha - amax[dst])
            denom = jax.ops.segment_sum(ex, dst, num_segments=n)
            a = ex / (denom[dst] + 1e-16)
            out = jax.ops.segment_sum(a[:, :, None] * vj, dst, num_segments=n)
            out = out.mean(axis=1)
            return out + x @ ws + bs
        src, dst = (edge_index[0], edge_index[1])
        h = _transformer_conv(x, src, dst, l1_wq, l1_bq, l1_wk, l1_bk, l1_wv, l1_bv, l1_ws, l1_bs)
        h = _transformer_conv(h, src, dst, l2_wq, l2_bq, l2_wk, l2_bk, l2_wv, l2_bv, l2_ws, l2_bs)
        return h

    def _L2_gnn_ref(x, edge_index, edge_type, num_nodes, basis, coeff, self_weight, bias):
        import jax, jax.numpy as jnp
        import numpy as np
        N_NODES = 50000
        N_EDGES = 12500
        IN_F = 64
        OUT_F = 64
        N_REL = 32
        N_BASES = 30
        rel_weight = jnp.einsum('rb,bio->rio', coeff, basis)
        source_idx = edge_index[0]
        target_idx = edge_index[1]
        src_feats = x[source_idx]

        def body(out, rw_r):
            rw, r = rw_r
            mask = (edge_type == r).astype(jnp.float32)
            msg = src_feats @ rw * mask[:, None]
            return (out.at[target_idx].add(msg), None)
        out0 = jnp.zeros((num_nodes, rel_weight.shape[-1]), dtype=jnp.float32)
        out, _ = jax.lax.scan(body, out0, (rel_weight, jnp.arange(rel_weight.shape[0])))
        in_degree = jnp.zeros((num_nodes,), dtype=jnp.float32).at[target_idx].add(1.0)
        in_degree = jnp.maximum(in_degree, 1.0)
        out = out / in_degree[:, None]
        out = out + x @ self_weight + bias
        return out

    def _L3_gnn_ref(hv, e, src, dst, W_msg, b_msg, W_ih, W_hh, b_ih, b_hh):
        import jax, jax.numpy as jnp
        import numpy as np
        N_NODES = 20000
        N_EDGES = 10000
        H = 64
        E_FEAT = 16
        T = 2

        def _gru_cell(a, h, W_ih, W_hh, b_ih, b_hh):
            gi = a @ W_ih.T + b_ih
            gh = h @ W_hh.T + b_hh
            i_r, i_z, i_n = jnp.split(gi, 3, axis=1)
            h_r, h_z, h_n = jnp.split(gh, 3, axis=1)
            r = jax.nn.sigmoid(i_r + h_r)
            z = jax.nn.sigmoid(i_z + h_z)
            n = jnp.tanh(i_n + r * h_n)
            return (1.0 - z) * n + z * h
        num_nodes = hv.shape[0]
        num_rounds = W_msg.shape[0]
        for t in range(num_rounds):
            msg_in = jnp.concatenate([hv[dst], hv[src], e], axis=1)
            msgs = msg_in @ W_msg[t] + b_msg[t]
            a = jax.ops.segment_sum(msgs, dst, num_segments=num_nodes)
            hv = _gru_cell(a, hv, W_ih[t], W_hh[t], b_ih[t], b_hh[t])
        return hv
    edge_index = jnp.stack([src, dst])
    x = _layernorm(x + _L0_gnn_ref(x, edge_weight, src, dst, edge_weight_n2, L0_gnn_Wq, L0_gnn_Wk, L0_gnn_Wv), axis=-1)
    x = _layernorm(x + _L1_gnn_ref(x, edge_index, L1_gnn_l1_wq, L1_gnn_l1_bq, L1_gnn_l1_wk, L1_gnn_l1_bk, L1_gnn_l1_wv, L1_gnn_l1_bv, L1_gnn_l1_ws, L1_gnn_l1_bs, L1_gnn_l2_wq, L1_gnn_l2_bq, L1_gnn_l2_wk, L1_gnn_l2_bk, L1_gnn_l2_wv, L1_gnn_l2_bv, L1_gnn_l2_ws, L1_gnn_l2_bs), axis=-1)
    x = _layernorm(x + _L2_gnn_ref(x, edge_index, edge_type_32, 100000, L2_gnn_basis, L2_gnn_coeff, L2_gnn_self_weight, L2_gnn_bias), axis=-1)
    x = _layernorm(x + _L3_gnn_ref(x, edge_attr_16, src, dst, L3_gnn_W_msg, L3_gnn_b_msg, L3_gnn_W_ih, L3_gnn_W_hh, L3_gnn_b_ih, L3_gnn_b_hh), axis=-1)
    return x

_drawn_inputs = setup_inputs


def setup_inputs(seed=0):
    import zlib

    import numpy as np

    out = dict(_drawn_inputs(seed))
    spreads = {'L1_gnn_l1_bq': (0.0, 0.8),
     'L1_gnn_l1_bk': (0.0, 2.0),
     'L1_gnn_l1_bv': (0.0, 0.335),
     'L1_gnn_l1_bs': (0.0, 0.1),
     'L1_gnn_l2_bq': (0.0, 2.0),
     'L1_gnn_l2_bk': (0.0, 2.0),
     'L1_gnn_l2_bv': (0.0, 0.1),
     'L1_gnn_l2_bs': (0.0, 0.1),
     'L2_gnn_bias': (0.0, 0.1)}
    factors = {'L1_gnn_l1_wq': 4.501,
     'L1_gnn_l1_wk': 4.427,
     'L1_gnn_l2_wq': 8.0,
     'L1_gnn_l2_wk': 8.0,
     'L2_gnn_basis': 8.0,
     'L2_gnn_coeff': 8.0}
    for name, (base, spread) in spreads.items():
        noise = np.random.default_rng([zlib.crc32(name.encode()), seed]).standard_normal(out[name].shape)
        drawn = base * np.exp(spread * noise) if base else spread * noise
        out[name] = jnp.asarray(drawn.astype(out[name].dtype))
    for name, factor in factors.items():
        out[name] = (out[name] * factor).astype(out[name].dtype)
    return out
```

```python
from contextlib import ExitStack

import concourse.bass as bass
from concourse import mybir

F32 = mybir.dt.float32
I32 = mybir.dt.int32
ALU = mybir.AluOpType
ACT = mybir.ActivationFunctionType
AX = mybir.AxisListType.X

P = 128
SLOTS = 4
GROUP = P * SLOTS
ROWS = 8
CHUNK = P * ROWS
CROWS = 4
CCHUNK = P * CROWS
BIG = 1e30
NOWHERE = 1 << 20
EPS = 1e-5
META = 8
M_SRC, M_DST, M_LAST, M_W, M_SRCF, M_DSTF, M_RDEG, M_TYPE = range(META)
PEEL = 2
NEWTON = 3
ROOT_STEPS = 2 + 4 * NEWTON
RANK_CHUNK = 896
ZCOLS = 3584


def wait(eng, sem, value):
    if isinstance(value, int) and value <= 0:
        return
    eng.wait_ge(sem, value)


def pipeline(eng, iters, unroll, *stages):
    stages = [s if isinstance(s, tuple) else (n, s) for n, s in enumerate(stages)]

    def step(i, u):
        for d, stage in stages:
            back = -((u - d) // unroll)
            at = i - back
            if isinstance(at, int) and not 0 <= at < iters:
                continue
            stage(at, u - d + back * unroll)

    for i in range(PEEL):
        for u in range(unroll):
            step(i, u)
    with eng.Fori(PEEL, iters) as i:
        for u in range(unroll):
            step(i, u)
    for t in range(max(d for d, _ in stages)):
        step(iters + t // unroll, t % unroll)


class Steps:

    def __init__(self, eng, sem):
        self.eng, self.sem, self.n = eng, sem, 0

    def __call__(self, ins):
        self.n += 1
        ins.then_inc(self.sem, 1)
        self.eng.wait_ge(self.sem, self.n)


def gnn_kernel(nc, x, src, dst, attr, etype, ew, ew2, Wq0, Wk0, Wv0, wq, bq, wk, bk, wv, bv, ws, bs,
               basis, coeff, self_w, rel_bias, Wmsg, bmsg, Wih, Whh, bih, bhh, out):
    N, D = x.shape
    E = src.shape[0]
    NA = attr.shape[1]
    H0, FH = Wq0.shape[0], Wq0.shape[1]
    H1 = wq[0].shape[1] // D
    NREL, NB = coeff.shape
    NPAIR = NREL // 2
    GI = 3 * D
    NG = -(-E // GROUP)
    NG += NG % 2
    EP = NG * GROUP
    EC = EP // P
    NCH = -(-N // CHUNK)
    NCH += NCH % 2
    NP = NCH * CHUNK
    NCC = NP // CCHUNK
    NI, CI, CCI = NG // 2, NCH // 2, NCC // 4
    AW = D + 32
    EW = D + NA + 1
    PARTS, REST = E // EC, E % EC
    LAST_PARTS = (N - (NCH - 1) * CHUNK) // ROWS
    C_FULL, C_PARTS = N // CCHUNK, N % CCHUNK // CROWS
    NBC = D * D // 512
    assert (N - (NCH - 1) * CHUNK) % ROWS == 0 and 0 < LAST_PARTS <= P and N % CROWS == 0
    assert D == 64 and H0 * FH == D and H1 * D == P and NA == 16 and NCC % 4 == 0 and REST > 1
    assert N + NOWHERE < 1 << 24 and EP % RANK_CHUNK == 0 and NP * D % (P * ZCOLS) == 0

    ctx = ExitStack()
    with ctx:
        prep_only = ExitStack()

        def sb(name, shape, dt=F32, life=ctx):
            return life.enter_context(nc.sbuf_tensor(name, shape, dt))

        def sem(name):
            return ctx.enter_context(nc.semaphore(name))

        def pair(name, shape, dt=F32, n=2):
            return [sb(f"{name}{k}", shape, dt) for k in range(n)]

        def sems(name, n=2):
            return [sem(f"{name}{k}") for k in range(n)]

        def dram(name, shape, dt=F32):
            return nc.dram_tensor(name, shape, dt).ap()

        x1, h1, x2, x3, v1 = (dram(n, (NP, D)) for n in ("x1", "h1", "x2", "x3", "v1"))
        agg0 = dram("agg0", (NP + GROUP, D))
        agg = dram("agg", (NP, D))
        aggw = dram("aggw", (NP, AW))
        meta_d, attr_d = dram("meta_d", (EP, META)), dram("attr_d", (EP, NA))
        srec_d, satt_d, key_d = dram("srec_d", (EP, META)), dram("satt_d", (EP, NA)), dram("key_d", (EP,))
        srcf_d, type_d, same_d = (dram(n, (EP,)) for n in ("srcf_d", "type_d", "same_d"))
        tgt_d = dram("tgt_d", (EP + 2,))
        logit_d, coef_d = dram("logit_d", (H1, EP)), dram("coef_d", (H1, EP))
        xst_d = dram("xst_d", (NG, D, GROUP))
        relw_d = dram("relw_d", (NREL, D * D))

        ident = sb("ident", [P, P])
        later = sb("later", [P, SLOTS, GROUP])
        trash = sb("trash", [P, SLOTS])
        ones_row, ones_col = sb("ones_row", [1, P]), sb("ones_col", [P, 1])
        stops = sb("stops", [1, 2])
        zeros = sb("zeros", [P, ZCOLS])
        qkv_w = sb("qkv_w", [D, 3 * D])
        wk_t, wq_t = pair("wk_t", [P, P]), pair("wq_t", [P, P])
        wv_t = pair("wv_t", [D, P])
        bias_t = sb("bias_t", [P, 2, 3])
        head_sum = sb("head_sum", [P, H1])
        head_mean = sb("head_mean", [P, D])
        lin_w = pair("lin_w", [P, P], n=3)
        lin_b = pair("lin_b", [1, ROWS * D], n=3)
        basis_t, relw_t = sb("basis_t", [NB, D * D]), sb("relw_t", [NREL, D * D])
        coeff_t, coeffT = sb("coeff_t", [NREL, NB]), sb("coeffT", [NB, NREL])
        rel_w = sb("rel_w", [P, NPAIR, D])
        rel_id = sb("rel_id", [P, NPAIR])
        raw_w = sb("raw_w", [P, 4, P])
        raw_h = sb("raw_h", [P, 2, D])
        turned_w = sb("turned_w", [P, 2, GI])
        whhT = pair("whhT", [D, GI])
        gate_w = pair("gate_w", [P, GI])
        gate_v = pair("gate_v", [96, 4 * D])

        roww = pair("roww", [P, SLOTS, AW])
        scan = pair("scan", [P, GROUP])
        cell_in = pair("cell_in", [P, CROWS, D + AW + D], n=4)
        psame, nsame, pneg, nneg = (sb(n, [P, EC]) for n in ("psame", "nsame", "pneg", "nneg"))
        ends2 = sb("ends2", [P, 4, H1])
        ends_row = sb("ends_row", [H1, 4, P])
        flag, flag_i = sb("flag", [P, 1]), sb("flag_i", [1, 1], I32)
        sc_a, sc_b, sc_c = (sb(n, [P, H1, EC]) for n in ("sc_a", "sc_b", "sc_c"))
        end_col, in_col = sb("end_col", [P, H1]), sb("in_col", [P, H1])
        end_row, in_row = sb("end_row", [H1, P]), sb("in_row", [H1, P + 1])

        def once(name, shape, dt=F32):
            return sb(name, shape, dt, prep_only)

        src_i, dst_i, next_i, type_i = (once(n, [P, EC], I32) for n in ("src_i", "dst_i", "next_i", "type_i"))
        w1_t, w2_t = once("w1_t", [P, EC]), once("w2_t", [P, EC])
        rec = once("rec", [P, EC, META])
        att = once("att", [P, EC, NA])
        colf = once("colf", [P, 5, EC])

        s_key, s_pos, s_lt, s_eq = (once(n, [P, RANK_CHUNK]) for n in ("s_key", "s_pos", "s_lt", "s_eq"))
        s_cur, s_cnt = once("s_cur", [P, 3]), once("s_cnt", [P, 2])
        s_posc, s_rank = once("s_posc", [P, EC]), once("s_rank", [P, EC])
        s_rec, s_att, s_idx = once("s_rec", [P, META]), once("s_att", [P, NA]), once("s_idx", [P, 1], I32)
        prep_only.close()

        edge_only = ExitStack()

        def esb(name, shape, dt=F32):
            return sb(name, shape, dt, edge_only)

        def epair(name, shape, dt=F32, n=2):
            return [esb(f"{name}{k}", shape, dt) for k in range(n)]

        meta = epair("meta", [P, SLOTS, META])
        rowb = epair("rowb", [P, GROUP])
        sameb = epair("sameb", [P, GROUP])
        rows = epair("rows", [P, SLOTS, P])
        turn = epair("turn", [P, GROUP])
        fmaj = epair("fmaj", [P, GROUP])
        prod = epair("prod", [P, GROUP])
        outr = epair("outr", [P, SLOTS, AW])
        outd = epair("outd", [P, SLOTS, D])
        idx = epair("idx", [P, SLOTS], I32)
        eq = epair("eq", [P, SLOTS, GROUP])
        junk = esb("junk", [P, SLOTS, GROUP])
        cnt, gap, shift = epair("cnt", [P, SLOTS]), epair("gap", [P, SLOTS]), epair("shift", [P, SLOTS])
        q_t, qk_t, msg_t = epair("q_t", [P, SLOTS, D]), epair("qk_t", [P, SLOTS, D]), epair("msg_t", [P, SLOTS, D])
        al_t, aw_t = epair("al_t", [P, SLOTS, H0]), epair("aw_t", [P, SLOTS, H0])
        logit = epair("logit", [H1, GROUP])
        masked = epair("masked", [P, GROUP], n=4)

        edge_only.close()

        node_a, node_g, node_r = (pair(n, [P, ROWS, D]) for n in ("node_a", "node_g", "node_r"))
        node_t, node_p, node_y = (pair(n, [P, ROWS, D]) for n in ("node_t", "node_p", "node_y"))
        node_c, node_q, node_o = (pair(n, [P, ROWS, D]) for n in ("node_c", "node_q", "node_o"))
        node_s, node_v, node_i = (pair(n, [P, ROWS]) for n in ("node_s", "node_v", "node_i"))
        cell_t, cell_u = pair("cell_t", [P, CROWS * P]), pair("cell_u", [96, CROWS * P])
        cell_rz = pair("cell_rz", [P, CROWS, 2 * D])
        H_AT, S_AT, E_AT, DEG_AT = D + AW, D, 2 * D, 2 * D + NA

        ps = ctx.enter_context(nc.psum_tensor("ps", [P, 8, 512], F32))

        phase_done, passed = sem("phase_done"), sem("passed")
        ends_of = {}

        def phase_end(eng, name):
            n = ends_of.setdefault(name, len(ends_of) + 1)
            eng.drain().then_inc(phase_done, 1)
            eng.wait_ge(phase_done, 5 * n)

        def steady(eng):
            eng.sem_inc(passed, 1)

        def spread(flat, parts):
            return flat.unsqueeze(0).broadcast_to([parts, flat.shape[0]])

        def group_of(flat, i, k):
            return flat[bass.ds((2 * i + k) * GROUP, GROUP)]

        def to_row(t, n=GROUP):
            return t.rearrange("f (j p) -> f p j", j=SLOTS)

        def in_order(t):
            return t.rearrange("f (p j) -> f p j", j=SLOTS)

        def slot_of(t, j):
            return t.rearrange("f (p j) -> f j p", j=SLOTS)[:, j, :]

        const_ready, in_ready, w_ready, dve_step = (sem(n) for n in ("const_ready", "in_ready", "w_ready", "dve_step"))
        raw_ready, pe_turned, act_moved, rel_stored = (
            sem(n) for n in ("raw_ready", "pe_turned", "act_moved", "rel_stored"))
        w_late = sem("w_late")
        agg0_zero, tables_zero = sem("agg0_zero"), sem("tables_zero")
        flag_sum, flag_set = sem("flag_sum"), sem("flag_set")
        sort_key, sort_in, sort_counted, sort_staged, sort_put, sort_back = (
            sem(n) for n in ("sort_key", "sort_in", "sort_counted", "sort_staged", "sort_put", "sort_back"))
        tgt_stored, tgt_in, recs_stored = sem("tgt_stored"), sem("tgt_in"), sem("recs_stored")
        end_ready, end_turned = sem("end_ready"), sem("end_turned")
        said = {}

        def consts(pool):
            g = nc.gpsimd
            n = [0]

            def const(ins):
                n[0] += 1
                ins.then_inc(const_ready, 1)
                pool.wait_ge(const_ready, n[0])

            const(g.memset(zeros[:], 0.0))
            blank = [(ident, 0.0), (later, 1.0), (ones_row, 1.0), (ones_col, 1.0), (qkv_w, 0.0), (head_sum, 0.0)]
            blank += [(t, 0.0) for t in wk_t + wq_t + gate_v + lin_w + roww + cell_in + scan]
            blank += [(dst_i, N), (next_i, N), (src_i, 0), (type_i, 0), (w1_t, 0.0), (w2_t, 0.0), (att, 0.0)]
            for t, v in blank:
                const(g.memset(t[:], v))
            const(g.memset(stops[0:1, 0:1], -1.0))
            const(g.memset(stops[0:1, 1:2], -2.0))
            said["blank"] = n[0]
            const(g.affine_select(out=ident[:], in_=ident[:], compare_op=ALU.not_equal, fill=1.0, base=0,
                                  pattern=[[-1, P]], channel_multiplier=1))
            const(g.affine_select(out=later[:], in_=later[:], compare_op=ALU.is_gt, fill=0.0, base=0,
                                  pattern=[[-1, SLOTS], [1, GROUP]], channel_multiplier=-SLOTS))
            const(g.memset(head_sum[0:D, 0:1], float(D) ** -0.5))
            const(g.memset(head_sum[D:P, 1:2], float(D) ** -0.5))
            const(g.iota(trash[:], pattern=[[1, SLOTS]], base=NP, channel_multiplier=SLOTS,
                         allow_small_or_imprecise_dtypes=True))
            const(g.iota(rel_id[0:D, :], pattern=[[2, NPAIR]], base=0, channel_multiplier=0,
                         allow_small_or_imprecise_dtypes=True))
            const(g.iota(rel_id[D:P, :], pattern=[[2, NPAIR]], base=1, channel_multiplier=0,
                         allow_small_or_imprecise_dtypes=True))
            for t in roww:
                const(g.memset(t[:, :, D + NA:D + NA + 1], 1.0))
            for t in cell_in:
                const(g.memset(t[:, :, DEG_AT + 1:DEG_AT + 3], 1.0))
            said["const"] = n[0]

        N_LOADS = 14

        def prep_sync(sp):
            sp.wait_ge(const_ready, said["blank"])
            for t, flat, at in ((dst_i, dst, 0), (src_i, src, 0), (type_i, etype, 0), (w1_t, ew, 0),
                                (w2_t, ew2, 0), (next_i, dst, 1)):
                sp.dma_start(t[0:PARTS, :], flat[at:at + PARTS * EC].rearrange("(p c) -> p c", c=EC)) \
                  .then_inc(in_ready, 16)
                sp.dma_start(t[PARTS:PARTS + 1, 0:REST - at], flat[at + PARTS * EC:E].unsqueeze(0)) \
                  .then_inc(in_ready, 16)
            sp.dma_start(att[0:PARTS, :, :], attr[0:PARTS * EC, :].rearrange("(p c) a -> p c a", c=EC)) \
              .then_inc(in_ready, 16)
            sp.dma_start(att[PARTS:PARTS + 1, 0:REST, :], attr[PARTS * EC:E, :].unsqueeze(0)).then_inc(in_ready, 16)
            n = [0]

            def put(to, of):
                n[0] += 1
                with nc.allow_non_contiguous_dma(reason="small weights"):
                    sp.dma_start(to, of).then_inc(w_ready, 16)

            put(basis_t[:], basis.rearrange("b i o -> b (i o)"))
            put(coeff_t[:], coeff[:, :])
            for m, w in enumerate((Wq0, Wk0, Wv0)):
                for h in range(H0):
                    put(qkv_w[h * FH:(h + 1) * FH, m * D + h * FH:m * D + (h + 1) * FH], w[h])
            for r in range(2):
                put(wk_t[r][0:D, :], wk[r][:, :])
                put(wq_t[r][D:P, :], wq[r][:, :])
                put(wv_t[r][:], wv[r][:, :])
                for m, b in enumerate((bk[r], bq[r], bv[r])):
                    put(bias_t[:, r, m:m + 1], b.unsqueeze(1))
                put(gate_v[r][NA + 1:NA + 2, 0:GI], bih[r:r + 1, :])
                put(gate_v[r][NA + 2:NA + 3, 0:2 * D], bhh[r:r + 1, 0:2 * D])
                put(gate_v[r][NA + 2:NA + 3, GI:GI + D], bhh[r:r + 1, 2 * D:GI])
            for m, (w, b) in enumerate(((ws[0], bs[0]), (ws[1], bs[1]), (self_w, rel_bias))):
                put(lin_w[m][0:D, 0:D], w[:, :])
                put(lin_w[m][D:P, D:P], w[:, :])
                for c in range(ROWS):
                    put(lin_b[m][0:1, c * D:(c + 1) * D], b.unsqueeze(0))
            said["weights"] = n[0]
            for r in range(2):
                if r:
                    sp.wait_ge(pe_turned, 1)
                for to, of in ((raw_w[:, 0, :], Wih[r, 0:P, :]), (raw_w[0:GI - P, 1, :], Wih[r, P:GI, :]),
                               (raw_w[:, 2, :], Wmsg[r, 0:P, :]), (raw_w[0:NA, 3, :], Wmsg[r, P:P + NA, :]),
                               (raw_w[NA:NA + 1, 3, :], bmsg[r:r + 1, :]),
                               (raw_h[:, 0, :], Whh[r, 0:P, :]), (raw_h[0:GI - P, 1, :], Whh[r, P:GI, :])):
                    sp.dma_start(to, of).then_inc(raw_ready, 16)
            for r in range(2):
                sp.wait_ge(act_moved, 2 * r + 1)
                sp.dma_start(gate_v[r][32:96, 0:2 * D], whhT[r][:, 0:2 * D]).then_inc(w_late, 16)
                sp.dma_start(gate_v[r][32:96, GI:GI + D], whhT[r][:, 2 * D:GI]).then_inc(w_late, 16)
            sp.wait_ge(act_moved, 5 + NBC)
            sp.dma_start(relw_d[:, :], relw_t[:]).then_inc(rel_stored, 16)
            sp.wait_ge(rel_stored, 16)
            by_pair = relw_d.rearrange("(m t) (i o) -> t i m o", t=2, o=D)
            sp.dma_start(rel_w[0:D, :, :], by_pair[0]).then_inc(w_late, 16)
            sp.dma_start(rel_w[D:P, :, :], by_pair[1]).then_inc(w_late, 16)
            sp.wait_ge(w_late, 16 * 6)

        def prep_tensor(pe):
            t = nc.tensor
            pe.wait_ge(const_ready, said["const"])
            for r in range(2):
                pe.wait_ge(raw_ready, 16 * 7 * (r + 1))
                if r:
                    pe.wait_ge(act_moved, 2)
                t.transpose(ps[:, 0, 0:P], raw_w[:, 0, :], ident[:])
                t.transpose(ps[:, 0, P:GI], raw_w[0:GI - P, 1, :], ident[0:GI - P, 0:GI - P])
                t.transpose(ps[:, 1, 0:P], raw_w[:, 2, :], ident[:])
                t.transpose(ps[:, 1, P:P + NA + 1], raw_w[0:NA + 1, 3, :], ident[0:NA + 1, 0:NA + 1])
                t.transpose(ps[0:D, 2, 0:P], raw_h[:, 0, :], ident[:])
                t.transpose(ps[0:D, 2, P:GI], raw_h[0:GI - P, 1, :], ident[0:GI - P, 0:GI - P]) \
                 .then_inc(pe_turned, 1)
                pe.wait_ge(act_moved, 2 * r + 1)
                t.matmul(ps[:, 3, 0:GI], turned_w[:, 1, 0:P], turned_w[:, 0, :], start=True, stop=True)
                t.matmul(ps[0:NA + 1, 4, 0:GI], turned_w[:, 1, P:P + NA + 1], turned_w[:, 0, :],
                         start=True, stop=True).then_inc(pe_turned, 1)
            pe.wait_ge(w_ready, 16 * said["weights"])
            t.transpose(ps[0:NB, 5, 0:NREL], coeff_t[:], ident[0:NREL, 0:NREL]).then_inc(pe_turned, 1)
            pe.wait_ge(act_moved, 5)
            for c in range(NBC):
                if c >= 2:
                    pe.wait_ge(act_moved, 5 + c - 1)
                t.matmul(ps[0:NREL, 6 + c % 2, :], coeffT[:], basis_t[:, 512 * c:512 * (c + 1)],
                         start=True, stop=True).then_inc(pe_turned, 1)
            pe.wait_ge(dve_step, said["flag"])
            t.matmul(ps[0:1, 5, 0:1], flag[:], ones_col[:], start=True, stop=True).then_inc(flag_sum, 1)

        def prep_scalar(act):
            a = nc.scalar
            act.wait_ge(const_ready, 1)
            for table, zero in ((agg0[0:NP, :], agg0_zero), (agg, tables_zero), (aggw, tables_zero)):
                flat = table.rearrange("(p c) d -> p (c d)", p=P)
                for c in range(flat.shape[1] // ZCOLS):
                    act.dma_start(flat[:, ZCOLS * c:ZCOLS * (c + 1)], zeros[:]).then_inc(zero, 16)
            act.dma_start(agg0[NP:NP + GROUP, :].rearrange("(p c) d -> p (c d)", p=P),
                          zeros[:, 0:SLOTS * D]).then_inc(agg0_zero, 16)
            for r in range(2):
                act.wait_ge(pe_turned, 2 * r + 1)
                if r:
                    act.wait_ge(pe_turned, 2)
                a.copy(turned_w[:, 0, :], ps[:, 0, 0:GI])
                a.copy(turned_w[:, 1, 0:P + NA + 1], ps[:, 1, 0:P + NA + 1])
                a.copy(whhT[r][:], ps[0:D, 2, 0:GI]).then_inc(act_moved, 1)
                act.wait_ge(pe_turned, 2 * r + 2)
                a.copy(gate_w[r][:], ps[:, 3, 0:GI])
                a.copy(gate_v[r][0:NA + 1, 0:GI], ps[0:NA + 1, 4, 0:GI]).then_inc(act_moved, 1)
            act.wait_ge(pe_turned, 5)
            a.copy(coeffT[:], ps[0:NB, 5, 0:NREL]).then_inc(act_moved, 1)
            for c in range(NBC):
                act.wait_ge(pe_turned, 6 + c)
                a.copy(relw_t[:, 512 * c:512 * (c + 1)], ps[0:NREL, 6 + c % 2, :]).then_inc(act_moved, 1)

        rec_i = rec[:].bitcast(I32)

        def prep_vector(dve, st):
            v = nc.vector
            dve.wait_ge(const_ready, said["const"])
            st(v.tensor_tensor(head_mean[:], ident[:, 0:D], ident[:, D:P], ALU.add))
            st(v.tensor_scalar(head_mean[:], head_mean[:], 1.0 / H1, None, ALU.mult))
            dve.wait_ge(in_ready, 16 * N_LOADS)
            st(v.tensor_tensor(rec[:, :, M_W], w1_t[:], w2_t[:], ALU.mult))
            st(v.tensor_copy(rec[:, :, M_SRCF], src_i[:]))
            st(v.tensor_copy(rec[:, :, M_DSTF], dst_i[:]))
            st(v.tensor_copy(rec[:, :, M_TYPE], type_i[:]))
            st(v.tensor_copy(rec_i[:, :, M_SRC], src_i[:]))
            st(v.tensor_copy(rec_i[:, :, M_DST], dst_i[:]))
            st(v.tensor_copy(rec_i[:, :, M_LAST], dst_i[:]))
            st(v.memset(rec[:, :, M_RDEG], 0.0))
            st(v.tensor_tensor(colf[:, 0, :], dst_i[:], next_i[:], ALU.is_gt))
            st(v.tensor_reduce(flag[:], colf[:, 0, :], AX, ALU.add))
            said["flag"] = st.n
            dve.wait_ge(flag_sum, 1)
            v.tensor_copy(flag_i[:], ps[0:1, 5, 0:1]).then_inc(flag_set, 1)

        def unsorted(eng):
            eng.wait_ge(flag_set, 1)
            return eng.If(eng.value_load(flag_i[0:1, 0:1]) > 0)

        def sort_sync(sp):
            with unsorted(sp):
                sp.wait_ge(sort_counted, 1)
                sp.dma_start(key_d.rearrange("(p c) -> p c", c=EC), colf[:, 1, :]).then_inc(sort_key, 16)
                sp.wait_ge(sort_key, 16)
                with sp.Fori(0, EP // RANK_CHUNK) as c:
                    sp.wait_ge(sort_counted, c + 1)
                    sp.dma_start(s_key[:], spread(key_d[bass.ds(c * RANK_CHUNK, RANK_CHUNK)], P)) \
                      .then_inc(sort_in, 16)
                sp.wait_ge(sort_put, 32 * EC)
                sp.dma_start(rec[:], srec_d.rearrange("(p c) k -> p c k", c=EC)).then_inc(sort_back, 16)
                sp.dma_start(att[:], satt_d.rearrange("(p c) k -> p c k", c=EC)).then_inc(sort_back, 16)
                sp.wait_ge(sort_back, 32)

        def sort_gpsimd(pool):
            with unsorted(pool):
                nc.gpsimd.iota(s_pos[:], pattern=[[1, RANK_CHUNK]], base=0, channel_multiplier=0,
                               allow_small_or_imprecise_dtypes=True).then_inc(sort_key2, 1)
                nc.gpsimd.iota(s_posc[:], pattern=[[1, EC]], base=0, channel_multiplier=EC,
                               allow_small_or_imprecise_dtypes=True).then_inc(sort_key2, 1)
                with pool.Fori(0, EC) as c:
                    pool.wait_ge(sort_staged, c + 1)
                    steady(pool)
                    for table, of in ((srec_d, s_rec), (satt_d, s_att)):
                        nc.gpsimd.indirect_dma_start(table[:, :], bass.IndirectOffsetOnAxis(ap=s_idx[:, 0:1], axis=0),
                                                     of[:], None).then_inc(sort_put, 16)

        sort_key2 = sem("sort_key2")

        def sort_vector(dve):
            v = nc.vector
            with unsorted(dve):
                v.memset(s_rank[:], 0.0)
                v.tensor_copy(colf[:, 1, :], dst_i[:]).then_inc(sort_counted, 1)
                dve.wait_ge(sort_key2, 2)
                with dve.Fori(0, EP // RANK_CHUNK) as c:
                    dve.wait_ge(sort_in, 16 * c + 16)
                    steady(dve)
                    with dve.Fori(0, EC) as e:
                        v.tensor_copy(s_cur[:, 0:1], colf[:, 1, bass.ds(e, 1)])
                        v.tensor_copy(s_cur[:, 1:2], s_posc[:, bass.ds(e, 1)])
                        v.tensor_copy(s_cur[:, 2:3], s_rank[:, bass.ds(e, 1)])
                        v.drain()
                        v.tensor_scalar(s_lt[:], s_key[:], s_cur[:, 0:1], s_cur[:, 2:3], ALU.is_lt, ALU.add,
                                        accum_out=s_cnt[:, 0:1])
                        v.tensor_scalar(s_eq[:], s_pos[:], s_cur[:, 1:2], None, ALU.is_lt)
                        v.drain()
                        v.scalar_tensor_tensor(s_lt[:], s_key[:], s_cur[:, 0:1], s_eq[:], ALU.is_equal, ALU.mult)
                        v.drain()
                        v.tensor_reduce(s_cnt[:, 1:2], s_lt[:], AX, ALU.add)
                        v.drain()
                        v.tensor_tensor(s_rank[:, bass.ds(e, 1)], s_cnt[:, 0:1], s_cnt[:, 1:2], ALU.add)
                        v.drain()
                    v.tensor_scalar(s_posc[:], s_posc[:], float(-RANK_CHUNK), None, ALU.add)
                    v.drain().then_inc(sort_counted, 1)
                with dve.Fori(0, EC) as e:
                    v.tensor_copy(s_rec[:], rec[:, bass.ds(e, 1), :].rearrange("p o k -> p (o k)"))
                    v.tensor_copy(s_att[:], att[:, bass.ds(e, 1), :].rearrange("p o k -> p (o k)"))
                    v.tensor_copy(s_idx[:], s_rank[:, bass.ds(e, 1)])
                    v.drain().then_inc(sort_staged, 1)
                    dve.wait_ge(sort_put, 32 * e + 32)
                dve.wait_ge(sort_back, 32)

        def seg_scan(dve, n, to, keep, of, op0, op1, start, kind, forward):
            v = nc.vector
            way = slice(None) if forward else slice(None, None, -1)
            last = EC - 1 if forward else 0

            def inside(first):
                for h in range(H1):
                    v.tensor_tensor_scan(to[:, h, way], keep[:, way], of[:, h, way],
                                         start if first else in_col[:, h:h + 1], op0, op1).then_inc(scan_step, 1)
                scan_n[0] += H1
                dve.wait_ge(scan_step, scan_n[0])

            inside(True)
            v.tensor_copy(end_col[:], to[:, :, last]).then_inc(end_ready, 1)
            dve.wait_ge(end_turned, 2 * n + 1)
            v.tensor_copy(end_row[:], ps[0:H1, 7, 0:P]).then_inc(scan_step, 1)
            v.memset(in_row[:], start).then_inc(scan_step, 1)
            scan_n[0] += 2
            dve.wait_ge(scan_step, scan_n[0])
            row = in_row[:, 1:P + 1] if forward else in_row[:, 0:P]
            v.tensor_tensor_scan(row[:, way], ends_row[:, kind, way], end_row[:, way], start, op0, op1) \
             .then_inc(end_ready, 1)
            dve.wait_ge(end_turned, 2 * n + 2)
            v.tensor_copy(in_col[:], ps[:, 6, 0:H1]).then_inc(scan_step, 1)
            scan_n[0] += 1
            dve.wait_ge(scan_step, scan_n[0])
            inside(False)

        scan_step = sem("scan_step")
        scan_n = [0]

        def seg_scan_tensor(pe, n, forward):
            pe.wait_ge(end_ready, 2 * n + 1)
            nc.tensor.transpose(ps[0:H1, 7, 0:P], end_col[:], ident[:]).then_inc(end_turned, 1)
            pe.wait_ge(end_ready, 2 * n + 2)
            row = in_row[:, 0:P] if forward else in_row[:, 1:P + 1]
            nc.tensor.transpose(ps[:, 6, 0:H1], row, ident[0:H1, 0:H1]).then_inc(end_turned, 1)

        PSAME, NSAME, PNEG, NNEG = range(4)

        def order_vector(dve, st):
            v = nc.vector
            for n, m in ((0, M_DSTF), (3, M_SRCF), (4, M_TYPE)):
                st(v.tensor_copy(colf[:, n, :], rec[:, :, m]))
            said["flat"] = st.n
            dve.wait_ge(tgt_in, 32)
            st(v.tensor_tensor(psame[:], colf[:, 0, :], colf[:, 1, :], ALU.is_equal))
            st(v.tensor_tensor(nsame[:], colf[:, 0, :], colf[:, 2, :], ALU.is_equal))
            st(v.tensor_scalar(pneg[:], psame[:], 1.0, BIG, ALU.subtract, ALU.mult))
            st(v.tensor_scalar(nneg[:], nsame[:], 1.0, BIG, ALU.subtract, ALU.mult))
            for kind, t in ((PSAME, psame), (NSAME, nsame), (PNEG, pneg), (NNEG, nneg)):
                for h in range(H1):
                    st(v.tensor_reduce(ends2[:, kind, h:h + 1], t[:], AX, ALU.min))
            said["ends"] = st.n
            dve.wait_ge(ends_turned, 1)
            st(v.tensor_copy(ends_row[:], ps[0:H1, 0, :].rearrange("h (k p) -> h k p", k=4)))
            st(v.memset(sc_a[:], 1.0))
            seg_scan(dve, 0, sc_b, psame, sc_a, ALU.mult, ALU.add, 0.0, PSAME, True)
            st(v.reciprocal(rec[:, :, M_RDEG], sc_b[:, 0, :]))
            st(v.scalar_tensor_tensor(rec_i[:, :, M_LAST], nsame[:], float(NOWHERE), colf[:, 0, :],
                                      ALU.mult, ALU.add))
            st(v.scalar_tensor_tensor(rec_i[:, :, M_DST], colf[:, 0, :], float(N), colf[:, 0, :],
                                      ALU.is_lt, ALU.mult))
            said["records"] = st.n

        ends_turned = sem("ends_turned")

        def order_tensor(pe):
            pe.wait_ge(dve_step, said["ends"])
            for kind in range(4):
                mm = nc.tensor.transpose(ps[0:H1, 0, kind * P:(kind + 1) * P], ends2[:, kind, :], ident[:])
            mm.then_inc(ends_turned, 1)
            seg_scan_tensor(pe, 0, True)

        def order_sync(sp):
            flat = lambda t: t.rearrange("(p c) -> p c", c=EC)
            sp.wait_ge(dve_step, said["flat"])
            sp.dma_start(flat(tgt_d[1:EP + 1]), colf[:, 0, :]).then_inc(tgt_stored, 16)
            sp.dma_start(tgt_d[0:1].unsqueeze(0), stops[0:1, 0:1]).then_inc(tgt_stored, 16)
            sp.dma_start(tgt_d[EP + 1:EP + 2].unsqueeze(0), stops[0:1, 1:2]).then_inc(tgt_stored, 16)
            sp.wait_ge(tgt_stored, 48)
            sp.dma_start(colf[:, 1, :], flat(tgt_d[0:EP])).then_inc(tgt_in, 16)
            sp.dma_start(colf[:, 2, :], flat(tgt_d[2:EP + 2])).then_inc(tgt_in, 16)
            sp.dma_start(flat(srcf_d), colf[:, 3, :]).then_inc(recs_stored, 16)
            sp.dma_start(flat(type_d), colf[:, 4, :]).then_inc(recs_stored, 16)
            sp.dma_start(attr_d.rearrange("(p c) a -> p c a", c=EC), att[:]).then_inc(recs_stored, 16)
            sp.wait_ge(dve_step, said["records"])
            sp.dma_start(flat(same_d), psame[:]).then_inc(recs_stored, 16)
            sp.dma_start(meta_d.rearrange("(p c) k -> p c k", c=EC), rec[:]).then_inc(recs_stored, 16)
            sp.wait_ge(recs_stored, 80)

        def nth(r, i, k):
            return r * NG + 2 * i + k + 1

        def landed(n, r, i):
            return 16 * n * (r * NI + i + 1)

        def record(k, m):
            return lambda j: meta[k][:, j, m:m + 1].bitcast(I32)

        def rows_of(k):
            return lambda j: idx[k][:, j:j + 1]

        def gather(pool, to, table, column, done):
            steady(pool)
            for j in range(SLOTS):
                nc.gpsimd.indirect_dma_start(
                    to[:, j, 0:D] if to.shape[2] != D else to[:, j, :], None, table,
                    bass.IndirectOffsetOnAxis(ap=column(j), axis=0)).then_inc(done, 16)

        def evac(out_, in_):
            return nc.scalar.copy(out_, in_)

        e0_loaded, e0_gathered, e0_scattered = sems("e0_loaded"), sems("e0_gathered"), sems("e0_scattered")
        e0_turned, e0_copied, e0_qkv, e0_q, e0_qk, e0_al, e0_aw, e0_msg, e0_eq, e0_cnt, e0_shift, e0_idx, e0_sum, \
            e0_out = (sem(f"e0_{n}") for n in ("turned", "copied", "qkv", "q", "qk", "al", "aw", "msg", "eq", "cnt",
                                               "shift", "idx", "sum", "out"))
        qkv_ps = [ps[:, 2 + 2 * k:4 + 2 * k, :].rearrange("p b n -> p (b n)").rearrange("p (j c) -> p j c", j=SLOTS)
                  for k in range(2)]

        def e0_sync(sp):
            def load(i, k):
                wait(sp, e0_msg, nth(0, i - 1, k))
                steady(sp)
                wait(sp, e0_cnt, nth(0, i - 1, k))
                steady(sp)
                sp.dma_start(meta[k][:], group_rec(i, k)).then_inc(e0_loaded[k], 16)
                sp.dma_start(rowb[k][:], spread(group_of(srcf_d, i, k), P)).then_inc(e0_loaded[k], 16)
            pipeline(sp, NI, 2, load)

        def group_rec(i, k):
            return meta_d[bass.ds((2 * i + k) * GROUP, GROUP), :].rearrange("(p j) m -> p j m", j=SLOTS)

        def e0_gpsimd(pool):
            pool.wait_ge(agg0_zero, 16 * (NP * D // (P * ZCOLS) + 1))

            def take(i, k):
                pool.wait_ge(e0_loaded[k], landed(2, 0, i))
                wait(pool, e0_turned, nth(0, i - 1, k))
                gather(pool, rows[k], x[:, :], record(k, M_DST), e0_gathered[k])

            def give(i, k):
                pool.wait_ge(e0_out, nth(0, i, k))
                pool.wait_ge(e0_idx, nth(0, i, k))
                wait(pool, e0_scattered[1 - k], landed(SLOTS, 0, i if k else i - 1))
                steady(pool)
                for j in range(SLOTS):
                    nc.gpsimd.indirect_dma_start(
                        agg0[:, :], bass.IndirectOffsetOnAxis(ap=idx[k][:, j:j + 1], axis=0),
                        outd[k][:, j, :], None, compute_op=ALU.add).then_inc(e0_scattered[k], 16)
            pipeline(pool, NI, 2, take, (2, give))
            for k in range(2):
                pool.wait_ge(e0_scattered[k], landed(SLOTS, 0, NI - 1))

        def e0_tensor(pe):
            t = nc.tensor

            def front(i, k):
                pe.wait_ge(e0_gathered[k], landed(SLOTS, 0, i))
                wait(pe, e0_copied, nth(0, i - 1, k))
                steady(pe)
                for j in range(SLOTS):
                    mm = t.transpose(ps[0:D, k, j * P:(j + 1) * P], rows[k][:, j, 0:D], ident[:])
                mm.then_inc(e0_turned, 1)
                pe.wait_ge(e0_copied, nth(0, i, k))
                wait(pe, e0_msg, nth(0, i - 1, k))
                wait(pe, e0_q, nth(0, i - 1, k))
                steady(pe)
                for j in range(SLOTS):
                    mm = t.matmul(qkv_ps[k][:, j, 0:3 * D], turn[k][0:D, j * P:(j + 1) * P], qkv_w[:],
                                  start=True, stop=True)
                mm.then_inc(e0_qkv, 1)

            def back(i, k):
                pe.wait_ge(e0_msg, nth(0, i, k))
                pe.wait_ge(e0_eq, nth(0, i, k))
                wait(pe, e0_out, nth(0, i - 1, k))
                steady(pe)
                for j in range(SLOTS):
                    for m in range(SLOTS):
                        mm = t.matmul(ps[:, 6 + k, j * D:(j + 1) * D], slot_of(eq[k][:, m, :], j),
                                      msg_t[k][:, m, :], start=(m == 0), stop=(m == SLOTS - 1))
                mm.then_inc(e0_sum, 1)
            pipeline(pe, NI, 2, front, back)

        def e0_scalar(act):
            def front(i, k):
                act.wait_ge(e0_turned, nth(0, i, k))
                wait(act, e0_qkv, nth(0, i - 1, k))
                evac(turn[k][0:D, :], ps[0:D, k, :]).then_inc(e0_copied, 1)
                act.wait_ge(e0_qkv, nth(0, i, k))
                wait(act, e0_qk, nth(0, i - 1, k))
                evac(q_t[k][:], qkv_ps[k][:, :, 0:D]).then_inc(e0_q, 1)

            def back(i, k):
                act.wait_ge(e0_sum, nth(0, i, k))
                wait(act, e0_scattered[k], landed(SLOTS, 0, i - 1))
                evac(outd[k][:], ps[:, 6 + k, 0:SLOTS * D].rearrange("p (j d) -> p j d", j=SLOTS)) \
                    .then_inc(e0_out, 1)
            pipeline(act, NI, 2, front, back)

        def e0_vector(dve):
            v = nc.vector

            def match(i, k):
                dve.wait_ge(e0_loaded[k], landed(2, 0, i))
                wait(dve, e0_sum, nth(0, i - 1, k))
                for j in range(SLOTS):
                    op = v.tensor_scalar(eq[k][:, j, :], rowb[k][:], meta[k][:, j, M_SRCF:M_SRCF + 1], None,
                                         ALU.is_equal)
                op.then_inc(e0_eq, 1)
                dve.wait_ge(e0_eq, nth(0, i, k))
                for j in range(SLOTS):
                    v.tensor_tensor_reduce(junk[:, j, :], eq[k][:, j, :], later[:, j, :], 1.0, 0.0, ALU.mult, ALU.add,
                                           cnt[k][:, j:j + 1])
                v.tensor_tensor(gap[k][:], trash[:], meta[k][:, :, M_SRCF], ALU.subtract).then_inc(e0_cnt, 1)
                dve.wait_ge(e0_cnt, nth(0, i, k))
                v.scalar_tensor_tensor(shift[k][:], cnt[k][:], 0.0, gap[k][:], ALU.is_gt, ALU.mult) \
                 .then_inc(e0_shift, 1)
                dve.wait_ge(e0_shift, nth(0, i, k))
                wait(dve, e0_scattered[k], landed(SLOTS, 0, i - 1))
                v.tensor_tensor(idx[k][:], shift[k][:], meta[k][:, :, M_SRCF], ALU.add).then_inc(e0_idx, 1)

            def message(i, k):
                dve.wait_ge(e0_q, nth(0, i, k))
                v.tensor_tensor(qk_t[k][:], q_t[k][:], qkv_ps[k][:, :, D:2 * D], ALU.mult).then_inc(e0_qk, 1)
                dve.wait_ge(e0_qk, nth(0, i, k))
                v.tensor_reduce(al_t[k][:], qk_t[k][:].rearrange("p j (h f) -> p j h f", f=FH), AX, ALU.add) \
                 .then_inc(e0_al, 1)
                dve.wait_ge(e0_al, nth(0, i, k))
                v.scalar_tensor_tensor(aw_t[k][:], al_t[k][:], float(FH) ** -0.5,
                                       meta[k][:, :, M_W].unsqueeze(2).broadcast_to([P, SLOTS, H0]),
                                       ALU.mult, ALU.mult).then_inc(e0_aw, 1)
                dve.wait_ge(e0_aw, nth(0, i, k))
                wait(dve, e0_sum, nth(0, i - 1, k))
                v.tensor_tensor(msg_t[k][:].rearrange("p j (h f) -> p j h f", f=FH),
                                qkv_ps[k][:, :, 2 * D:3 * D].rearrange("p j (h f) -> p j h f", f=FH),
                                aw_t[k][:].unsqueeze(3).broadcast_to([P, SLOTS, H0, FH]), ALU.mult) \
                 .then_inc(e0_msg, 1)

            def both(i, k):
                match(i, k)
                message(i, k)
            pipeline(dve, NI, 2, both)

        e1_loaded, e1_gathered = sems("e1_loaded"), sems("e1_gathered")
        e1_xst, e1_lst = sems("e1_xst"), sems("e1_lst")
        e1_turned, e1_copied, e1_qk, e1_k, e1_prod, e1_sum, e1_logit = (
            sem(f"e1_{n}") for n in ("turned", "copied", "qk", "k", "prod", "sum", "logit"))

        def e1_sync(sp, r):
            def load(i, k):
                wait(sp, e1_gathered[k], landed(2 * SLOTS, r, i - 1))
                steady(sp)
                sp.dma_start(meta[k][:], group_rec(i, k)).then_inc(e1_loaded[k], 16)
            pipeline(sp, NI, 2, load)

        def e1_gpsimd(pool, r, table):
            def take(i, k):
                pool.wait_ge(e1_loaded[k], landed(1, r, i))
                wait(pool, e1_turned, nth(r, i - 1, k))
                for at, m in ((0, M_SRC), (D, M_DST)):
                    gather(pool, rows[k][:, :, at:at + D], table, record(k, m), e1_gathered[k])
            pipeline(pool, NI, 2, take)

        def e1_tensor(pe, r):
            t = nc.tensor

            def front(i, k):
                pe.wait_ge(e1_gathered[k], landed(2 * SLOTS, r, i))
                wait(pe, e1_copied, nth(r, i - 1, k))
                steady(pe)
                for j in range(SLOTS):
                    mm = t.transpose(ps[:, k, j * P:(j + 1) * P], rows[k][:, j, :], ident[:])
                mm.then_inc(e1_turned, 1)
                pe.wait_ge(e1_copied, nth(r, i, k))
                wait(pe, e1_prod, nth(r, i - 1, k))
                t.matmul(ps[:, 2 + k, :], wk_t[r][:], turn[k][:], start=True, stop=True)
                t.matmul(ps[:, 4 + k, :], wq_t[r][:], turn[k][:], start=True, stop=True).then_inc(e1_qk, 1)

            def back(i, k):
                pe.wait_ge(e1_prod, nth(r, i, k))
                wait(pe, e1_logit, nth(r, i - 1, k))
                t.matmul(ps[0:H1, 6 + k, :], head_sum[:], prod[k][:], start=True, stop=True).then_inc(e1_sum, 1)
            pipeline(pe, NI, 2, front, back)

        def e1_scalar(act, r):
            def front(i, k):
                act.wait_ge(e1_turned, nth(r, i, k))
                wait(act, e1_qk, nth(r, i - 1, k))
                wait(act, e1_xst[k], landed(1, r, i - 1))
                evac(in_order(turn[k][:]), to_row(ps[:, k, :])).then_inc(e1_copied, 1)
                act.wait_ge(e1_copied, nth(r, i, k))
                steady(act)
                act.dma_start(xst_d[bass.ds(2 * i + k, 1), :, :].rearrange("o d c -> (o d) c"), turn[k][0:D, :]) \
                   .then_inc(e1_xst[k], 16)
                act.wait_ge(e1_qk, nth(r, i, k))
                wait(act, e1_prod, nth(r, i - 1, k))
                nc.scalar.activation(fmaj[k][:], ps[:, 2 + k, :], ACT.Identity, bias=bias_t[:, r, 0:1]) \
                  .then_inc(e1_k, 1)

            def back(i, k):
                act.wait_ge(e1_sum, nth(r, i, k))
                wait(act, e1_lst[k], landed(1, r, i - 1))
                evac(logit[k][:], ps[0:H1, 6 + k, :]).then_inc(e1_logit, 1)
                act.wait_ge(e1_logit, nth(r, i, k))
                steady(act)
                act.dma_start(logit_d[:, bass.ds((2 * i + k) * GROUP, GROUP)], logit[k][:]).then_inc(e1_lst[k], 16)
            pipeline(act, NI, 2, front, back)
            for k in range(2):
                act.wait_ge(e1_xst[k], landed(1, r, NI - 1))
                act.wait_ge(e1_lst[k], landed(1, r, NI - 1))

        def e1_vector(dve, r):
            def times(i, k):
                dve.wait_ge(e1_k, nth(r, i, k))
                wait(dve, e1_sum, nth(r, i - 1, k))
                nc.vector.scalar_tensor_tensor(prod[k][:], ps[:, 4 + k, :], bias_t[:, r, 1:2], fmaj[k][:],
                                               ALU.add, ALU.mult).then_inc(e1_prod, 1)
            pipeline(dve, NI, 2, times)

        sm_loaded, sm_shifted, sm_exp, sm_stored = sem("sm_loaded"), sem("sm_shifted"), sem("sm_exp"), sem("sm_stored")
        by_head = lambda t: t.rearrange("h (p c) -> p h c", c=EC)

        def softmax_sync(sp, r):
            sp.dma_start(sc_a[:], by_head(logit_d)).then_inc(sm_loaded, 16)
            sp.wait_ge(dve_step, said["coef", r])
            steady(sp)
            sp.dma_start(by_head(coef_d), sc_c[:]).then_inc(sm_stored, 16)
            sp.wait_ge(sm_stored, 16 * (r + 1))

        def softmax_scalar(act, r):
            act.wait_ge(dve_step, said["shifted", r])
            nc.scalar.activation(sc_c[:], sc_a[:], ACT.Exp).then_inc(sm_exp, 1)

        def softmax_tensor(pe, r):
            for n, forward in enumerate((True, False, True, False)):
                seg_scan_tensor(pe, 1 + 4 * r + n, forward)

        def softmax_vector(dve, st, r):
            v = nc.vector
            n = 1 + 4 * r
            dve.wait_ge(sm_loaded, 16 * (r + 1))
            seg_scan(dve, n, sc_b, pneg, sc_a, ALU.add, ALU.max, -BIG, PNEG, True)
            seg_scan(dve, n + 1, sc_c, nneg, sc_b, ALU.add, ALU.max, -BIG, NNEG, False)
            st(v.tensor_tensor(sc_a[:], sc_a[:], sc_c[:], ALU.subtract))
            said["shifted", r] = st.n
            dve.wait_ge(sm_exp, r + 1)
            seg_scan(dve, n + 2, sc_b, psame, sc_c, ALU.mult, ALU.add, 0.0, PSAME, True)
            for h in range(H1):
                st(v.tensor_scalar(sc_a[:, h, :], nsame[:], -1.0, 1.0, ALU.mult, ALU.add))
            st(v.tensor_tensor(sc_b[:], sc_b[:], sc_a[:], ALU.mult))
            seg_scan(dve, n + 3, sc_a, nsame, sc_b, ALU.mult, ALU.add, 0.0, NSAME, False)
            st(v.tensor_scalar(sc_a[:], sc_a[:], 1e-16, None, ALU.add))
            st(v.reciprocal(sc_b[:], sc_a[:]))
            st(v.tensor_tensor(sc_c[:], sc_c[:], sc_b[:], ALU.mult))
            said["coef", r] = st.n

        e2_loaded, e2_scattered = sems("e2_loaded"), sems("e2_scattered")
        e2_v, e2_prod, e2_scan, e2_sum, e2_out = (sem(f"e2_{n}") for n in ("v", "prod", "scan", "sum", "out"))
        E2_LOADS = 3 + H1

        def give_rows(pool, table, of, column, done):
            steady(pool)
            for j in range(SLOTS):
                nc.gpsimd.indirect_dma_start(
                    table, bass.IndirectOffsetOnAxis(ap=column(j), axis=0), of[:, j, :], None,
                    bounds_check=N - 1, oob_is_err=False).then_inc(done, 16)

        def e2_sync(sp, r):
            def load(i, k):
                wait(sp, e2_scattered[k], landed(SLOTS, r, i - 1))
                steady(sp)
                wait(sp, e2_scan, nth(r, i - 1, k))
                steady(sp)
                sp.dma_start(turn[k][0:D, :], xst_d[bass.ds(2 * i + k, 1), :, :].rearrange("o d c -> (o d) c")) \
                  .then_inc(e2_loaded[k], 16)
                for h in range(H1):
                    sp.dma_start(rowb[k][h * D:(h + 1) * D, :], spread(group_of(coef_d[h], i, k), D)) \
                      .then_inc(e2_loaded[k], 16)
                sp.dma_start(sameb[k][:], spread(group_of(same_d, i, k), P)).then_inc(e2_loaded[k], 16)
                sp.dma_start(meta[k][:], group_rec(i, k)).then_inc(e2_loaded[k], 16)
            pipeline(sp, NI, 2, load)

        def e2_tensor(pe, r):
            t = nc.tensor

            def front(i, k):
                pe.wait_ge(e2_loaded[k], landed(E2_LOADS, r, i))
                wait(pe, e2_prod, nth(r, i - 1, k))
                t.matmul(ps[:, k, :], wv_t[r][:], turn[k][0:D, :], start=True, stop=True).then_inc(e2_v, 1)

            def back(i, k):
                pe.wait_ge(e2_scan, nth(r, i, k))
                wait(pe, e2_out, nth(r, i - 1, k))
                steady(pe)
                for j in range(SLOTS):
                    mm = t.matmul(ps[:, 2 + k, j * D:(j + 1) * D], slot_of(scan[k][:], j), head_mean[:],
                                  start=True, stop=True)
                mm.then_inc(e2_sum, 1)
            pipeline(pe, NI, 2, front, back)

        def run_scan(dve, i, k, rows_, of, done, r):
            dve.wait_ge(done, nth(r, i, k) - 1) if not (isinstance(i, int) and nth(r, i, k) == 1) else None
            nc.vector.tensor_tensor_scan(scan[k][0:rows_, :], sameb[k][0:rows_, :], of,
                                         scan[1 - k][0:rows_, GROUP - 1:GROUP], ALU.mult, ALU.add) \
              .then_inc(done, 1)

        def e2_vector(dve, r):
            def weigh(i, k):
                dve.wait_ge(e2_v, nth(r, i, k))
                nc.vector.scalar_tensor_tensor(prod[k][:], ps[:, k, :], bias_t[:, r, 2:3], rowb[k][:],
                                               ALU.add, ALU.mult).then_inc(e2_prod, 1)
                dve.wait_ge(e2_prod, nth(r, i, k))
                wait(dve, e2_sum, nth(r, i - 1, k))
                run_scan(dve, i, k, P, prod[k][:], e2_scan, r)
            pipeline(dve, NI, 2, weigh)

        def e2_scalar(act, r):
            def back(i, k):
                act.wait_ge(e2_sum, nth(r, i, k))
                wait(act, e2_scattered[k], landed(SLOTS, r, i - 1))
                evac(outd[k][:], ps[:, 2 + k, 0:SLOTS * D].rearrange("p (j d) -> p j d", j=SLOTS)) \
                    .then_inc(e2_out, 1)
            pipeline(act, NI, 2, back)

        def e2_gpsimd(pool, r):
            def give(i, k):
                pool.wait_ge(e2_out, nth(r, i, k))
                give_rows(pool, agg[:, :], outd[k], record(k, M_LAST), e2_scattered[k])
            pipeline(pool, NI, 2, give)
            for k in range(2):
                pool.wait_ge(e2_scattered[k], landed(SLOTS, r, NI - 1))

        e3_loaded, e3_gathered, e3_scattered = sems("e3_loaded"), sems("e3_gathered"), sems("e3_scattered")
        e3_twice, e3_turned, e3_copied, e3_masked, e3_used, e3_msg, e3_scan, e3_sum, e3_out, e3_idx = (
            sem(f"e3_{n}") for n in ("twice", "turned", "copied", "masked", "used", "msg", "scan", "sum", "out", "idx"))

        def e3_sync(sp):
            def load(i, k):
                wait(sp, e3_gathered[k], landed(SLOTS, 0, i - 1))
                steady(sp)
                wait(sp, e3_scan, nth(0, i - 1, k))
                steady(sp)
                wait(sp, e3_out, nth(0, i - 1, k))
                steady(sp)
                sp.dma_start(meta[k][:], group_rec(i, k)).then_inc(e3_loaded[k], 16)
                sp.dma_start(rowb[k][:], spread(group_of(type_d, i, k), P)).then_inc(e3_loaded[k], 16)
                sp.dma_start(sameb[k][0:D, :], spread(group_of(same_d, i, k), D)).then_inc(e3_loaded[k], 16)
            pipeline(sp, NI, 2, load)

        def e3_gpsimd(pool):
            def take(i, k):
                pool.wait_ge(e3_loaded[k], landed(3, 0, i))
                wait(pool, e3_turned, nth(0, i - 1, k))
                gather(pool, rows[k], x2[:, :], record(k, M_SRC), e3_gathered[k])

            def give(i, k):
                pool.wait_ge(e3_out, nth(0, i, k))
                give_rows(pool, agg[:, :], outd[k], rows_of(k), e3_scattered[k])
            pipeline(pool, NI, 2, take, (2, give))
            for k in range(2):
                pool.wait_ge(e3_scattered[k], landed(SLOTS, 0, NI - 1))

        def e3_tensor(pe):
            t = nc.tensor

            def front(i, k):
                pe.wait_ge(e3_twice, nth(0, i, k))
                wait(pe, e3_copied, nth(0, i - 1, k))
                steady(pe)
                for j in range(SLOTS):
                    mm = t.transpose(ps[:, k, j * P:(j + 1) * P], rows[k][:, j, :], ident[:])
                mm.then_inc(e3_turned, 1)

            def middle(i, k):
                wait(pe, e3_scan, nth(0, i - 1, k))
                for m in range(NPAIR):
                    pe.wait_ge(e3_masked, (nth(0, i, k) - 1) * NPAIR + m + 1)
                    mm = t.matmul(ps[0:D, 2 + k, :], rel_w[:, m, :], masked[m % 4][:],
                                  start=(m == 0), stop=(m == NPAIR - 1))
                    mm.then_inc(e3_used, 1)

            def back(i, k):
                pe.wait_ge(e3_scan, nth(0, i, k))
                wait(pe, e3_out, nth(0, i - 1, k))
                steady(pe)
                for j in range(SLOTS):
                    mm = t.transpose(ps[:, 4 + k, j * D:(j + 1) * D], slot_of(scan[k][0:D, :], j), ident[0:D, 0:D])
                mm.then_inc(e3_sum, 1)
            pipeline(pe, NI, 2, (0, front), (1, middle), (1, back))

        def e3_scalar(act):
            def front(i, k):
                act.wait_ge(e3_gathered[k], landed(SLOTS, 0, i))
                evac(rows[k][:, :, D:P], rows[k][:, :, 0:D]).then_inc(e3_twice, 1)
                act.wait_ge(e3_turned, nth(0, i, k))
                wait(act, e3_used, NPAIR * nth(0, i - 1, k))
                evac(in_order(turn[k][:]), to_row(ps[:, k, :])).then_inc(e3_copied, 1)
            pipeline(act, NI, 2, front)

        def e3_vector(dve):
            v = nc.vector

            def mask(i, k):
                dve.wait_ge(e3_copied, nth(0, i, k))
                dve.wait_ge(e3_loaded[k], landed(3, 0, i))
                for m in range(NPAIR):
                    if m >= 4:
                        dve.wait_ge(e3_used, (nth(0, i, k) - 1) * NPAIR + m - 3)
                    else:
                        wait(dve, e3_used, (nth(0, i, k) - 1) * NPAIR + m - 3)
                    v.scalar_tensor_tensor(masked[m % 4][:], rowb[k][:], rel_id[:, m:m + 1], turn[k][:],
                                           ALU.is_equal, ALU.mult).then_inc(e3_masked, 1)

            def add(i, k):
                dve.wait_ge(e3_used, NPAIR * nth(0, i, k))
                wait(dve, e3_sum, nth(0, i - 1, k))
                run_scan(dve, i, k, D, ps[0:D, 2 + k, :], e3_scan, 0)

            def back(i, k):
                wait(dve, e3_scattered[k], landed(SLOTS, 0, i - 1))
                v.tensor_copy(idx[k][:], meta[k][:, :, M_LAST].bitcast(I32)).then_inc(e3_idx, 1)
                dve.wait_ge(e3_sum, nth(0, i, k))
                dve.wait_ge(e3_idx, nth(0, i, k))
                v.tensor_tensor(outd[k][:], ps[:, 4 + k, 0:SLOTS * D].rearrange("p (j d) -> p j d", j=SLOTS),
                                meta[k][:, :, M_RDEG].unsqueeze(2).broadcast_to([P, SLOTS, D]), ALU.mult) \
                 .then_inc(e3_out, 1)
            pipeline(dve, NI, 2, (0, mask), (0, add), (0, back))

        e4_loaded, e4_gathered, e4_scattered = sems("e4_loaded"), sems("e4_gathered"), sems("e4_scattered")
        e4_turned, e4_copied, e4_scan, e4_sum, e4_out, e4_idx = (
            sem(f"e4_{n}") for n in ("turned", "copied", "scan", "sum", "out", "idx"))

        def e4_sync(sp, r):
            def load(i, k):
                wait(sp, e4_turned, nth(r, i - 1, k))
                steady(sp)
                wait(sp, e4_idx, nth(r, i - 1, k))
                steady(sp)
                wait(sp, e4_gathered[k], landed(SLOTS, r, i - 1))
                steady(sp)
                wait(sp, e4_scan, nth(r, i - 1, k))
                steady(sp)
                sp.dma_start(meta[k][:], group_rec(i, k)).then_inc(e4_loaded[k], 16)
                sp.dma_start(roww[k][:, :, D:D + NA], attr_d[bass.ds((2 * i + k) * GROUP, GROUP), :]
                             .rearrange("(p j) a -> p j a", j=SLOTS)).then_inc(e4_loaded[k], 16)
                sp.dma_start(sameb[k][0:AW, :], spread(group_of(same_d, i, k), AW)).then_inc(e4_loaded[k], 16)
            pipeline(sp, NI, 2, load)

        def e4_gpsimd(pool, r, table):
            def take(i, k):
                pool.wait_ge(e4_loaded[k], landed(3, r, i))
                wait(pool, e4_turned, nth(r, i - 1, k))
                gather(pool, roww[k], table, record(k, M_SRC), e4_gathered[k])

            def give(i, k):
                pool.wait_ge(e4_out, nth(r, i, k))
                pool.wait_ge(e4_idx, nth(r, i, k))
                give_rows(pool, aggw[:, :], outr[k], rows_of(k), e4_scattered[k])
            pipeline(pool, NI, 2, take, (2, give))
            for k in range(2):
                pool.wait_ge(e4_scattered[k], landed(SLOTS, r, NI - 1))

        def e4_tensor(pe, r):
            t = nc.tensor

            def front(i, k):
                pe.wait_ge(e4_gathered[k], landed(SLOTS, r, i))
                wait(pe, e4_copied, nth(r, i - 1, k))
                steady(pe)
                for j in range(SLOTS):
                    mm = t.transpose(ps[0:AW, k, j * P:(j + 1) * P], roww[k][:, j, :], ident[:])
                mm.then_inc(e4_turned, 1)

            def back(i, k):
                pe.wait_ge(e4_scan, nth(r, i, k))
                wait(pe, e4_out, nth(r, i - 1, k))
                steady(pe)
                for j in range(SLOTS):
                    mm = t.transpose(ps[:, 2 + k, j * AW:(j + 1) * AW], slot_of(scan[k][0:AW, :], j),
                                     ident[0:AW, 0:AW])
                mm.then_inc(e4_sum, 1)
            pipeline(pe, NI, 2, front, back)

        def e4_scalar(act, r):
            def front(i, k):
                act.wait_ge(e4_turned, nth(r, i, k))
                wait(act, e4_scan, nth(r, i - 1, k))
                evac(in_order(turn[k][0:AW, :]), to_row(ps[0:AW, k, :])).then_inc(e4_copied, 1)

            def back(i, k):
                act.wait_ge(e4_sum, nth(r, i, k))
                wait(act, e4_scattered[k], landed(SLOTS, r, i - 1))
                evac(outr[k][:], ps[:, 2 + k, 0:SLOTS * AW].rearrange("p (j d) -> p j d", j=SLOTS)) \
                    .then_inc(e4_out, 1)
            pipeline(act, NI, 2, front, back)

        def e4_vector(dve, r):
            def add(i, k):
                dve.wait_ge(e4_copied, nth(r, i, k))
                dve.wait_ge(e4_loaded[k], landed(3, r, i))
                wait(dve, e4_sum, nth(r, i - 1, k))
                run_scan(dve, i, k, AW, turn[k][0:AW, :], e4_scan, r)
                wait(dve, e4_scattered[k], landed(SLOTS, r, i - 1))
                nc.vector.tensor_copy(idx[k][:], meta[k][:, :, M_LAST].bitcast(I32)).then_inc(e4_idx, 1)
            pipeline(dve, NI, 2, add)

        N_LOADED = (2, 2, 3, 2)
        HAS_LINEAR, HAS_NORM = (0, 1, 1, 1), (1, 0, 1, 1)
        nd_loaded, nd_stored = sems("nd_loaded"), sems("nd_stored")
        nd_turned, nd_copied, nd_mm, nd_part, nd_y, nd_s, nd_c, nd_q, nd_v, nd_i, nd_o = (
            sem(f"nd_{n}") for n in ("turned", "copied", "mm", "part", "y", "s", "c", "q", "v", "i", "o"))

        nd_w = sem("nd_w")
        node_e, node_w = pair("node_e", [P, ROWS]), pair("node_w", [P, ROWS])

        def nd(r, i, k):
            return r * NCH + 2 * i + k + 1

        def nd_lin(r, i, k):
            return sum(HAS_LINEAR[:r]) * NCH + 2 * i + k + 1

        def nd_nrm(r, i, k):
            return sum(HAS_NORM[:r]) * NCH + 2 * i + k + 1

        def chunk_of(table, i, k, parts=P):
            return table[bass.ds((2 * i + k) * CHUNK, parts * ROWS), :].rearrange("(p c) d -> p c d", c=ROWS)

        def node_sync(sp, r, a, g, res):
            def load(i, k):
                wait(sp, nd_y, nd(r, i - 1, k))
                last = r == 0 and isinstance(i, int) and i == CI - 1 and k == 1
                parts = LAST_PARTS if last else P
                for t, of in ((node_a[k], a), (node_g[k], g), (node_r[k], res)):
                    if of is not None:
                        n = parts if of is x else P
                        sp.dma_start(t[0:n], chunk_of(of, i, k, n)).then_inc(nd_loaded[k], 16)
            if r == 0:
                pipeline(sp, CI - 1, 2, load)
                for k in range(2):
                    load(CI - 1, k)
            else:
                pipeline(sp, CI, 2, load)

        def nd_landed(r, i):
            return 16 * (CI * sum(N_LOADED[:r]) + N_LOADED[r] * (i + 1))

        def node_tensor(pe, r):
            t = nc.tensor
            w, b = lin_w[r - 1], lin_b[r - 1]

            def front(i, k):
                pe.wait_ge(nd_loaded[k], nd_landed(r, i))
                wait(pe, nd_copied, nd_lin(r, i - 1, k))
                for c in range(0, ROWS, 2):
                    mm = t.transpose(ps[:, k, c * D:(c + 2) * D], node_a[k][:, c:c + 2, :].rearrange("p c d -> p (c d)"),
                                     ident[:])
                mm.then_inc(nd_turned, 1)

            def back(i, k):
                pe.wait_ge(nd_copied, nd_lin(r, i, k))
                wait(pe, nd_y, nd(r, i - 1, k))
                t.matmul(ps[:, 2 + k, :], ones_row[:], b[:], start=True, stop=False, skip_group_check=True)
                for c in range(0, ROWS, 2):
                    mm = t.matmul(ps[:, 2 + k, c * D:(c + 2) * D], node_t[k][:, c:c + 2, :].rearrange("p c d -> p (c d)"),
                                  w[:], start=False, stop=True, skip_group_check=True)
                mm.then_inc(nd_mm, 1)
            pipeline(pe, CI, 2, front, back)

        def node_scalar(act, r):
            def front(i, k):
                act.wait_ge(nd_turned, nd_lin(r, i, k))
                wait(act, nd_mm, nd_lin(r, i - 1, k))
                evac(node_t[k][:].rearrange("p c d -> p (c d)"), ps[:, k, :]).then_inc(nd_copied, 1)

            def square(i, k):
                act.wait_ge(nd_c, nd_nrm(r, i, k))
                wait(act, nd_v, nd_nrm(r, i - 1, k))
                nc.scalar.activation(node_q[k][:], node_c[k][:], ACT.Square).then_inc(nd_q, 1)
            pipeline(act, CI, 2, *([(0, front)] if HAS_LINEAR[r] else []), *([(1, square)] if HAS_NORM[r] else []))

        def node_vector(dve, r):
            v = nc.vector

            def add(i, k):
                y = node_y[k] if HAS_NORM[r] else node_o[k]
                dve.wait_ge(nd_loaded[k], nd_landed(r, i))
                if not HAS_NORM[r]:
                    wait(dve, nd_stored[k], 16 * (r * CI + i))
                if HAS_LINEAR[r]:
                    dve.wait_ge(nd_mm, nd_lin(r, i, k))
                mm = ps[:, 2 + k, :].rearrange("p (c d) -> p c d", d=D)
                if r == 0:
                    v.tensor_tensor(y[:], node_r[k][:], node_g[k][:], ALU.add).then_inc(nd_y, 1)
                elif r == 1:
                    v.tensor_tensor(y[:], mm, node_g[k][:], ALU.add).then_inc(nd_y, 1)
                else:
                    v.tensor_tensor(node_p[k][:], mm, node_g[k][:], ALU.add).then_inc(nd_part, 1)
                    dve.wait_ge(nd_part, (r - 2) * NCH + 2 * i + k + 1)
                    v.tensor_tensor(y[:], node_p[k][:], node_r[k][:] if r == 2 else node_a[k][:], ALU.add) \
                     .then_inc(nd_y, 1)
                if HAS_NORM[r]:
                    center(dve, k, y, nd_y, nd(r, i, k), nd_nrm(r, i, k))

            def spread_of(i, k):
                variance(dve, k, ROWS, nd_nrm(r, i, k))

            def scale(i, k):
                wait(dve, nd_stored[k], 16 * (r * CI + i))
                norm(dve, k, node_o[k], nd_nrm(r, i, k))
            pipeline(dve, CI, 2, *([(1, spread_of), (0, add), (1, scale)] if HAS_NORM[r] else [add]))

        def center(dve, k, y, y_ready, ready, n):
            v = nc.vector
            rows_ = y.shape[1]
            dve.wait_ge(y_ready, ready)
            v.tensor_reduce(node_s[k][:, 0:rows_], y[:], AX, ALU.add).then_inc(nd_s, 1)
            dve.wait_ge(nd_s, n)
            v.scalar_tensor_tensor(node_c[k][:, 0:rows_, :], node_s[k][:, 0:rows_].unsqueeze(2).broadcast_to([P, rows_, D]),
                                   -1.0 / D, y[:], ALU.mult, ALU.add).then_inc(nd_c, 1)

        def variance(dve, k, rows_, n):
            dve.wait_ge(nd_q, n)
            nc.vector.tensor_reduce(node_v[k][:, 0:rows_], node_q[k][:, 0:rows_, :], AX, ALU.add).then_inc(nd_v, 1)

        def inverse_root(pool, k, rows_, n):
            g = nc.gpsimd
            var, root_, work = (t[k][:, 0:rows_] for t in (node_e, node_i, node_w))
            done = [(n - 1) * ROOT_STEPS]

            def step(ins):
                done[0] = done[0] + 1
                ins.then_inc(nd_w, 1)
                pool.wait_ge(nd_w, done[0])
                steady(pool)

            pool.wait_ge(nd_v, n)
            steady(pool)
            step(g.tensor_scalar(var, node_v[k][:, 0:rows_], D * EPS, None, ALU.add))
            step(g.tensor_scalar(root_.bitcast(I32), var.bitcast(I32), -0.5, float(0x5f3759df), ALU.mult, ALU.add))
            for _ in range(NEWTON):
                step(g.tensor_tensor(work, root_, root_, ALU.mult))
                step(g.tensor_tensor(work, work, var, ALU.mult))
                step(g.tensor_scalar(work, work, -0.5, 1.5, ALU.mult, ALU.add))
                step(g.tensor_tensor(root_, root_, work, ALU.mult))
            g.engine_nop().then_inc(nd_i, 1)

        def norm(dve, k, to, n):
            rows_ = to.shape[1]
            dve.wait_ge(nd_i, n)
            nc.vector.scalar_tensor_tensor(to[:], node_c[k][:, 0:rows_, :], float(D) ** 0.5,
                                           node_i[k][:, 0:rows_].unsqueeze(2).broadcast_to([P, rows_, D]),
                                           ALU.mult, ALU.mult).then_inc(nd_o, 1)

        def node_gpsimd(pool, r, to):
            def store(i, k):
                if HAS_NORM[r]:
                    pool.wait_ge(nd_o, nd_nrm(r, i, k))
                else:
                    pool.wait_ge(nd_y, nd(r, i, k))
                steady(pool)
                pool.dma_start(chunk_of(to, i, k), node_o[k][:]).then_inc(nd_stored[k], 16)

            def root(i, k):
                wait(pool, nd_o, nd_nrm(r, i - 1, k))
                inverse_root(pool, k, ROWS, nd_nrm(r, i, k))
            pipeline(pool, CI, 2, *([root, store] if HAS_NORM[r] else [store]))
            for k in range(2):
                pool.wait_ge(nd_stored[k], 16 * (r + 1) * CI)

        gc_loaded, gc_stored = sems("gc_loaded", 4), sems("gc_stored")
        gc_res = sems("gc_res", 4)
        gc_dh, gc_turned, gc_copied, gc_mm, gc_rz, gc_rn, gc_pre, gc_n, gc_d, gc_zd, gc_h, gc_y = (
            sem(f"gc_{n}") for n in ("dh", "turned", "copied", "mm", "rz", "rn", "pre", "n", "d", "zd", "h", "y"))
        cell_n, cell_p, cell_d, cell_z = (pair(n, [P, CROWS, D]) for n in ("cell_n", "cell_p", "cell_d", "cell_z"))
        cell_q, cell_h, cell_y, cell_o = (pair(n, [P, CROWS, D]) for n in ("cell_q", "cell_h", "cell_y", "cell_o"))
        cell_r = pair("cell_r", [P, CROWS, D], n=4)
        gate_ps = [ps[:, 4 + 2 * k:6 + 2 * k, :].rearrange("p b n -> p (b n)").rearrange("p (c n) -> p c n", c=CROWS)
                   for k in range(2)]

        def gc(r, i, u):
            return r * NCC + 4 * i + u + 1

        def gc_before(r, i, u, d=2):
            return gc(r, i, u) - d if r == 0 else gc(r, i, u) - d

        def cell_chunk(table, i, u, parts=P):
            return table[bass.ds((4 * i + u) * CCHUNK, parts * CROWS), :].rearrange("(p c) d -> p c d", c=CROWS)

        def cell_sync(sp, r, h):
            def load(i, u):
                wait(sp, gc_h, gc(r, i, u) - 4)
                steady(sp)
                sp.dma_start(cell_in[u][:, :, H_AT:H_AT + D], cell_chunk(h, i, u)).then_inc(gc_loaded[u], 16)
                sp.dma_start(cell_in[u][:, :, S_AT:S_AT + EW], aggw[bass.ds((4 * i + u) * CCHUNK, CCHUNK), 0:EW]
                             .rearrange("(p c) d -> p c d", c=CROWS)).then_inc(gc_loaded[u], 16)
                if r == 1:
                    wait(sp, gc_y, 4 * i + u + 1 - 4)
                    steady(sp)
                    sp.dma_start(cell_r[u][:], cell_chunk(x3, i, u)).then_inc(gc_res[u], 16)
            pipeline(sp, CCI, 4, load)

        def cell_tensor(pe, r):
            t = nc.tensor

            def turn_in(i, u):
                k = u % 2
                pe.wait_ge(gc_dh, gc(r, i, u))
                wait(pe, gc_copied, gc(r, i, u) - 2)
                for c in range(CROWS):
                    t.transpose(ps[:, k, c * P:(c + 1) * P], cell_in[u][:, c, 0:P], ident[:])
                    mm = t.transpose(ps[0:96, 2 + k, c * P:(c + 1) * P], cell_in[u][:, c, P:P + 96], ident[:])
                mm.then_inc(gc_turned, 1)

            def gates(i, u):
                k = u % 2
                pe.wait_ge(gc_copied, gc(r, i, u))
                wait(pe, gc_pre, gc(r, i, u) - 2)
                for c in range(CROWS):
                    t.matmul(gate_ps[k][:, c, :], cell_u[k][:, c * P:(c + 1) * P], gate_v[r][:],
                             start=True, stop=False, skip_group_check=True)
                    mm = t.matmul(gate_ps[k][:, c, 0:GI], cell_t[k][:, c * P:(c + 1) * P], gate_w[r][:],
                                  start=False, stop=True, skip_group_check=True)
                mm.then_inc(gc_mm, 1)
            pipeline(pe, CCI, 4, turn_in, gates)

        def cell_scalar(act, r):
            a = nc.scalar

            def copy(i, u):
                k = u % 2
                act.wait_ge(gc_turned, gc(r, i, u))
                wait(act, gc_mm, gc(r, i, u) - 2)
                evac(cell_t[k][:], ps[:, k, :])
                evac(cell_u[k][:], ps[0:96, 2 + k, :]).then_inc(gc_copied, 1)

            def gates(i, u):
                k = u % 2
                act.wait_ge(gc_mm, gc(r, i, u))
                wait(act, gc_zd, gc(r, i, u) - 2)
                a.activation(cell_rz[k][:], gate_ps[k][:, :, 0:2 * D], ACT.Sigmoid).then_inc(gc_rz, 1)

            def new(i, u):
                k = u % 2
                act.wait_ge(gc_pre, gc(r, i, u))
                wait(act, gc_h, gc(r, i, u) - 2)
                a.activation(cell_n[k][:], cell_p[k][:], ACT.Tanh).then_inc(gc_n, 1)

            def square(i, u):
                k = u % 2
                act.wait_ge(nd_c, sum(HAS_NORM) * NCH + 4 * i + u + 1)
                wait(act, nd_v, sum(HAS_NORM) * NCH + 4 * i + u + 1 - 2)
                a.activation(node_q[k][:, 0:CROWS, :], node_c[k][:, 0:CROWS, :], ACT.Square).then_inc(nd_q, 1)
            pipeline(act, CCI, 4, copy, gates, new, *([square] if r == 1 else []))

        def cell_vector(dve, r):
            v = nc.vector

            def scale_in(i, u):
                dve.wait_ge(gc_loaded[u], 16 * 2 * (r * CCI + i + 1))
                v.tensor_tensor(cell_in[u][:, :, 0:D], cell_in[u][:, :, H_AT:H_AT + D],
                                cell_in[u][:, :, DEG_AT:DEG_AT + 1].broadcast_to([P, CROWS, D]), ALU.mult) \
                 .then_inc(gc_dh, 1)

            def gates(i, u):
                k = u % 2
                dve.wait_ge(gc_rz, gc(r, i, u))
                v.tensor_tensor(cell_q[k][:], cell_rz[k][:, :, 0:D], gate_ps[k][:, :, GI:GI + D], ALU.mult) \
                 .then_inc(gc_rn, 1)
                dve.wait_ge(gc_rn, gc(r, i, u))
                wait(dve, gc_n, gc(r, i, u) - 2)
                v.tensor_tensor(cell_p[k][:], cell_q[k][:], gate_ps[k][:, :, 2 * D:GI], ALU.add).then_inc(gc_pre, 1)

            def finish(i, u):
                k = u % 2
                to = cell_o[k] if r == 0 else cell_h[k]
                dve.wait_ge(gc_n, gc(r, i, u))
                v.tensor_tensor(cell_d[k][:], cell_in[u][:, :, H_AT:H_AT + D], cell_n[k][:], ALU.subtract) \
                 .then_inc(gc_d, 1)
                dve.wait_ge(gc_d, gc(r, i, u))
                v.tensor_tensor(cell_z[k][:], cell_rz[k][:, :, D:2 * D], cell_d[k][:], ALU.mult).then_inc(gc_zd, 1)
                dve.wait_ge(gc_zd, gc(r, i, u))
                if r == 0:
                    wait(dve, gc_stored[k], 16 * ((4 * i + u) // 2 if isinstance(i, int) else 2 * i + u // 2))
                v.tensor_tensor(to[:], cell_n[k][:], cell_z[k][:], ALU.add).then_inc(gc_h, 1)
                if r == 1:
                    dve.wait_ge(gc_h, gc(r, i, u))
                    dve.wait_ge(gc_res[u], 16 * (i + 1))
                    v.tensor_tensor(cell_y[k][:], cell_h[k][:], cell_r[u][:], ALU.add).then_inc(gc_y, 1)
                    center(dve, k, cell_y[k], gc_y, 4 * i + u + 1, sum(HAS_NORM) * NCH + 4 * i + u + 1)

            def scale(i, u):
                k = u % 2
                wait(dve, gc_stored[k], 16 * (NCC // 2 + 2 * i + u // 2))
                norm(dve, k, cell_o[k], sum(HAS_NORM) * NCH + 4 * i + u + 1)

            def spread_of(i, u):
                variance(dve, u % 2, CROWS, sum(HAS_NORM) * NCH + 4 * i + u + 1)
            pipeline(dve, CCI, 4, *([(4, spread_of)] if r == 1 else []), (0, scale_in), (2, gates), (3, finish),
                     *([(4, scale)] if r == 1 else []))

        def cell_gpsimd(pool, r, to):
            def store(i, u):
                if r == 0:
                    pool.wait_ge(gc_h, gc(r, i, u))
                    steady(pool)
                    pool.dma_start(cell_chunk(to, i, u), cell_o[u % 2][:]).then_inc(gc_stored[u % 2], 16)
                    return
                pool.wait_ge(nd_o, sum(HAS_NORM) * NCH + 4 * i + u + 1)
                n = 4 * i + u if isinstance(i, int) else 0
                parts = P if n < C_FULL else C_PARTS if n == C_FULL else 0
                if parts:
                    pool.dma_start(cell_chunk(to, i, u, parts), cell_o[u % 2][0:parts]).then_inc(gc_stored[u % 2], 16)

            def root(i, u):
                wait(pool, nd_o, sum(HAS_NORM) * NCH + 4 * i + u + 1 - 2)
                inverse_root(pool, u % 2, CROWS, sum(HAS_NORM) * NCH + 4 * i + u + 1)
            if r == 0:
                pipeline(pool, CCI, 4, store)
            else:
                pipeline(pool, CCI - 1, 4, root, store)
                for u in range(4):
                    root(CCI - 1, u)
                    store(CCI - 1, u)
            for k in range(2):
                pool.wait_ge(gc_stored[k], 16 * (r + 1) * NCC // 2)

        conv_in = (x1, h1)
        block = ctx.enter_context(nc.Block())

        @block.gpsimd
        def _(pool):
            consts(pool)
            sort_gpsimd(pool)
            phase_end(pool, "prepare")
            e0_gpsimd(pool)
            phase_end(pool, "edges 0")
            node_gpsimd(pool, 0, x1)
            phase_end(pool, "nodes 0")
            for r in range(2):
                e1_gpsimd(pool, r, conv_in[r][:, :])
                phase_end(pool, f"logits {r}")
                phase_end(pool, f"softmax {r}")
                e2_gpsimd(pool, r)
                phase_end(pool, f"values {r}")
                node_gpsimd(pool, 1 + r, (h1, x2)[r])
                phase_end(pool, f"nodes {1 + r}")
            e3_gpsimd(pool)
            phase_end(pool, "relations")
            node_gpsimd(pool, 3, x3)
            phase_end(pool, "nodes 3")
            for r in range(2):
                e4_gpsimd(pool, r, (x3, v1)[r][:, :])
                phase_end(pool, f"messages {r}")
                cell_gpsimd(pool, r, (v1, out)[r])
                phase_end(pool, f"cell {r}")

        @block.vector
        def _(dve):
            st = Steps(dve, dve_step)
            prep_vector(dve, st)
            sort_vector(dve)
            order_vector(dve, st)
            phase_end(dve, "prepare")
            e0_vector(dve)
            phase_end(dve, "edges 0")
            node_vector(dve, 0)
            phase_end(dve, "nodes 0")
            for r in range(2):
                e1_vector(dve, r)
                phase_end(dve, f"logits {r}")
                softmax_vector(dve, st, r)
                phase_end(dve, f"softmax {r}")
                e2_vector(dve, r)
                phase_end(dve, f"values {r}")
                node_vector(dve, 1 + r)
                phase_end(dve, f"nodes {1 + r}")
            e3_vector(dve)
            phase_end(dve, "relations")
            node_vector(dve, 3)
            phase_end(dve, "nodes 3")
            for r in range(2):
                e4_vector(dve, r)
                phase_end(dve, f"messages {r}")
                cell_vector(dve, r)
                phase_end(dve, f"cell {r}")

        @block.sync
        def _(sp):
            prep_sync(sp)
            sort_sync(sp)
            order_sync(sp)
            phase_end(sp, "prepare")
            e0_sync(sp)
            phase_end(sp, "edges 0")
            node_sync(sp, 0, None, agg0, x)
            phase_end(sp, "nodes 0")
            for r in range(2):
                e1_sync(sp, r)
                phase_end(sp, f"logits {r}")
                softmax_sync(sp, r)
                phase_end(sp, f"softmax {r}")
                e2_sync(sp, r)
                phase_end(sp, f"values {r}")
                node_sync(sp, 1 + r, conv_in[r], agg, (None, x1)[r])
                phase_end(sp, f"nodes {1 + r}")
            e3_sync(sp)
            phase_end(sp, "relations")
            node_sync(sp, 3, x2, agg, None)
            phase_end(sp, "nodes 3")
            for r in range(2):
                e4_sync(sp, r)
                phase_end(sp, f"messages {r}")
                cell_sync(sp, r, (x3, v1)[r])
                phase_end(sp, f"cell {r}")

        @block.tensor
        def _(pe):
            prep_tensor(pe)
            order_tensor(pe)
            phase_end(pe, "prepare")
            e0_tensor(pe)
            phase_end(pe, "edges 0")
            phase_end(pe, "nodes 0")
            for r in range(2):
                e1_tensor(pe, r)
                phase_end(pe, f"logits {r}")
                softmax_tensor(pe, r)
                phase_end(pe, f"softmax {r}")
                e2_tensor(pe, r)
                phase_end(pe, f"values {r}")
                node_tensor(pe, 1 + r)
                phase_end(pe, f"nodes {1 + r}")
            e3_tensor(pe)
            phase_end(pe, "relations")
            node_tensor(pe, 3)
            phase_end(pe, "nodes 3")
            for r in range(2):
                e4_tensor(pe, r)
                phase_end(pe, f"messages {r}")
                cell_tensor(pe, r)
                phase_end(pe, f"cell {r}")

        @block.scalar
        def _(act):
            prep_scalar(act)
            act.wait_ge(agg0_zero, 16 * (NP * D // (P * ZCOLS) + 1))
            phase_end(act, "prepare")
            e0_scalar(act)
            act.wait_ge(tables_zero, 16 * (NP * (D + AW) // (P * ZCOLS)))
            phase_end(act, "edges 0")
            node_scalar(act, 0)
            phase_end(act, "nodes 0")
            for r in range(2):
                e1_scalar(act, r)
                phase_end(act, f"logits {r}")
                softmax_scalar(act, r)
                phase_end(act, f"softmax {r}")
                e2_scalar(act, r)
                phase_end(act, f"values {r}")
                node_scalar(act, 1 + r)
                phase_end(act, f"nodes {1 + r}")
            e3_scalar(act)
            phase_end(act, "relations")
            node_scalar(act, 3)
            phase_end(act, "nodes 3")
            for r in range(2):
                e4_scalar(act, r)
                phase_end(act, f"messages {r}")
                cell_scalar(act, r)
                phase_end(act, f"cell {r}")


_INS = ["x", "src", "dst", "edge_attr_16", "edge_type_32", "edge_weight", "edge_weight_n2", "L0_gnn_Wq", "L0_gnn_Wk",
        "L0_gnn_Wv"]
_CONV = [f"L1_gnn_l{layer}_{kind}{name}" for layer in (1, 2) for name in "qkvs" for kind in "wb"]
_REST = ["L2_gnn_basis", "L2_gnn_coeff", "L2_gnn_self_weight", "L2_gnn_bias", "L3_gnn_W_msg", "L3_gnn_b_msg",
         "L3_gnn_W_ih", "L3_gnn_W_hh", "L3_gnn_b_ih", "L3_gnn_b_hh"]


def kernel(**inputs):
    import numpy as _np
    import concourse.bacc as _bacc
    from concourse import mybir as _mybir
    from concourse.bass_utils import run_bass_kernel_spmd as _run

    nc = _bacc.Bacc("TRN2", target_bir_lowering=False, num_devices=1)
    arrays, aps = {}, {}
    for name in _INS + _CONV + _REST:
        a = _np.ascontiguousarray(inputs[name])
        arrays[f"in_{name}_dram"] = a
        aps[name] = nc.dram_tensor(f"in_{name}_dram", a.shape, _mybir.dt.from_np(a.dtype), kind="ExternalInput").ap()
    shape = inputs["x"].shape
    out = nc.dram_tensor("out_0_dram", shape, _mybir.dt.from_np(_np.dtype("float32")), kind="ExternalOutput").ap()
    conv = [[aps[f"L1_gnn_l{layer}_{kind}{name}"] for layer in (1, 2)] for name in "qkvs" for kind in "wb"]
    gnn_kernel(nc, *(aps[n] for n in _INS), *conv, *(aps[n] for n in _REST), out)
    r = _run(nc, [arrays], core_ids=[0])
    return r.results[0]["out_0_dram"]
```

```python
from contextlib import ExitStack

import concourse.bass as bass
from concourse import mybir

F32 = mybir.dt.float32
I32 = mybir.dt.int32
ALU = mybir.AluOpType
ACT = mybir.ActivationFunctionType
AX = mybir.AxisListType.X

P = 128
SLOTS = 4
GROUP = P * SLOTS
ROWS = 8
CHUNK = P * ROWS
CROWS = 4
CCHUNK = P * CROWS
BIG = 1e30
NOWHERE = 1 << 20
EPS = 1e-5
META = 8
M_SRC, M_DST, M_LAST, M_W, M_SRCF, M_DSTF, M_RDEG, M_TYPE = range(META)
UNROLL = 4
PEEL = 2
NEWTON = 3
ROOT_STEPS = 2 + 4 * NEWTON
RANK_CHUNK = 896
ZCOLS = 3584


def wait(eng, sem, value):
    if isinstance(value, int) and value <= 0:
        return
    eng.wait_ge(sem, value)


def pipeline(eng, items, *stages, tail=0):
    stages = [s if isinstance(s, tuple) else (n, s) for n, s in enumerate(stages)]
    loops = items // UNROLL - tail

    def step(i, u):
        for d, stage in stages:
            back = -((u - d) // UNROLL)
            at = i - back
            if isinstance(at, int) and not 0 <= UNROLL * i + u - d < items:
                continue
            stage(at, u - d + back * UNROLL)

    for i in range(PEEL):
        for u in range(UNROLL):
            step(i, u)
    with eng.Fori(PEEL, loops) as i:
        for u in range(UNROLL):
            step(i, u)
    for n in range(UNROLL * loops, items + max(d for d, _ in stages)):
        step(n // UNROLL, n % UNROLL)


class Steps:

    def __init__(self, eng, sem):
        self.eng, self.sem, self.n = eng, sem, 0

    def __call__(self, ins):
        self.n += 1
        ins.then_inc(self.sem, 1)
        self.eng.wait_ge(self.sem, self.n)


def gnn_kernel(nc, x, src, dst, attr, etype, ew, ew2, Wq0, Wk0, Wv0, wq, bq, wk, bk, wv, bv, ws, bs,
               basis, coeff, self_w, rel_bias, Wmsg, bmsg, Wih, Whh, bih, bhh, out):
    N, D = x.shape
    E = src.shape[0]
    NA = attr.shape[1]
    H0, FH = Wq0.shape[0], Wq0.shape[1]
    H1 = wq[0].shape[1] // D
    NREL, NB = coeff.shape
    NPAIR = NREL // 2
    GI = 3 * D
    NG = -(-E // GROUP)
    NG += NG % 2
    EP = NG * GROUP
    EC = EP // P
    NCH = -(-N // CHUNK)
    NCH += NCH % 2
    NP = NCH * CHUNK
    NCC = NP // CCHUNK
    AW = D + 32
    EW = D + NA + 1
    PARTS, REST = E // EC, E % EC
    LAST_PARTS = (N - (NCH - 1) * CHUNK) // ROWS
    C_FULL, C_PARTS = N // CCHUNK, N % CCHUNK // CROWS
    NBC = D * D // 512
    assert (N - (NCH - 1) * CHUNK) % ROWS == 0 and 0 < LAST_PARTS <= P and N % CROWS == 0
    assert D == 64 and H0 * FH == D and H1 * D == P and NA == 16 and NCC % 4 == 0 and REST > 1
    assert N + NOWHERE < 1 << 24 and EP % RANK_CHUNK == 0 and NP * D % (P * ZCOLS) == 0

    ctx = ExitStack()
    with ctx:
        prep_only = ExitStack()

        def sb(name, shape, dt=F32, life=ctx):
            return life.enter_context(nc.sbuf_tensor(name, shape, dt))

        def sem(name):
            return ctx.enter_context(nc.semaphore(name))

        def pair(name, shape, dt=F32, n=2):
            return [sb(f"{name}{k}", shape, dt) for k in range(n)]

        def sems(name, n=2):
            return [sem(f"{name}{k}") for k in range(n)]

        def dram(name, shape, dt=F32):
            return nc.dram_tensor(name, shape, dt).ap()

        x1, h1, x2, x3, v1 = (dram(n, (NP, D)) for n in ("x1", "h1", "x2", "x3", "v1"))
        agg0 = dram("agg0", (NP + GROUP, D))
        agg = dram("agg", (NP, D))
        aggw = dram("aggw", (NP, AW))
        meta_d, attr_d = dram("meta_d", (EP, META)), dram("attr_d", (EP, NA))
        srec_d, satt_d, key_d = dram("srec_d", (EP, META)), dram("satt_d", (EP, NA)), dram("key_d", (EP,))
        srcf_d, type_d, same_d = (dram(n, (EP,)) for n in ("srcf_d", "type_d", "same_d"))
        tgt_d = dram("tgt_d", (EP + 2,))
        logit_d, coef_d = dram("logit_d", (H1, EP)), dram("coef_d", (H1, EP))
        xst_d = dram("xst_d", (NG, D, GROUP))
        relw_d = dram("relw_d", (NREL, D * D))

        ident = sb("ident", [P, P])
        later = sb("later", [P, SLOTS, GROUP])
        trash = sb("trash", [P, SLOTS])
        ones_row, ones_col = sb("ones_row", [1, P]), sb("ones_col", [P, 1])
        stops = sb("stops", [1, 2])
        zeros = sb("zeros", [P, ZCOLS])
        qkv_w = sb("qkv_w", [D, 3 * D])
        wk_t, wq_t = pair("wk_t", [P, P]), pair("wq_t", [P, P])
        wv_t = pair("wv_t", [D, P])
        bias_t = sb("bias_t", [P, 2, 3])
        head_sum = sb("head_sum", [P, H1])
        head_mean = sb("head_mean", [P, D])
        lin_w = pair("lin_w", [P, P], n=3)
        lin_b = pair("lin_b", [1, ROWS * D], n=3)
        rel_w = sb("rel_w", [P, NPAIR, D])
        rel_id = sb("rel_id", [P, NPAIR])
        gate_w = pair("gate_w", [P, GI])
        gate_v = pair("gate_v", [96, 4 * D])

        roww = pair("roww", [P, SLOTS, AW], n=UNROLL)
        scan = pair("scan", [P, GROUP], n=UNROLL)
        cell_in = pair("cell_in", [P, CROWS, D + AW + D], n=4)
        psame, nsame, pneg, nneg = (sb(n, [P, EC]) for n in ("psame", "nsame", "pneg", "nneg"))
        ends2 = sb("ends2", [P, 4, H1])
        ends_row = sb("ends_row", [H1, 4, P])
        flag, flag_i = sb("flag", [P, 1]), sb("flag_i", [1, 1], I32)
        sc_a, sc_b, sc_c = (sb(n, [P, H1, EC]) for n in ("sc_a", "sc_b", "sc_c"))
        end_col, in_col = sb("end_col", [P, H1]), sb("in_col", [P, H1])
        end_row, in_row = sb("end_row", [H1, P]), sb("in_row", [H1, P + 1])

        def once(name, shape, dt=F32):
            return sb(name, shape, dt, prep_only)

        src_i, dst_i, next_i, type_i = (once(n, [P, EC], I32) for n in ("src_i", "dst_i", "next_i", "type_i"))
        w1_t, w2_t = once("w1_t", [P, EC]), once("w2_t", [P, EC])
        rec = once("rec", [P, EC, META])
        att = once("att", [P, EC, NA])
        colf = once("colf", [P, 5, EC])
        basis_t, relw_t = once("basis_t", [NB, D * D]), once("relw_t", [NREL, D * D])
        coeff_t, coeffT = once("coeff_t", [NREL, NB]), once("coeffT", [NB, NREL])
        raw_w = once("raw_w", [P, 4, P])
        raw_h = once("raw_h", [P, 2, D])
        turned_w = once("turned_w", [P, 2, GI])
        whhT = [once(f"whhT{r}", [D, GI]) for r in range(2)]

        s_key, s_pos, s_lt, s_eq = (once(n, [P, RANK_CHUNK]) for n in ("s_key", "s_pos", "s_lt", "s_eq"))
        s_cur, s_cnt = once("s_cur", [P, 3]), once("s_cnt", [P, 2])
        s_posc, s_rank = once("s_posc", [P, EC]), once("s_rank", [P, EC])
        s_rec, s_att, s_idx = once("s_rec", [P, META]), once("s_att", [P, NA]), once("s_idx", [P, 1], I32)
        prep_only.close()

        edge_only = ExitStack()

        def esb(name, shape, dt=F32):
            return sb(name, shape, dt, edge_only)

        def epair(name, shape, dt=F32, n=UNROLL):
            return [esb(f"{name}{k}", shape, dt) for k in range(n)]

        meta = epair("meta", [P, SLOTS, META])
        rowb = epair("rowb", [P, GROUP])
        sameb = epair("sameb", [P, GROUP])
        rows = epair("rows", [P, SLOTS, P])
        turn = epair("turn", [P, GROUP])
        fmaj = epair("fmaj", [P, GROUP], n=2)
        prod = epair("prod", [P, GROUP])
        outr = epair("outr", [P, SLOTS, AW])
        outd = epair("outd", [P, SLOTS, D])
        idx = epair("idx", [P, SLOTS], I32)
        eq = epair("eq", [P, SLOTS, GROUP])
        junk = esb("junk", [P, SLOTS, GROUP])
        cnt, gap, shift = epair("cnt", [P, SLOTS]), epair("gap", [P, SLOTS]), epair("shift", [P, SLOTS])
        q_t, qk_t, msg_t = epair("q_t", [P, SLOTS, D]), epair("qk_t", [P, SLOTS, D]), epair("msg_t", [P, SLOTS, D])
        al_t, aw_t = epair("al_t", [P, SLOTS, H0]), epair("aw_t", [P, SLOTS, H0])
        logit = epair("logit", [H1, GROUP])

        edge_only.close()

        node_a, node_g, node_r = (pair(n, [P, ROWS, D], n=UNROLL) for n in ("node_a", "node_g", "node_r"))
        node_t, node_p, node_y = (pair(n, [P, ROWS, D], n=UNROLL) for n in ("node_t", "node_p", "node_y"))
        node_c, node_q, node_o = (pair(n, [P, ROWS, D], n=UNROLL) for n in ("node_c", "node_q", "node_o"))
        node_s, node_v, node_i = (pair(n, [P, ROWS], n=UNROLL) for n in ("node_s", "node_v", "node_i"))
        cell_t, cell_u = pair("cell_t", [P, CROWS * P]), pair("cell_u", [96, CROWS * P])
        cell_rz = pair("cell_rz", [P, CROWS, 2 * D])
        H_AT, S_AT, E_AT, DEG_AT = D + AW, D, 2 * D, 2 * D + NA

        ps = ctx.enter_context(nc.psum_tensor("ps", [P, 8, 512], F32))

        phase_done, passed = sem("phase_done"), sem("passed")
        ends_of = {}

        def phase_end(eng, name):
            n = ends_of.setdefault(name, len(ends_of) + 1)
            eng.drain().then_inc(phase_done, 1)
            eng.wait_ge(phase_done, 5 * n)

        def steady(eng):
            eng.sem_inc(passed, 1)

        def spread(flat, parts):
            return flat.unsqueeze(0).broadcast_to([parts, flat.shape[0]])

        def group_of(flat, i, k):
            return flat[bass.ds((UNROLL * i + k) * GROUP, GROUP)]

        def to_row(t, n=GROUP):
            return t.rearrange("f (j p) -> f p j", j=SLOTS)

        def in_order(t):
            return t.rearrange("f (p j) -> f p j", j=SLOTS)

        def slot_of(t, j):
            return t.rearrange("f (p j) -> f j p", j=SLOTS)[:, j, :]

        const_ready, in_ready, w_ready, dve_step = (sem(n) for n in ("const_ready", "in_ready", "w_ready", "dve_step"))
        raw_ready, pe_turned, act_moved, rel_stored = (
            sem(n) for n in ("raw_ready", "pe_turned", "act_moved", "rel_stored"))
        w_late = sem("w_late")
        agg0_zero, tables_zero = sem("agg0_zero"), sem("tables_zero")
        flag_sum, flag_set = sem("flag_sum"), sem("flag_set")
        sort_key, sort_in, sort_counted, sort_staged, sort_put, sort_back = (
            sem(n) for n in ("sort_key", "sort_in", "sort_counted", "sort_staged", "sort_put", "sort_back"))
        tgt_stored, tgt_in, recs_stored = sem("tgt_stored"), sem("tgt_in"), sem("recs_stored")
        end_ready, end_turned = sem("end_ready"), sem("end_turned")
        said = {}

        def consts(pool):
            g = nc.gpsimd
            n = [0]

            def const(ins):
                n[0] += 1
                ins.then_inc(const_ready, 1)
                pool.wait_ge(const_ready, n[0])

            const(g.memset(zeros[:], 0.0))
            blank = [(ident, 0.0), (later, 1.0), (ones_row, 1.0), (ones_col, 1.0), (qkv_w, 0.0), (head_sum, 0.0)]
            blank += [(t, 0.0) for t in wk_t + wq_t + gate_v + lin_w + roww + cell_in + scan]
            blank += [(dst_i, N), (next_i, N), (src_i, 0), (type_i, 0), (w1_t, 0.0), (w2_t, 0.0), (att, 0.0)]
            for t, v in blank:
                const(g.memset(t[:], v))
            const(g.memset(stops[0:1, 0:1], -1.0))
            const(g.memset(stops[0:1, 1:2], -2.0))
            said["blank"] = n[0]
            const(g.affine_select(out=ident[:], in_=ident[:], compare_op=ALU.not_equal, fill=1.0, base=0,
                                  pattern=[[-1, P]], channel_multiplier=1))
            const(g.affine_select(out=later[:], in_=later[:], compare_op=ALU.is_gt, fill=0.0, base=0,
                                  pattern=[[-1, SLOTS], [1, GROUP]], channel_multiplier=-SLOTS))
            const(g.memset(head_sum[0:D, 0:1], float(D) ** -0.5))
            const(g.memset(head_sum[D:P, 1:2], float(D) ** -0.5))
            const(g.iota(trash[:], pattern=[[1, SLOTS]], base=NP, channel_multiplier=SLOTS,
                         allow_small_or_imprecise_dtypes=True))
            const(g.iota(rel_id[0:D, :], pattern=[[2, NPAIR]], base=0, channel_multiplier=0,
                         allow_small_or_imprecise_dtypes=True))
            const(g.iota(rel_id[D:P, :], pattern=[[2, NPAIR]], base=1, channel_multiplier=0,
                         allow_small_or_imprecise_dtypes=True))
            for t in roww:
                const(g.memset(t[:, :, D + NA:D + NA + 1], 1.0))
            for t in cell_in:
                const(g.memset(t[:, :, DEG_AT + 1:DEG_AT + 3], 1.0))
            said["const"] = n[0]

        N_LOADS = 14

        def prep_sync(sp):
            sp.wait_ge(const_ready, said["blank"])
            for t, flat, at in ((dst_i, dst, 0), (src_i, src, 0), (type_i, etype, 0), (w1_t, ew, 0),
                                (w2_t, ew2, 0), (next_i, dst, 1)):
                sp.dma_start(t[0:PARTS, :], flat[at:at + PARTS * EC].rearrange("(p c) -> p c", c=EC)) \
                  .then_inc(in_ready, 16)
                sp.dma_start(t[PARTS:PARTS + 1, 0:REST - at], flat[at + PARTS * EC:E].unsqueeze(0)) \
                  .then_inc(in_ready, 16)
            sp.dma_start(att[0:PARTS, :, :], attr[0:PARTS * EC, :].rearrange("(p c) a -> p c a", c=EC)) \
              .then_inc(in_ready, 16)
            sp.dma_start(att[PARTS:PARTS + 1, 0:REST, :], attr[PARTS * EC:E, :].unsqueeze(0)).then_inc(in_ready, 16)
            n = [0]

            def put(to, of):
                n[0] += 1
                with nc.allow_non_contiguous_dma(reason="small weights"):
                    sp.dma_start(to, of).then_inc(w_ready, 16)

            put(basis_t[:], basis.rearrange("b i o -> b (i o)"))
            put(coeff_t[:], coeff[:, :])
            for m, w in enumerate((Wq0, Wk0, Wv0)):
                for h in range(H0):
                    put(qkv_w[h * FH:(h + 1) * FH, m * D + h * FH:m * D + (h + 1) * FH], w[h])
            for r in range(2):
                put(wk_t[r][0:D, :], wk[r][:, :])
                put(wq_t[r][D:P, :], wq[r][:, :])
                put(wv_t[r][:], wv[r][:, :])
                for m, b in enumerate((bk[r], bq[r], bv[r])):
                    put(bias_t[:, r, m:m + 1], b.unsqueeze(1))
                put(gate_v[r][NA + 1:NA + 2, 0:GI], bih[r:r + 1, :])
                put(gate_v[r][NA + 2:NA + 3, 0:2 * D], bhh[r:r + 1, 0:2 * D])
                put(gate_v[r][NA + 2:NA + 3, GI:GI + D], bhh[r:r + 1, 2 * D:GI])
            for m, (w, b) in enumerate(((ws[0], bs[0]), (ws[1], bs[1]), (self_w, rel_bias))):
                put(lin_w[m][0:D, 0:D], w[:, :])
                put(lin_w[m][D:P, D:P], w[:, :])
                for c in range(ROWS):
                    put(lin_b[m][0:1, c * D:(c + 1) * D], b.unsqueeze(0))
            said["weights"] = n[0]
            for r in range(2):
                if r:
                    sp.wait_ge(pe_turned, 1)
                for to, of in ((raw_w[:, 0, :], Wih[r, 0:P, :]), (raw_w[0:GI - P, 1, :], Wih[r, P:GI, :]),
                               (raw_w[:, 2, :], Wmsg[r, 0:P, :]), (raw_w[0:NA, 3, :], Wmsg[r, P:P + NA, :]),
                               (raw_w[NA:NA + 1, 3, :], bmsg[r:r + 1, :]),
                               (raw_h[:, 0, :], Whh[r, 0:P, :]), (raw_h[0:GI - P, 1, :], Whh[r, P:GI, :])):
                    sp.dma_start(to, of).then_inc(raw_ready, 16)
            for r in range(2):
                sp.wait_ge(act_moved, 2 * r + 1)
                sp.dma_start(gate_v[r][32:96, 0:2 * D], whhT[r][:, 0:2 * D]).then_inc(w_late, 16)
                sp.dma_start(gate_v[r][32:96, GI:GI + D], whhT[r][:, 2 * D:GI]).then_inc(w_late, 16)
            sp.wait_ge(act_moved, 5 + NBC)
            sp.dma_start(relw_d[:, :], relw_t[:]).then_inc(rel_stored, 16)
            sp.wait_ge(rel_stored, 16)
            by_pair = relw_d.rearrange("(m t) (i o) -> t i m o", t=2, o=D)
            sp.dma_start(rel_w[0:D, :, :], by_pair[0]).then_inc(w_late, 16)
            sp.dma_start(rel_w[D:P, :, :], by_pair[1]).then_inc(w_late, 16)
            sp.wait_ge(w_late, 16 * 6)

        def prep_tensor(pe):
            t = nc.tensor
            pe.wait_ge(const_ready, said["const"])
            for r in range(2):
                pe.wait_ge(raw_ready, 16 * 7 * (r + 1))
                if r:
                    pe.wait_ge(act_moved, 2)
                t.transpose(ps[:, 0, 0:P], raw_w[:, 0, :], ident[:])
                t.transpose(ps[:, 0, P:GI], raw_w[0:GI - P, 1, :], ident[0:GI - P, 0:GI - P])
                t.transpose(ps[:, 1, 0:P], raw_w[:, 2, :], ident[:])
                t.transpose(ps[:, 1, P:P + NA + 1], raw_w[0:NA + 1, 3, :], ident[0:NA + 1, 0:NA + 1])
                t.transpose(ps[0:D, 2, 0:P], raw_h[:, 0, :], ident[:])
                t.transpose(ps[0:D, 2, P:GI], raw_h[0:GI - P, 1, :], ident[0:GI - P, 0:GI - P]) \
                 .then_inc(pe_turned, 1)
                pe.wait_ge(act_moved, 2 * r + 1)
                t.matmul(ps[:, 3, 0:GI], turned_w[:, 1, 0:P], turned_w[:, 0, :], start=True, stop=True)
                t.matmul(ps[0:NA + 1, 4, 0:GI], turned_w[:, 1, P:P + NA + 1], turned_w[:, 0, :],
                         start=True, stop=True).then_inc(pe_turned, 1)
            pe.wait_ge(w_ready, 16 * said["weights"])
            t.transpose(ps[0:NB, 5, 0:NREL], coeff_t[:], ident[0:NREL, 0:NREL]).then_inc(pe_turned, 1)
            pe.wait_ge(act_moved, 5)
            for c in range(NBC):
                if c >= 2:
                    pe.wait_ge(act_moved, 5 + c - 1)
                t.matmul(ps[0:NREL, 6 + c % 2, :], coeffT[:], basis_t[:, 512 * c:512 * (c + 1)],
                         start=True, stop=True).then_inc(pe_turned, 1)
            pe.wait_ge(dve_step, said["flag"])
            t.matmul(ps[0:1, 5, 0:1], flag[:], ones_col[:], start=True, stop=True).then_inc(flag_sum, 1)

        def prep_scalar(act):
            a = nc.scalar
            act.wait_ge(const_ready, 1)
            for table, zero in ((agg0[0:NP, :], agg0_zero), (agg, tables_zero), (aggw, tables_zero)):
                flat = table.rearrange("(p c) d -> p (c d)", p=P)
                for c in range(flat.shape[1] // ZCOLS):
                    act.dma_start(flat[:, ZCOLS * c:ZCOLS * (c + 1)], zeros[:]).then_inc(zero, 16)
            act.dma_start(agg0[NP:NP + GROUP, :].rearrange("(p c) d -> p (c d)", p=P),
                          zeros[:, 0:SLOTS * D]).then_inc(agg0_zero, 16)
            for r in range(2):
                act.wait_ge(pe_turned, 2 * r + 1)
                if r:
                    act.wait_ge(pe_turned, 2)
                a.copy(turned_w[:, 0, :], ps[:, 0, 0:GI])
                a.copy(turned_w[:, 1, 0:P + NA + 1], ps[:, 1, 0:P + NA + 1])
                a.copy(whhT[r][:], ps[0:D, 2, 0:GI]).then_inc(act_moved, 1)
                act.wait_ge(pe_turned, 2 * r + 2)
                a.copy(gate_w[r][:], ps[:, 3, 0:GI])
                a.copy(gate_v[r][0:NA + 1, 0:GI], ps[0:NA + 1, 4, 0:GI]).then_inc(act_moved, 1)
            act.wait_ge(pe_turned, 5)
            a.copy(coeffT[:], ps[0:NB, 5, 0:NREL]).then_inc(act_moved, 1)
            for c in range(NBC):
                act.wait_ge(pe_turned, 6 + c)
                a.copy(relw_t[:, 512 * c:512 * (c + 1)], ps[0:NREL, 6 + c % 2, :]).then_inc(act_moved, 1)

        rec_i = rec[:].bitcast(I32)

        def prep_vector(dve, st):
            v = nc.vector
            dve.wait_ge(const_ready, said["const"])
            st(v.tensor_tensor(head_mean[:], ident[:, 0:D], ident[:, D:P], ALU.add))
            st(v.tensor_scalar(head_mean[:], head_mean[:], 1.0 / H1, None, ALU.mult))
            dve.wait_ge(in_ready, 16 * N_LOADS)
            st(v.tensor_tensor(rec[:, :, M_W], w1_t[:], w2_t[:], ALU.mult))
            st(v.tensor_copy(rec[:, :, M_SRCF], src_i[:]))
            st(v.tensor_copy(rec[:, :, M_DSTF], dst_i[:]))
            st(v.tensor_copy(rec[:, :, M_TYPE], type_i[:]))
            st(v.tensor_copy(rec_i[:, :, M_SRC], src_i[:]))
            st(v.tensor_copy(rec_i[:, :, M_DST], dst_i[:]))
            st(v.tensor_copy(rec_i[:, :, M_LAST], dst_i[:]))
            st(v.memset(rec[:, :, M_RDEG], 0.0))
            st(v.tensor_tensor(colf[:, 0, :], dst_i[:], next_i[:], ALU.is_gt))
            st(v.tensor_reduce(flag[:], colf[:, 0, :], AX, ALU.add))
            said["flag"] = st.n
            dve.wait_ge(flag_sum, 1)
            v.tensor_copy(flag_i[:], ps[0:1, 5, 0:1]).then_inc(flag_set, 1)

        def unsorted(eng):
            eng.wait_ge(flag_set, 1)
            return eng.If(eng.value_load(flag_i[0:1, 0:1]) > 0)

        def sort_sync(sp):
            with unsorted(sp):
                sp.wait_ge(sort_counted, 1)
                sp.dma_start(key_d.rearrange("(p c) -> p c", c=EC), colf[:, 1, :]).then_inc(sort_key, 16)
                sp.wait_ge(sort_key, 16)
                with sp.Fori(0, EP // RANK_CHUNK) as c:
                    sp.wait_ge(sort_counted, c + 1)
                    sp.dma_start(s_key[:], spread(key_d[bass.ds(c * RANK_CHUNK, RANK_CHUNK)], P)) \
                      .then_inc(sort_in, 16)
                sp.wait_ge(sort_put, 32 * EC)
                sp.dma_start(rec[:], srec_d.rearrange("(p c) k -> p c k", c=EC)).then_inc(sort_back, 16)
                sp.dma_start(att[:], satt_d.rearrange("(p c) k -> p c k", c=EC)).then_inc(sort_back, 16)
                sp.wait_ge(sort_back, 32)

        def sort_gpsimd(pool):
            with unsorted(pool):
                nc.gpsimd.iota(s_pos[:], pattern=[[1, RANK_CHUNK]], base=0, channel_multiplier=0,
                               allow_small_or_imprecise_dtypes=True).then_inc(sort_key2, 1)
                nc.gpsimd.iota(s_posc[:], pattern=[[1, EC]], base=0, channel_multiplier=EC,
                               allow_small_or_imprecise_dtypes=True).then_inc(sort_key2, 1)
                with pool.Fori(0, EC) as c:
                    pool.wait_ge(sort_staged, c + 1)
                    steady(pool)
                    for table, of in ((srec_d, s_rec), (satt_d, s_att)):
                        nc.gpsimd.indirect_dma_start(table[:, :], bass.IndirectOffsetOnAxis(ap=s_idx[:, 0:1], axis=0),
                                                     of[:], None).then_inc(sort_put, 16)

        sort_key2 = sem("sort_key2")

        def sort_vector(dve):
            v = nc.vector
            with unsorted(dve):
                v.memset(s_rank[:], 0.0)
                v.tensor_copy(colf[:, 1, :], dst_i[:]).then_inc(sort_counted, 1)
                dve.wait_ge(sort_key2, 2)
                with dve.Fori(0, EP // RANK_CHUNK) as c:
                    dve.wait_ge(sort_in, 16 * c + 16)
                    steady(dve)
                    with dve.Fori(0, EC) as e:
                        v.tensor_copy(s_cur[:, 0:1], colf[:, 1, bass.ds(e, 1)])
                        v.tensor_copy(s_cur[:, 1:2], s_posc[:, bass.ds(e, 1)])
                        v.tensor_copy(s_cur[:, 2:3], s_rank[:, bass.ds(e, 1)])
                        v.drain()
                        v.tensor_scalar(s_lt[:], s_key[:], s_cur[:, 0:1], s_cur[:, 2:3], ALU.is_lt, ALU.add,
                                        accum_out=s_cnt[:, 0:1])
                        v.tensor_scalar(s_eq[:], s_pos[:], s_cur[:, 1:2], None, ALU.is_lt)
                        v.drain()
                        v.scalar_tensor_tensor(s_lt[:], s_key[:], s_cur[:, 0:1], s_eq[:], ALU.is_equal, ALU.mult)
                        v.drain()
                        v.tensor_reduce(s_cnt[:, 1:2], s_lt[:], AX, ALU.add)
                        v.drain()
                        v.tensor_tensor(s_rank[:, bass.ds(e, 1)], s_cnt[:, 0:1], s_cnt[:, 1:2], ALU.add)
                        v.drain()
                    v.tensor_scalar(s_posc[:], s_posc[:], float(-RANK_CHUNK), None, ALU.add)
                    v.drain().then_inc(sort_counted, 1)
                with dve.Fori(0, EC) as e:
                    v.tensor_copy(s_rec[:], rec[:, bass.ds(e, 1), :].rearrange("p o k -> p (o k)"))
                    v.tensor_copy(s_att[:], att[:, bass.ds(e, 1), :].rearrange("p o k -> p (o k)"))
                    v.tensor_copy(s_idx[:], s_rank[:, bass.ds(e, 1)])
                    v.drain().then_inc(sort_staged, 1)
                    dve.wait_ge(sort_put, 32 * e + 32)
                dve.wait_ge(sort_back, 32)

        def seg_scan(dve, n, to, keep, of, op0, op1, start, kind, forward):
            v = nc.vector
            way = slice(None) if forward else slice(None, None, -1)
            last = EC - 1 if forward else 0

            def inside(first):
                for h in range(H1):
                    v.tensor_tensor_scan(to[:, h, way], keep[:, way], of[:, h, way],
                                         start if first else in_col[:, h:h + 1], op0, op1).then_inc(scan_step, 1)
                scan_n[0] += H1
                dve.wait_ge(scan_step, scan_n[0])

            inside(True)
            v.tensor_copy(end_col[:], to[:, :, last]).then_inc(end_ready, 1)
            dve.wait_ge(end_turned, 2 * n + 1)
            v.tensor_copy(end_row[:], ps[0:H1, 7, 0:P]).then_inc(scan_step, 1)
            v.memset(in_row[:], start).then_inc(scan_step, 1)
            scan_n[0] += 2
            dve.wait_ge(scan_step, scan_n[0])
            row = in_row[:, 1:P + 1] if forward else in_row[:, 0:P]
            v.tensor_tensor_scan(row[:, way], ends_row[:, kind, way], end_row[:, way], start, op0, op1) \
             .then_inc(end_ready, 1)
            dve.wait_ge(end_turned, 2 * n + 2)
            v.tensor_copy(in_col[:], ps[:, 6, 0:H1]).then_inc(scan_step, 1)
            scan_n[0] += 1
            dve.wait_ge(scan_step, scan_n[0])
            inside(False)

        scan_step = sem("scan_step")
        scan_n = [0]

        def seg_scan_tensor(pe, n, forward):
            pe.wait_ge(end_ready, 2 * n + 1)
            nc.tensor.transpose(ps[0:H1, 7, 0:P], end_col[:], ident[:]).then_inc(end_turned, 1)
            pe.wait_ge(end_ready, 2 * n + 2)
            row = in_row[:, 0:P] if forward else in_row[:, 1:P + 1]
            nc.tensor.transpose(ps[:, 6, 0:H1], row, ident[0:H1, 0:H1]).then_inc(end_turned, 1)

        PSAME, NSAME, PNEG, NNEG = range(4)

        def order_vector(dve, st):
            v = nc.vector
            for n, m in ((0, M_DSTF), (3, M_SRCF), (4, M_TYPE)):
                st(v.tensor_copy(colf[:, n, :], rec[:, :, m]))
            said["flat"] = st.n
            dve.wait_ge(tgt_in, 32)
            st(v.tensor_tensor(psame[:], colf[:, 0, :], colf[:, 1, :], ALU.is_equal))
            st(v.tensor_tensor(nsame[:], colf[:, 0, :], colf[:, 2, :], ALU.is_equal))
            st(v.tensor_scalar(pneg[:], psame[:], 1.0, BIG, ALU.subtract, ALU.mult))
            st(v.tensor_scalar(nneg[:], nsame[:], 1.0, BIG, ALU.subtract, ALU.mult))
            for kind, t in ((PSAME, psame), (NSAME, nsame), (PNEG, pneg), (NNEG, nneg)):
                for h in range(H1):
                    st(v.tensor_reduce(ends2[:, kind, h:h + 1], t[:], AX, ALU.min))
            said["ends"] = st.n
            dve.wait_ge(ends_turned, 1)
            st(v.tensor_copy(ends_row[:], ps[0:H1, 0, :].rearrange("h (k p) -> h k p", k=4)))
            st(v.memset(sc_a[:], 1.0))
            seg_scan(dve, 0, sc_b, psame, sc_a, ALU.mult, ALU.add, 0.0, PSAME, True)
            st(v.reciprocal(rec[:, :, M_RDEG], sc_b[:, 0, :]))
            st(v.scalar_tensor_tensor(rec_i[:, :, M_LAST], nsame[:], float(NOWHERE), colf[:, 0, :],
                                      ALU.mult, ALU.add))
            st(v.scalar_tensor_tensor(rec_i[:, :, M_DST], colf[:, 0, :], float(N), colf[:, 0, :],
                                      ALU.is_lt, ALU.mult))
            said["records"] = st.n

        ends_turned = sem("ends_turned")

        def order_tensor(pe):
            pe.wait_ge(dve_step, said["ends"])
            for kind in range(4):
                mm = nc.tensor.transpose(ps[0:H1, 0, kind * P:(kind + 1) * P], ends2[:, kind, :], ident[:])
            mm.then_inc(ends_turned, 1)
            seg_scan_tensor(pe, 0, True)

        def order_sync(sp):
            flat = lambda t: t.rearrange("(p c) -> p c", c=EC)
            sp.wait_ge(dve_step, said["flat"])
            sp.dma_start(flat(tgt_d[1:EP + 1]), colf[:, 0, :]).then_inc(tgt_stored, 16)
            sp.dma_start(tgt_d[0:1].unsqueeze(0), stops[0:1, 0:1]).then_inc(tgt_stored, 16)
            sp.dma_start(tgt_d[EP + 1:EP + 2].unsqueeze(0), stops[0:1, 1:2]).then_inc(tgt_stored, 16)
            sp.wait_ge(tgt_stored, 48)
            sp.dma_start(colf[:, 1, :], flat(tgt_d[0:EP])).then_inc(tgt_in, 16)
            sp.dma_start(colf[:, 2, :], flat(tgt_d[2:EP + 2])).then_inc(tgt_in, 16)
            sp.dma_start(flat(srcf_d), colf[:, 3, :]).then_inc(recs_stored, 16)
            sp.dma_start(flat(type_d), colf[:, 4, :]).then_inc(recs_stored, 16)
            sp.dma_start(attr_d.rearrange("(p c) a -> p c a", c=EC), att[:]).then_inc(recs_stored, 16)
            sp.wait_ge(dve_step, said["records"])
            sp.dma_start(flat(same_d), psame[:]).then_inc(recs_stored, 16)
            sp.dma_start(meta_d.rearrange("(p c) k -> p c k", c=EC), rec[:]).then_inc(recs_stored, 16)
            sp.wait_ge(recs_stored, 80)

        def nth(r, i, k):
            return r * NG + UNROLL * i + k + 1

        kinds = {n: sems(n, UNROLL) for n in ("loaded", "gathered", "scattered", "stored", "kept", "extra")}
        loaded, gathered, scattered, stored, kept, extra = kinds.values()
        uses = [("e0", NG, dict(loaded=2, gathered=SLOTS, scattered=SLOTS)), ("n0", NCH, dict(loaded=2, stored=1))]
        for r in range(2):
            uses += [(f"e1{r}", NG, dict(loaded=1, gathered=2 * SLOTS, kept=1, extra=1)),
                     (f"e2{r}", NG, dict(loaded=3 + H1, scattered=SLOTS)),
                     (f"n{1 + r}", NCH, dict(loaded=2 + r, stored=1))]
        uses += [("e3", NG, dict(loaded=3, gathered=SLOTS, scattered=SLOTS)), ("n3", NCH, dict(loaded=2, stored=1))]
        for r in range(2):
            uses += [(f"e4{r}", NG, dict(loaded=3, gathered=SLOTS, scattered=SLOTS)),
                     (f"c{r}", NCC, dict(loaded=2, stored=1, extra=r))]
        base, total = {}, {(kind, k): 0 for kind in kinds for k in range(UNROLL)}
        for phase, items, counts in uses:
            for kind, n in counts.items():
                for k in range(UNROLL):
                    mine = len(range(k, items, UNROLL))
                    base[kind, phase, k] = (total[kind, k], n, mine)
                    total[kind, k] += n * mine

        def landed(kind, phase, i, k):
            before, n, _ = base[kind, phase, k]
            return 16 * (before + n * (i + 1))

        def wait_all(eng, kind, phase):
            for k in range(UNROLL):
                eng.wait_ge(kinds[kind][k], landed(kind, phase, base[kind, phase, k][2] - 1, k))

        def two(k):
            return k % 2

        def record(k, m):
            return lambda j: meta[k][:, j, m:m + 1].bitcast(I32)

        def rows_of(k):
            return lambda j: idx[k][:, j:j + 1]

        def gather(pool, to, table, column, done):
            steady(pool)
            for j in range(SLOTS):
                nc.gpsimd.indirect_dma_start(
                    to[:, j, 0:D] if to.shape[2] != D else to[:, j, :], None, table,
                    bass.IndirectOffsetOnAxis(ap=column(j), axis=0)).then_inc(done, 16)

        def evac(out_, in_):
            return nc.scalar.copy(out_, in_)

        e0_turned, e0_copied, e0_qkv, e0_q, e0_qk, e0_al, e0_aw, e0_msg, e0_eq, e0_cnt, e0_shift, e0_idx, e0_sum, \
            e0_out = (sem(f"e0_{n}") for n in ("turned", "copied", "qkv", "q", "qk", "al", "aw", "msg", "eq", "cnt",
                                               "shift", "idx", "sum", "out"))
        qkv_ps = [ps[:, 2 + 2 * k:4 + 2 * k, :].rearrange("p b n -> p (b n)").rearrange("p (j c) -> p j c", j=SLOTS)
                  for k in range(2)]

        def e0_sync(sp):
            def load(i, k):
                wait(sp, e0_msg, nth(0, i - 1, k))
                steady(sp)
                wait(sp, e0_cnt, nth(0, i - 1, k))
                steady(sp)
                sp.dma_start(meta[k][:], group_rec(i, k)).then_inc(loaded[k], 16)
                sp.dma_start(rowb[k][:], spread(group_of(srcf_d, i, k), P)).then_inc(loaded[k], 16)
            pipeline(sp, NG, load)

        def group_rec(i, k):
            return meta_d[bass.ds((UNROLL * i + k) * GROUP, GROUP), :].rearrange("(p j) m -> p j m", j=SLOTS)

        def e0_gpsimd(pool):
            pool.wait_ge(agg0_zero, 16 * (NP * D // (P * ZCOLS) + 1))

            def take(i, k):
                pool.wait_ge(loaded[k], landed("loaded", "e0", i, k))
                wait(pool, e0_turned, nth(0, i - 1, k))
                gather(pool, rows[k], x[:, :], record(k, M_DST), gathered[k])

            def give(i, k):
                pool.wait_ge(e0_out, nth(0, i, k))
                pool.wait_ge(e0_idx, nth(0, i, k))
                wait(pool, scattered[k - 1], landed("scattered", "e0", i if k else i - 1, (k - 1) % UNROLL))
                steady(pool)
                for j in range(SLOTS):
                    nc.gpsimd.indirect_dma_start(
                        agg0[:, :], bass.IndirectOffsetOnAxis(ap=idx[k][:, j:j + 1], axis=0),
                        outd[k][:, j, :], None, compute_op=ALU.add).then_inc(scattered[k], 16)
            pipeline(pool, NG, take, (3, give))
            wait_all(pool, "scattered", "e0")

        def e0_tensor(pe):
            t = nc.tensor

            def front(i, k):
                pe.wait_ge(gathered[k], landed("gathered", "e0", i, k))
                wait(pe, e0_copied, nth(0, i, k) - 2)
                steady(pe)
                for j in range(SLOTS):
                    mm = t.transpose(ps[0:D, k % 2, j * P:(j + 1) * P], rows[k][:, j, 0:D], ident[:])
                mm.then_inc(e0_turned, 1)

            def middle(i, k):
                pe.wait_ge(e0_copied, nth(0, i, k))
                wait(pe, e0_msg, nth(0, i, k) - 2)
                wait(pe, e0_q, nth(0, i, k) - 2)
                steady(pe)
                for j in range(SLOTS):
                    mm = t.matmul(qkv_ps[k % 2][:, j, 0:3 * D], turn[k][0:D, j * P:(j + 1) * P], qkv_w[:],
                                  start=True, stop=True)
                mm.then_inc(e0_qkv, 1)

            def back(i, k):
                pe.wait_ge(e0_msg, nth(0, i, k))
                pe.wait_ge(e0_eq, nth(0, i, k))
                wait(pe, e0_out, nth(0, i, k) - 2)
                steady(pe)
                for j in range(SLOTS):
                    for m in range(SLOTS):
                        mm = t.matmul(ps[:, 6 + k % 2, j * D:(j + 1) * D], slot_of(eq[k][:, m, :], j),
                                      msg_t[k][:, m, :], start=(m == 0), stop=(m == SLOTS - 1))
                mm.then_inc(e0_sum, 1)
            pipeline(pe, NG, front, middle, back)

        def e0_scalar(act):
            def front(i, k):
                act.wait_ge(e0_turned, nth(0, i, k))
                wait(act, e0_qkv, nth(0, i - 1, k))
                evac(turn[k][0:D, :], ps[0:D, k % 2, :]).then_inc(e0_copied, 1)

            def middle(i, k):
                act.wait_ge(e0_qkv, nth(0, i, k))
                wait(act, e0_qk, nth(0, i - 1, k))
                evac(q_t[k][:], qkv_ps[k % 2][:, :, 0:D]).then_inc(e0_q, 1)

            def back(i, k):
                act.wait_ge(e0_sum, nth(0, i, k))
                wait(act, scattered[k], landed("scattered", "e0", i - 1, k))
                evac(outd[k][:], ps[:, 6 + k % 2, 0:SLOTS * D].rearrange("p (j d) -> p j d", j=SLOTS)) \
                    .then_inc(e0_out, 1)
            pipeline(act, NG, front, middle, back)

        def e0_vector(dve):
            v = nc.vector

            def match(i, k):
                dve.wait_ge(loaded[k], landed("loaded", "e0", i, k))
                wait(dve, e0_sum, nth(0, i - 1, k))
                for j in range(SLOTS):
                    op = v.tensor_scalar(eq[k][:, j, :], rowb[k][:], meta[k][:, j, M_SRCF:M_SRCF + 1], None,
                                         ALU.is_equal)
                op.then_inc(e0_eq, 1)
                dve.wait_ge(e0_eq, nth(0, i, k))
                for j in range(SLOTS):
                    v.tensor_tensor_reduce(junk[:, j, :], eq[k][:, j, :], later[:, j, :], 1.0, 0.0, ALU.mult, ALU.add,
                                           cnt[k][:, j:j + 1])
                v.tensor_tensor(gap[k][:], trash[:], meta[k][:, :, M_SRCF], ALU.subtract).then_inc(e0_cnt, 1)
                dve.wait_ge(e0_cnt, nth(0, i, k))
                v.scalar_tensor_tensor(shift[k][:], cnt[k][:], 0.0, gap[k][:], ALU.is_gt, ALU.mult) \
                 .then_inc(e0_shift, 1)
                dve.wait_ge(e0_shift, nth(0, i, k))
                wait(dve, scattered[k], landed("scattered", "e0", i - 1, k))
                v.tensor_tensor(idx[k][:], shift[k][:], meta[k][:, :, M_SRCF], ALU.add).then_inc(e0_idx, 1)

            def message(i, k):
                dve.wait_ge(e0_q, nth(0, i, k))
                v.tensor_tensor(qk_t[k][:], q_t[k][:], qkv_ps[k % 2][:, :, D:2 * D], ALU.mult).then_inc(e0_qk, 1)
                dve.wait_ge(e0_qk, nth(0, i, k))
                v.tensor_reduce(al_t[k][:], qk_t[k][:].rearrange("p j (h f) -> p j h f", f=FH), AX, ALU.add) \
                 .then_inc(e0_al, 1)
                dve.wait_ge(e0_al, nth(0, i, k))
                v.scalar_tensor_tensor(aw_t[k][:], al_t[k][:], float(FH) ** -0.5,
                                       meta[k][:, :, M_W].unsqueeze(2).broadcast_to([P, SLOTS, H0]),
                                       ALU.mult, ALU.mult).then_inc(e0_aw, 1)
                dve.wait_ge(e0_aw, nth(0, i, k))
                wait(dve, e0_sum, nth(0, i - 1, k))
                v.tensor_tensor(msg_t[k][:].rearrange("p j (h f) -> p j h f", f=FH),
                                qkv_ps[k % 2][:, :, 2 * D:3 * D].rearrange("p j (h f) -> p j h f", f=FH),
                                aw_t[k][:].unsqueeze(3).broadcast_to([P, SLOTS, H0, FH]), ALU.mult) \
                 .then_inc(e0_msg, 1)

            pipeline(dve, NG, match, message)

        e1_turned, e1_copied, e1_qk, e1_k, e1_prod, e1_sum, e1_logit = (
            sem(f"e1_{n}") for n in ("turned", "copied", "qk", "k", "prod", "sum", "logit"))

        def e1_sync(sp, r):
            def load(i, k):
                wait(sp, gathered[k], landed("gathered", f"e1{r}", i - 1, k))
                steady(sp)
                sp.dma_start(meta[k][:], group_rec(i, k)).then_inc(loaded[k], 16)
            pipeline(sp, NG, load)

        def e1_gpsimd(pool, r, table):
            def take(i, k):
                pool.wait_ge(loaded[k], landed("loaded", f"e1{r}", i, k))
                wait(pool, e1_turned, nth(r, i - 1, k))
                for at, m in ((0, M_SRC), (D, M_DST)):
                    gather(pool, rows[k][:, :, at:at + D], table, record(k, m), gathered[k])
            pipeline(pool, NG, take)

        def e1_tensor(pe, r):
            t = nc.tensor

            def front(i, k):
                pe.wait_ge(gathered[k], landed("gathered", f"e1{r}", i, k))
                wait(pe, e1_copied, nth(r, i, k) - 2)
                steady(pe)
                for j in range(SLOTS):
                    mm = t.transpose(ps[:, k % 2, j * P:(j + 1) * P], rows[k][:, j, :], ident[:])
                mm.then_inc(e1_turned, 1)

            def middle(i, k):
                pe.wait_ge(e1_copied, nth(r, i, k))
                wait(pe, e1_prod, nth(r, i, k) - 2)
                t.matmul(ps[:, 2 + k % 2, :], wk_t[r][:], turn[k][:], start=True, stop=True)
                t.matmul(ps[:, 4 + k % 2, :], wq_t[r][:], turn[k][:], start=True, stop=True).then_inc(e1_qk, 1)

            def back(i, k):
                pe.wait_ge(e1_prod, nth(r, i, k))
                wait(pe, e1_logit, nth(r, i, k) - 2)
                t.matmul(ps[0:H1, 6 + k % 2, :], head_sum[:], prod[k][:], start=True, stop=True).then_inc(e1_sum, 1)
            pipeline(pe, NG, front, middle, back)

        def e1_scalar(act, r):
            def front(i, k):
                act.wait_ge(e1_turned, nth(r, i, k))
                wait(act, e1_qk, nth(r, i - 1, k))
                wait(act, kept[k], landed("kept", f"e1{r}", i - 1, k))
                evac(in_order(turn[k][:]), to_row(ps[:, k % 2, :])).then_inc(e1_copied, 1)
                act.wait_ge(e1_copied, nth(r, i, k))
                steady(act)
                act.dma_start(xst_d[bass.ds(UNROLL * i + k, 1), :, :].rearrange("o d c -> (o d) c"), turn[k][0:D, :]) \
                   .then_inc(kept[k], 16)

            def middle(i, k):
                act.wait_ge(e1_qk, nth(r, i, k))
                wait(act, e1_prod, nth(r, i, k) - 2)
                nc.scalar.activation(fmaj[k % 2][:], ps[:, 2 + k % 2, :], ACT.Identity, bias=bias_t[:, r, 0:1]) \
                  .then_inc(e1_k, 1)

            def back(i, k):
                act.wait_ge(e1_sum, nth(r, i, k))
                wait(act, extra[k], landed("extra", f"e1{r}", i - 1, k))
                evac(logit[k][:], ps[0:H1, 6 + k % 2, :]).then_inc(e1_logit, 1)
                act.wait_ge(e1_logit, nth(r, i, k))
                steady(act)
                act.dma_start(logit_d[:, bass.ds((UNROLL * i + k) * GROUP, GROUP)], logit[k][:]).then_inc(extra[k], 16)
            pipeline(act, NG, front, middle, (3, back))
            wait_all(act, "kept", f"e1{r}")
            wait_all(act, "extra", f"e1{r}")

        def e1_vector(dve, r):
            def times(i, k):
                dve.wait_ge(e1_k, nth(r, i, k))
                wait(dve, e1_sum, nth(r, i - 1, k))
                nc.vector.scalar_tensor_tensor(prod[k][:], ps[:, 4 + k % 2, :], bias_t[:, r, 1:2], fmaj[k % 2][:],
                                               ALU.add, ALU.mult).then_inc(e1_prod, 1)
            pipeline(dve, NG, times)

        sm_loaded, sm_shifted, sm_exp, sm_stored = sem("sm_loaded"), sem("sm_shifted"), sem("sm_exp"), sem("sm_stored")
        by_head = lambda t: t.rearrange("h (p c) -> p h c", c=EC)

        def softmax_sync(sp, r):
            sp.dma_start(sc_a[:], by_head(logit_d)).then_inc(sm_loaded, 16)
            sp.wait_ge(dve_step, said["coef", r])
            steady(sp)
            sp.dma_start(by_head(coef_d), sc_c[:]).then_inc(sm_stored, 16)
            sp.wait_ge(sm_stored, 16 * (r + 1))

        def softmax_scalar(act, r):
            act.wait_ge(dve_step, said["shifted", r])
            nc.scalar.activation(sc_c[:], sc_a[:], ACT.Exp).then_inc(sm_exp, 1)

        def softmax_tensor(pe, r):
            for n, forward in enumerate((True, False, True, False)):
                seg_scan_tensor(pe, 1 + 4 * r + n, forward)

        def softmax_vector(dve, st, r):
            v = nc.vector
            n = 1 + 4 * r
            dve.wait_ge(sm_loaded, 16 * (r + 1))
            seg_scan(dve, n, sc_b, pneg, sc_a, ALU.add, ALU.max, -BIG, PNEG, True)
            seg_scan(dve, n + 1, sc_c, nneg, sc_b, ALU.add, ALU.max, -BIG, NNEG, False)
            st(v.tensor_tensor(sc_a[:], sc_a[:], sc_c[:], ALU.subtract))
            said["shifted", r] = st.n
            dve.wait_ge(sm_exp, r + 1)
            seg_scan(dve, n + 2, sc_b, psame, sc_c, ALU.mult, ALU.add, 0.0, PSAME, True)
            for h in range(H1):
                st(v.tensor_scalar(sc_a[:, h, :], nsame[:], -1.0, 1.0, ALU.mult, ALU.add))
            st(v.tensor_tensor(sc_b[:], sc_b[:], sc_a[:], ALU.mult))
            seg_scan(dve, n + 3, sc_a, nsame, sc_b, ALU.mult, ALU.add, 0.0, NSAME, False)
            st(v.tensor_scalar(sc_a[:], sc_a[:], 1e-16, None, ALU.add))
            st(v.reciprocal(sc_b[:], sc_a[:]))
            st(v.tensor_tensor(sc_c[:], sc_c[:], sc_b[:], ALU.mult))
            said["coef", r] = st.n

        e2_v, e2_prod, e2_scan, e2_sum, e2_out, e2_idx = (
            sem(f"e2_{n}") for n in ("v", "prod", "scan", "sum", "out", "idx"))

        def give_rows(pool, table, of, column, done):
            steady(pool)
            for j in range(SLOTS):
                nc.gpsimd.indirect_dma_start(
                    table, bass.IndirectOffsetOnAxis(ap=column(j), axis=0), of[:, j, :], None,
                    bounds_check=N - 1, oob_is_err=False).then_inc(done, 16)

        def e2_sync(sp, r):
            def load(i, k):
                wait(sp, e2_idx, nth(r, i - 1, k))
                steady(sp)
                wait(sp, e2_scan, nth(r, i - 1, k))
                steady(sp)
                sp.dma_start(turn[k][0:D, :], xst_d[bass.ds(UNROLL * i + k, 1), :, :].rearrange("o d c -> (o d) c")) \
                  .then_inc(loaded[k], 16)
                for h in range(H1):
                    sp.dma_start(rowb[k][h * D:(h + 1) * D, :], spread(group_of(coef_d[h], i, k), D)) \
                      .then_inc(loaded[k], 16)
                sp.dma_start(sameb[k][:], spread(group_of(same_d, i, k), P)).then_inc(loaded[k], 16)
                sp.dma_start(meta[k][:], group_rec(i, k)).then_inc(loaded[k], 16)
            pipeline(sp, NG, load)

        def e2_tensor(pe, r):
            t = nc.tensor

            def front(i, k):
                pe.wait_ge(loaded[k], landed("loaded", f"e2{r}", i, k))
                wait(pe, e2_prod, nth(r, i, k) - 2)
                t.matmul(ps[:, k % 2, :], wv_t[r][:], turn[k][0:D, :], start=True, stop=True).then_inc(e2_v, 1)

            def back(i, k):
                pe.wait_ge(e2_scan, nth(r, i, k))
                wait(pe, e2_out, nth(r, i, k) - 2)
                steady(pe)
                for j in range(SLOTS):
                    mm = t.matmul(ps[:, 2 + k % 2, j * D:(j + 1) * D], slot_of(scan[k][:], j), head_mean[:],
                                  start=True, stop=True)
                mm.then_inc(e2_sum, 1)
            pipeline(pe, NG, front, back)

        def run_scan(dve, i, k, rows_, of, done, r):
            dve.wait_ge(done, nth(r, i, k) - 1) if not (isinstance(i, int) and nth(r, i, k) == 1) else None
            nc.vector.tensor_tensor_scan(scan[k][0:rows_, :], sameb[k][0:rows_, :], of,
                                         scan[k - 1][0:rows_, GROUP - 1:GROUP], ALU.mult, ALU.add) \
              .then_inc(done, 1)

        def e2_vector(dve, r):
            def weigh(i, k):
                dve.wait_ge(e2_v, nth(r, i, k))
                nc.vector.scalar_tensor_tensor(prod[k][:], ps[:, k % 2, :], bias_t[:, r, 2:3], rowb[k][:],
                                               ALU.add, ALU.mult).then_inc(e2_prod, 1)
                dve.wait_ge(e2_prod, nth(r, i, k))
                wait(dve, e2_sum, nth(r, i - 1, k))
                run_scan(dve, i, k, P, prod[k][:], e2_scan, r)
                wait(dve, scattered[k], landed("scattered", f"e2{r}", i - 1, k))
                nc.vector.tensor_copy(idx[k][:], meta[k][:, :, M_LAST].bitcast(I32)).then_inc(e2_idx, 1)
            pipeline(dve, NG, weigh)

        def e2_scalar(act, r):
            def back(i, k):
                act.wait_ge(e2_sum, nth(r, i, k))
                wait(act, scattered[k], landed("scattered", f"e2{r}", i - 1, k))
                evac(outd[k][:], ps[:, 2 + k % 2, 0:SLOTS * D].rearrange("p (j d) -> p j d", j=SLOTS)) \
                    .then_inc(e2_out, 1)
            pipeline(act, NG, back)

        def e2_gpsimd(pool, r):
            def give(i, k):
                pool.wait_ge(e2_out, nth(r, i, k))
                pool.wait_ge(e2_idx, nth(r, i, k))
                give_rows(pool, agg[:, :], outd[k], rows_of(k), scattered[k])
            pipeline(pool, NG, give)
            wait_all(pool, "scattered", f"e2{r}")

        e3_twice, e3_turned, e3_copied, e3_masked, e3_used, e3_msg, e3_scan, e3_sum, e3_out, e3_idx = (
            sem(f"e3_{n}") for n in ("twice", "turned", "copied", "masked", "used", "msg", "scan", "sum", "out", "idx"))

        def e3_sync(sp):
            def load(i, k):
                wait(sp, gathered[k], landed("gathered", "e3", i - 1, k))
                steady(sp)
                wait(sp, e3_scan, nth(0, i - 1, k))
                steady(sp)
                wait(sp, e3_out, nth(0, i - 1, k))
                steady(sp)
                sp.dma_start(meta[k][:], group_rec(i, k)).then_inc(loaded[k], 16)
                sp.dma_start(rowb[k][:], spread(group_of(type_d, i, k), P)).then_inc(loaded[k], 16)
                sp.dma_start(sameb[k][0:D, :], spread(group_of(same_d, i, k), D)).then_inc(loaded[k], 16)
            pipeline(sp, NG, load)

        def e3_gpsimd(pool):
            def take(i, k):
                pool.wait_ge(loaded[k], landed("loaded", "e3", i, k))
                wait(pool, e3_turned, nth(0, i - 1, k))
                gather(pool, rows[k], x2[:, :], record(k, M_SRC), gathered[k])

            def give(i, k):
                pool.wait_ge(e3_out, nth(0, i, k))
                give_rows(pool, agg[:, :], outd[k], rows_of(k), scattered[k])
            pipeline(pool, NG, take, (4, give))
            wait_all(pool, "scattered", "e3")

        def e3_tensor(pe):
            t = nc.tensor

            def front(i, k):
                pe.wait_ge(e3_twice, nth(0, i, k))
                wait(pe, e3_copied, nth(0, i, k) - 2)
                steady(pe)
                for j in range(SLOTS):
                    mm = t.transpose(ps[:, k % 2, j * P:(j + 1) * P], rows[k][:, j, :], ident[:])
                mm.then_inc(e3_turned, 1)

            def middle(i, k):
                wait(pe, e3_scan, nth(0, i, k) - 2)
                for m in range(NPAIR):
                    pe.wait_ge(e3_masked, (nth(0, i, k) - 1) * NPAIR + m + 1)
                    mm = t.matmul(ps[0:D, 2 + k % 2, :], rel_w[:, m, :], prod[m % UNROLL][:],
                                  start=(m == 0), stop=(m == NPAIR - 1))
                    mm.then_inc(e3_used, 1)

            def back(i, k):
                pe.wait_ge(e3_scan, nth(0, i, k))
                wait(pe, e3_out, nth(0, i, k) - 2)
                steady(pe)
                for j in range(SLOTS):
                    mm = t.transpose(ps[:, 4 + k % 2, j * D:(j + 1) * D], slot_of(scan[k][0:D, :], j), ident[0:D, 0:D])
                mm.then_inc(e3_sum, 1)
            pipeline(pe, NG, (0, front), (1, middle), (2, back))

        def e3_scalar(act):
            def front(i, k):
                act.wait_ge(gathered[k], landed("gathered", "e3", i, k))
                evac(rows[k][:, :, D:P], rows[k][:, :, 0:D]).then_inc(e3_twice, 1)
                act.wait_ge(e3_turned, nth(0, i, k))
                wait(act, e3_used, NPAIR * nth(0, i - 1, k))
                evac(in_order(turn[k][:]), to_row(ps[:, k % 2, :])).then_inc(e3_copied, 1)
            pipeline(act, NG, front)

        def e3_vector(dve):
            v = nc.vector

            def mask(i, k):
                dve.wait_ge(e3_copied, nth(0, i, k))
                dve.wait_ge(loaded[k], landed("loaded", "e3", i, k))
                for m in range(NPAIR):
                    if m >= 4:
                        dve.wait_ge(e3_used, (nth(0, i, k) - 1) * NPAIR + m - 3)
                    else:
                        wait(dve, e3_used, (nth(0, i, k) - 1) * NPAIR + m - 3)
                    v.scalar_tensor_tensor(prod[m % UNROLL][:], rowb[k][:], rel_id[:, m:m + 1], turn[k][:],
                                           ALU.is_equal, ALU.mult).then_inc(e3_masked, 1)

            def add(i, k):
                dve.wait_ge(e3_used, NPAIR * nth(0, i, k))
                wait(dve, e3_sum, nth(0, i - 1, k))
                run_scan(dve, i, k, D, ps[0:D, 2 + k % 2, :], e3_scan, 0)

            def back(i, k):
                wait(dve, scattered[k], landed("scattered", "e3", i - 1, k))
                v.tensor_copy(idx[k][:], meta[k][:, :, M_LAST].bitcast(I32)).then_inc(e3_idx, 1)
                dve.wait_ge(e3_sum, nth(0, i, k))
                dve.wait_ge(e3_idx, nth(0, i, k))
                v.tensor_tensor(outd[k][:], ps[:, 4 + k % 2, 0:SLOTS * D].rearrange("p (j d) -> p j d", j=SLOTS),
                                meta[k][:, :, M_RDEG].unsqueeze(2).broadcast_to([P, SLOTS, D]), ALU.mult) \
                 .then_inc(e3_out, 1)
            pipeline(dve, NG, (1, mask), (2, add), (3, back))

        e4_turned, e4_copied, e4_scan, e4_sum, e4_out, e4_idx = (
            sem(f"e4_{n}") for n in ("turned", "copied", "scan", "sum", "out", "idx"))

        def e4_sync(sp, r):
            def load(i, k):
                wait(sp, e4_turned, nth(r, i - 1, k))
                steady(sp)
                wait(sp, e4_idx, nth(r, i - 1, k))
                steady(sp)
                wait(sp, gathered[k], landed("gathered", f"e4{r}", i - 1, k))
                steady(sp)
                wait(sp, e4_scan, nth(r, i - 1, k))
                steady(sp)
                sp.dma_start(meta[k][:], group_rec(i, k)).then_inc(loaded[k], 16)
                sp.dma_start(roww[k][:, :, D:D + NA], attr_d[bass.ds((UNROLL * i + k) * GROUP, GROUP), :]
                             .rearrange("(p j) a -> p j a", j=SLOTS)).then_inc(loaded[k], 16)
                sp.dma_start(sameb[k][0:AW, :], spread(group_of(same_d, i, k), AW)).then_inc(loaded[k], 16)
            pipeline(sp, NG, load)

        def e4_gpsimd(pool, r, table):
            def take(i, k):
                pool.wait_ge(loaded[k], landed("loaded", f"e4{r}", i, k))
                wait(pool, e4_turned, nth(r, i - 1, k))
                gather(pool, roww[k], table, record(k, M_SRC), gathered[k])

            def give(i, k):
                pool.wait_ge(e4_out, nth(r, i, k))
                pool.wait_ge(e4_idx, nth(r, i, k))
                give_rows(pool, aggw[:, :], outr[k], rows_of(k), scattered[k])
            pipeline(pool, NG, take, (2, give))
            wait_all(pool, "scattered", f"e4{r}")

        def e4_tensor(pe, r):
            t = nc.tensor

            def front(i, k):
                pe.wait_ge(gathered[k], landed("gathered", f"e4{r}", i, k))
                wait(pe, e4_copied, nth(r, i, k) - 2)
                steady(pe)
                for j in range(SLOTS):
                    mm = t.transpose(ps[0:AW, k % 2, j * P:(j + 1) * P], roww[k][:, j, :], ident[:])
                mm.then_inc(e4_turned, 1)

            def back(i, k):
                pe.wait_ge(e4_scan, nth(r, i, k))
                wait(pe, e4_out, nth(r, i, k) - 2)
                steady(pe)
                for j in range(SLOTS):
                    mm = t.transpose(ps[:, 2 + k % 2, j * AW:(j + 1) * AW], slot_of(scan[k][0:AW, :], j),
                                     ident[0:AW, 0:AW])
                mm.then_inc(e4_sum, 1)
            pipeline(pe, NG, front, back)

        def e4_scalar(act, r):
            def front(i, k):
                act.wait_ge(e4_turned, nth(r, i, k))
                wait(act, e4_scan, nth(r, i - 1, k))
                evac(in_order(turn[k][0:AW, :]), to_row(ps[0:AW, k % 2, :])).then_inc(e4_copied, 1)

            def back(i, k):
                act.wait_ge(e4_sum, nth(r, i, k))
                wait(act, scattered[k], landed("scattered", f"e4{r}", i - 1, k))
                evac(outr[k][:], ps[:, 2 + k % 2, 0:SLOTS * AW].rearrange("p (j d) -> p j d", j=SLOTS)) \
                    .then_inc(e4_out, 1)
            pipeline(act, NG, front, back)

        def e4_vector(dve, r):
            def add(i, k):
                dve.wait_ge(e4_copied, nth(r, i, k))
                dve.wait_ge(loaded[k], landed("loaded", f"e4{r}", i, k))
                wait(dve, e4_sum, nth(r, i - 1, k))
                run_scan(dve, i, k, AW, turn[k][0:AW, :], e4_scan, r)
                wait(dve, scattered[k], landed("scattered", f"e4{r}", i - 1, k))
                nc.vector.tensor_copy(idx[k][:], meta[k][:, :, M_LAST].bitcast(I32)).then_inc(e4_idx, 1)
            pipeline(dve, NG, add)

        HAS_LINEAR, HAS_NORM = (0, 1, 1, 1), (1, 0, 1, 1)
        nd_turned, nd_copied, nd_mm, nd_part, nd_y, nd_s, nd_c, nd_q, nd_v, nd_i, nd_o = (
            sem(f"nd_{n}") for n in ("turned", "copied", "mm", "part", "y", "s", "c", "q", "v", "i", "o"))

        nd_w = sem("nd_w")
        node_e, node_w = (pair(n, [P, ROWS], n=UNROLL) for n in ("node_e", "node_w"))

        def nd(r, i, k):
            return r * NCH + UNROLL * i + k + 1

        def nd_lin(r, i, k):
            return sum(HAS_LINEAR[:r]) * NCH + UNROLL * i + k + 1

        def nd_nrm(r, i, k):
            return sum(HAS_NORM[:r]) * NCH + UNROLL * i + k + 1

        def chunk_of(table, i, k, parts=P):
            return table[bass.ds((UNROLL * i + k) * CHUNK, parts * ROWS), :].rearrange("(p c) d -> p c d", c=ROWS)

        def node_sync(sp, r, a, g, res):
            def load(i, k):
                wait(sp, nd_y, nd(r, i - 1, k))
                last = r == 0 and isinstance(i, int) and UNROLL * i + k == NCH - 1
                parts = LAST_PARTS if last else P
                for t, of in ((node_a[k], a), (node_g[k], g), (node_r[k], res)):
                    if of is not None:
                        n = parts if of is x else P
                        sp.dma_start(t[0:n], chunk_of(of, i, k, n)).then_inc(loaded[k], 16)
            pipeline(sp, NCH, load)

        def node_tensor(pe, r):
            t = nc.tensor
            w, b = lin_w[r - 1], lin_b[r - 1]

            def front(i, k):
                pe.wait_ge(loaded[k], landed("loaded", f"n{r}", i, k))
                wait(pe, nd_copied, nd_lin(r, i, k) - 2)
                for c in range(0, ROWS, 2):
                    mm = t.transpose(ps[:, k % 2, c * D:(c + 2) * D], node_a[k][:, c:c + 2, :].rearrange("p c d -> p (c d)"),
                                     ident[:])
                mm.then_inc(nd_turned, 1)

            def back(i, k):
                pe.wait_ge(nd_copied, nd_lin(r, i, k))
                wait(pe, nd_y, nd(r, i, k) - 2)
                t.matmul(ps[:, 2 + k % 2, :], ones_row[:], b[:], start=True, stop=False, skip_group_check=True)
                for c in range(0, ROWS, 2):
                    mm = t.matmul(ps[:, 2 + k % 2, c * D:(c + 2) * D], node_t[k][:, c:c + 2, :].rearrange("p c d -> p (c d)"),
                                  w[:], start=False, stop=True, skip_group_check=True)
                mm.then_inc(nd_mm, 1)
            pipeline(pe, NCH, front, back)

        def node_scalar(act, r):
            def front(i, k):
                act.wait_ge(nd_turned, nd_lin(r, i, k))
                wait(act, nd_mm, nd_lin(r, i - 1, k))
                evac(node_t[k][:].rearrange("p c d -> p (c d)"), ps[:, k % 2, :]).then_inc(nd_copied, 1)

            def square(i, k):
                act.wait_ge(nd_c, nd_nrm(r, i, k))
                wait(act, nd_v, nd_nrm(r, i - 1, k))
                nc.scalar.activation(node_q[k][:], node_c[k][:], ACT.Square).then_inc(nd_q, 1)
            pipeline(act, NCH, *([(0, front)] if HAS_LINEAR[r] else []), *([(2, square)] if HAS_NORM[r] else []))

        def node_vector(dve, r):
            v = nc.vector

            def add(i, k):
                y = node_y[k] if HAS_NORM[r] else node_o[k]
                dve.wait_ge(loaded[k], landed("loaded", f"n{r}", i, k))
                if not HAS_NORM[r]:
                    wait(dve, stored[k], landed("stored", f"n{r}", i - 1, k))
                if HAS_LINEAR[r]:
                    dve.wait_ge(nd_mm, nd_lin(r, i, k))
                mm = ps[:, 2 + k % 2, :].rearrange("p (c d) -> p c d", d=D)
                if r == 0:
                    v.tensor_tensor(y[:], node_r[k][:], node_g[k][:], ALU.add).then_inc(nd_y, 1)
                elif r == 1:
                    v.tensor_tensor(y[:], mm, node_g[k][:], ALU.add).then_inc(nd_y, 1)
                else:
                    v.tensor_tensor(node_p[k][:], mm, node_g[k][:], ALU.add).then_inc(nd_part, 1)
                    dve.wait_ge(nd_part, (r - 2) * NCH + UNROLL * i + k + 1)
                    v.tensor_tensor(y[:], node_p[k][:], node_r[k][:] if r == 2 else node_a[k][:], ALU.add) \
                     .then_inc(nd_y, 1)
                if HAS_NORM[r]:
                    center(dve, k, y, nd_y, nd(r, i, k), nd_nrm(r, i, k))

            def spread_of(i, k):
                variance(dve, k, ROWS, nd_nrm(r, i, k))

            def scale(i, k):
                wait(dve, stored[k], landed("stored", f"n{r}", i - 1, k))
                norm(dve, k, node_o[k], nd_nrm(r, i, k))
            pipeline(dve, NCH, *([(3, scale), (2, spread_of), (1, add)] if HAS_NORM[r] else [(1, add)]))

        def center(dve, k, y, y_ready, ready, n):
            v = nc.vector
            rows_ = y.shape[1]
            dve.wait_ge(y_ready, ready)
            v.tensor_reduce(node_s[k][:, 0:rows_], y[:], AX, ALU.add).then_inc(nd_s, 1)
            dve.wait_ge(nd_s, n)
            v.scalar_tensor_tensor(node_c[k][:, 0:rows_, :], node_s[k][:, 0:rows_].unsqueeze(2).broadcast_to([P, rows_, D]),
                                   -1.0 / D, y[:], ALU.mult, ALU.add).then_inc(nd_c, 1)

        def variance(dve, k, rows_, n):
            dve.wait_ge(nd_q, n)
            nc.vector.tensor_reduce(node_v[k][:, 0:rows_], node_q[k][:, 0:rows_, :], AX, ALU.add).then_inc(nd_v, 1)

        def inverse_root(pool, k, rows_, n):
            g = nc.gpsimd
            var, root_, work = (t[k][:, 0:rows_] for t in (node_e, node_i, node_w))
            done = [(n - 1) * ROOT_STEPS]

            def step(ins):
                done[0] = done[0] + 1
                ins.then_inc(nd_w, 1)
                pool.wait_ge(nd_w, done[0])
                steady(pool)

            pool.wait_ge(nd_v, n)
            steady(pool)
            step(g.tensor_scalar(var, node_v[k][:, 0:rows_], D * EPS, None, ALU.add))
            step(g.tensor_scalar(root_.bitcast(I32), var.bitcast(I32), -0.5, float(0x5f3759df), ALU.mult, ALU.add))
            for _ in range(NEWTON):
                step(g.tensor_tensor(work, root_, root_, ALU.mult))
                step(g.tensor_tensor(work, work, var, ALU.mult))
                step(g.tensor_scalar(work, work, -0.5, 1.5, ALU.mult, ALU.add))
                step(g.tensor_tensor(root_, root_, work, ALU.mult))
            g.engine_nop().then_inc(nd_i, 1)

        def norm(dve, k, to, n):
            rows_ = to.shape[1]
            dve.wait_ge(nd_i, n)
            nc.vector.scalar_tensor_tensor(to[:], node_c[k][:, 0:rows_, :], float(D) ** 0.5,
                                           node_i[k][:, 0:rows_].unsqueeze(2).broadcast_to([P, rows_, D]),
                                           ALU.mult, ALU.mult).then_inc(nd_o, 1)

        def node_gpsimd(pool, r, to):
            def store(i, k):
                if HAS_NORM[r]:
                    pool.wait_ge(nd_o, nd_nrm(r, i, k))
                else:
                    pool.wait_ge(nd_y, nd(r, i, k))
                steady(pool)
                pool.dma_start(chunk_of(to, i, k), node_o[k][:]).then_inc(stored[k], 16)

            def root(i, k):
                wait(pool, nd_o, nd_nrm(r, i - 1, k))
                inverse_root(pool, k, ROWS, nd_nrm(r, i, k))
            pipeline(pool, NCH, *([root, store] if HAS_NORM[r] else [store]))
            wait_all(pool, "stored", f"n{r}")

        gc_dh, gc_turned, gc_copied, gc_mm, gc_rz, gc_rn, gc_pre, gc_n, gc_d, gc_zd, gc_h, gc_y = (
            sem(f"gc_{n}") for n in ("dh", "turned", "copied", "mm", "rz", "rn", "pre", "n", "d", "zd", "h", "y"))
        cell_n, cell_p, cell_d, cell_z = (pair(n, [P, CROWS, D]) for n in ("cell_n", "cell_p", "cell_d", "cell_z"))
        cell_q, cell_h, cell_y = (pair(n, [P, CROWS, D]) for n in ("cell_q", "cell_h", "cell_y"))
        cell_o = pair("cell_o", [P, CROWS, D], n=UNROLL)
        cell_r = pair("cell_r", [P, CROWS, D], n=4)
        gate_ps = [ps[:, 4 + 2 * k:6 + 2 * k, :].rearrange("p b n -> p (b n)").rearrange("p (c n) -> p c n", c=CROWS)
                   for k in range(2)]

        def gc(r, i, u):
            return r * NCC + UNROLL * i + u + 1

        def cell_chunk(table, i, u, parts=P):
            return table[bass.ds((UNROLL * i + u) * CCHUNK, parts * CROWS), :].rearrange("(p c) d -> p c d", c=CROWS)

        def cell_sync(sp, r, h):
            def load(i, u):
                wait(sp, gc_h, gc(r, i, u) - 4)
                steady(sp)
                sp.dma_start(cell_in[u][:, :, H_AT:H_AT + D], cell_chunk(h, i, u)).then_inc(loaded[u], 16)
                sp.dma_start(cell_in[u][:, :, S_AT:S_AT + EW], aggw[bass.ds((UNROLL * i + u) * CCHUNK, CCHUNK), 0:EW]
                             .rearrange("(p c) d -> p c d", c=CROWS)).then_inc(loaded[u], 16)
                if r == 1:
                    wait(sp, gc_y, UNROLL * i + u + 1 - 4)
                    steady(sp)
                    sp.dma_start(cell_r[u][:], cell_chunk(x3, i, u)).then_inc(extra[u], 16)
            pipeline(sp, NCC, load)

        def cell_tensor(pe, r):
            t = nc.tensor

            def turn_in(i, u):
                k = u % 2
                pe.wait_ge(gc_dh, gc(r, i, u))
                wait(pe, gc_copied, gc(r, i, u) - 2)
                for c in range(CROWS):
                    t.transpose(ps[:, k % 2, c * P:(c + 1) * P], cell_in[u][:, c, 0:P], ident[:])
                    mm = t.transpose(ps[0:96, 2 + k % 2, c * P:(c + 1) * P], cell_in[u][:, c, P:P + 96], ident[:])
                mm.then_inc(gc_turned, 1)

            def gates(i, u):
                k = u % 2
                pe.wait_ge(gc_copied, gc(r, i, u))
                wait(pe, gc_pre, gc(r, i, u) - 2)
                for c in range(CROWS):
                    t.matmul(gate_ps[k][:, c, :], cell_u[k][:, c * P:(c + 1) * P], gate_v[r][:],
                             start=True, stop=False, skip_group_check=True)
                    mm = t.matmul(gate_ps[k][:, c, 0:GI], cell_t[k][:, c * P:(c + 1) * P], gate_w[r][:],
                                  start=False, stop=True, skip_group_check=True)
                mm.then_inc(gc_mm, 1)
            pipeline(pe, NCC, turn_in, gates)

        def cell_scalar(act, r):
            a = nc.scalar

            def copy(i, u):
                k = u % 2
                act.wait_ge(gc_turned, gc(r, i, u))
                wait(act, gc_mm, gc(r, i, u) - 2)
                evac(cell_t[k][:], ps[:, k % 2, :])
                evac(cell_u[k][:], ps[0:96, 2 + k % 2, :]).then_inc(gc_copied, 1)

            def gates(i, u):
                k = u % 2
                act.wait_ge(gc_mm, gc(r, i, u))
                wait(act, gc_zd, gc(r, i, u) - 2)
                a.activation(cell_rz[k][:], gate_ps[k][:, :, 0:2 * D], ACT.Sigmoid).then_inc(gc_rz, 1)

            def new(i, u):
                k = u % 2
                act.wait_ge(gc_pre, gc(r, i, u))
                wait(act, gc_h, gc(r, i, u) - 2)
                a.activation(cell_n[k][:], cell_p[k][:], ACT.Tanh).then_inc(gc_n, 1)

            def square(i, u):
                k = u % 2
                act.wait_ge(nd_c, sum(HAS_NORM) * NCH + UNROLL * i + u + 1)
                wait(act, nd_v, sum(HAS_NORM) * NCH + UNROLL * i + u + 1 - 2)
                a.activation(node_q[k][:, 0:CROWS, :], node_c[k][:, 0:CROWS, :], ACT.Square).then_inc(nd_q, 1)
            pipeline(act, NCC, copy, gates, new, *([square] if r == 1 else []))

        def cell_vector(dve, r):
            v = nc.vector

            def scale_in(i, u):
                dve.wait_ge(loaded[u], landed("loaded", f"c{r}", i, u))
                v.tensor_tensor(cell_in[u][:, :, 0:D], cell_in[u][:, :, H_AT:H_AT + D],
                                cell_in[u][:, :, DEG_AT:DEG_AT + 1].broadcast_to([P, CROWS, D]), ALU.mult) \
                 .then_inc(gc_dh, 1)

            def gates(i, u):
                k = u % 2
                dve.wait_ge(gc_rz, gc(r, i, u))
                v.tensor_tensor(cell_q[k][:], cell_rz[k][:, :, 0:D], gate_ps[k][:, :, GI:GI + D], ALU.mult) \
                 .then_inc(gc_rn, 1)
                dve.wait_ge(gc_rn, gc(r, i, u))
                wait(dve, gc_n, gc(r, i, u) - 2)
                v.tensor_tensor(cell_p[k][:], cell_q[k][:], gate_ps[k][:, :, 2 * D:GI], ALU.add).then_inc(gc_pre, 1)

            def finish(i, u):
                k = u % 2
                to = cell_o[u] if r == 0 else cell_h[k]
                dve.wait_ge(gc_n, gc(r, i, u))
                v.tensor_tensor(cell_d[k][:], cell_in[u][:, :, H_AT:H_AT + D], cell_n[k][:], ALU.subtract) \
                 .then_inc(gc_d, 1)
                dve.wait_ge(gc_d, gc(r, i, u))
                v.tensor_tensor(cell_z[k][:], cell_rz[k][:, :, D:2 * D], cell_d[k][:], ALU.mult).then_inc(gc_zd, 1)
                dve.wait_ge(gc_zd, gc(r, i, u))
                if r == 0:
                    wait(dve, stored[u], landed("stored", "c0", i - 1, u))
                v.tensor_tensor(to[:], cell_n[k][:], cell_z[k][:], ALU.add).then_inc(gc_h, 1)
                if r == 1:
                    dve.wait_ge(gc_h, gc(r, i, u))
                    dve.wait_ge(extra[u], landed("extra", "c1", i, u))
                    v.tensor_tensor(cell_y[k][:], cell_h[k][:], cell_r[u][:], ALU.add).then_inc(gc_y, 1)
                    center(dve, k, cell_y[k], gc_y, UNROLL * i + u + 1, sum(HAS_NORM) * NCH + UNROLL * i + u + 1)

            def scale(i, u):
                k = u % 2
                wait(dve, stored[u], landed("stored", "c1", i - 1, u))
                norm(dve, k, cell_o[u], sum(HAS_NORM) * NCH + UNROLL * i + u + 1)

            def spread_of(i, u):
                variance(dve, u % 2, CROWS, sum(HAS_NORM) * NCH + UNROLL * i + u + 1)
            pipeline(dve, NCC, *([(4, spread_of)] if r == 1 else []), (0, scale_in), (2, gates), (3, finish),
                     *([(4, scale)] if r == 1 else []))

        def cell_gpsimd(pool, r, to):
            def store(i, u):
                if r == 0:
                    pool.wait_ge(gc_h, gc(r, i, u))
                    steady(pool)
                    pool.dma_start(cell_chunk(to, i, u), cell_o[u][:]).then_inc(stored[u], 16)
                    return
                pool.wait_ge(nd_o, sum(HAS_NORM) * NCH + UNROLL * i + u + 1)
                n = UNROLL * i + u if isinstance(i, int) else 0
                parts = P if n < C_FULL else C_PARTS if n == C_FULL else 0
                if parts:
                    pool.dma_start(cell_chunk(to, i, u, parts), cell_o[u][0:parts]).then_inc(stored[u], 16)

            def root(i, u):
                wait(pool, nd_o, sum(HAS_NORM) * NCH + UNROLL * i + u + 1 - 2)
                inverse_root(pool, u % 2, CROWS, sum(HAS_NORM) * NCH + UNROLL * i + u + 1)
            pipeline(pool, NCC, *([store] if r == 0 else [(3, root), (5, store)]), tail=0 if r == 0 else 2)
            wait_all(pool, "stored", f"c{r}")

        conv_in = (x1, h1)
        block = ctx.enter_context(nc.Block())

        @block.gpsimd
        def _(pool):
            consts(pool)
            sort_gpsimd(pool)
            phase_end(pool, "prepare")
            e0_gpsimd(pool)
            phase_end(pool, "edges 0")
            node_gpsimd(pool, 0, x1)
            phase_end(pool, "nodes 0")
            for r in range(2):
                e1_gpsimd(pool, r, conv_in[r][:, :])
                phase_end(pool, f"logits {r}")
                phase_end(pool, f"softmax {r}")
                e2_gpsimd(pool, r)
                phase_end(pool, f"values {r}")
                node_gpsimd(pool, 1 + r, (h1, x2)[r])
                phase_end(pool, f"nodes {1 + r}")
            e3_gpsimd(pool)
            phase_end(pool, "relations")
            node_gpsimd(pool, 3, x3)
            phase_end(pool, "nodes 3")
            for r in range(2):
                e4_gpsimd(pool, r, (x3, v1)[r][:, :])
                phase_end(pool, f"messages {r}")
                cell_gpsimd(pool, r, (v1, out)[r])
                phase_end(pool, f"cell {r}")

        @block.vector
        def _(dve):
            st = Steps(dve, dve_step)
            prep_vector(dve, st)
            sort_vector(dve)
            order_vector(dve, st)
            phase_end(dve, "prepare")
            e0_vector(dve)
            phase_end(dve, "edges 0")
            node_vector(dve, 0)
            phase_end(dve, "nodes 0")
            for r in range(2):
                e1_vector(dve, r)
                phase_end(dve, f"logits {r}")
                softmax_vector(dve, st, r)
                phase_end(dve, f"softmax {r}")
                e2_vector(dve, r)
                phase_end(dve, f"values {r}")
                node_vector(dve, 1 + r)
                phase_end(dve, f"nodes {1 + r}")
            e3_vector(dve)
            phase_end(dve, "relations")
            node_vector(dve, 3)
            phase_end(dve, "nodes 3")
            for r in range(2):
                e4_vector(dve, r)
                phase_end(dve, f"messages {r}")
                cell_vector(dve, r)
                phase_end(dve, f"cell {r}")

        @block.sync
        def _(sp):
            prep_sync(sp)
            sort_sync(sp)
            order_sync(sp)
            phase_end(sp, "prepare")
            e0_sync(sp)
            phase_end(sp, "edges 0")
            node_sync(sp, 0, None, agg0, x)
            phase_end(sp, "nodes 0")
            for r in range(2):
                e1_sync(sp, r)
                phase_end(sp, f"logits {r}")
                softmax_sync(sp, r)
                phase_end(sp, f"softmax {r}")
                e2_sync(sp, r)
                phase_end(sp, f"values {r}")
                node_sync(sp, 1 + r, conv_in[r], agg, (None, x1)[r])
                phase_end(sp, f"nodes {1 + r}")
            e3_sync(sp)
            phase_end(sp, "relations")
            node_sync(sp, 3, x2, agg, None)
            phase_end(sp, "nodes 3")
            for r in range(2):
                e4_sync(sp, r)
                phase_end(sp, f"messages {r}")
                cell_sync(sp, r, (x3, v1)[r])
                phase_end(sp, f"cell {r}")

        @block.tensor
        def _(pe):
            prep_tensor(pe)
            order_tensor(pe)
            phase_end(pe, "prepare")
            e0_tensor(pe)
            phase_end(pe, "edges 0")
            phase_end(pe, "nodes 0")
            for r in range(2):
                e1_tensor(pe, r)
                phase_end(pe, f"logits {r}")
                softmax_tensor(pe, r)
                phase_end(pe, f"softmax {r}")
                e2_tensor(pe, r)
                phase_end(pe, f"values {r}")
                node_tensor(pe, 1 + r)
                phase_end(pe, f"nodes {1 + r}")
            e3_tensor(pe)
            phase_end(pe, "relations")
            node_tensor(pe, 3)
            phase_end(pe, "nodes 3")
            for r in range(2):
                e4_tensor(pe, r)
                phase_end(pe, f"messages {r}")
                cell_tensor(pe, r)
                phase_end(pe, f"cell {r}")

        @block.scalar
        def _(act):
            prep_scalar(act)
            act.wait_ge(agg0_zero, 16 * (NP * D // (P * ZCOLS) + 1))
            phase_end(act, "prepare")
            e0_scalar(act)
            act.wait_ge(tables_zero, 16 * (NP * (D + AW) // (P * ZCOLS)))
            phase_end(act, "edges 0")
            node_scalar(act, 0)
            phase_end(act, "nodes 0")
            for r in range(2):
                e1_scalar(act, r)
                phase_end(act, f"logits {r}")
                softmax_scalar(act, r)
                phase_end(act, f"softmax {r}")
                e2_scalar(act, r)
                phase_end(act, f"values {r}")
                node_scalar(act, 1 + r)
                phase_end(act, f"nodes {1 + r}")
            e3_scalar(act)
            phase_end(act, "relations")
            node_scalar(act, 3)
            phase_end(act, "nodes 3")
            for r in range(2):
                e4_scalar(act, r)
                phase_end(act, f"messages {r}")
                cell_scalar(act, r)
                phase_end(act, f"cell {r}")


_INS = ["x", "src", "dst", "edge_attr_16", "edge_type_32", "edge_weight", "edge_weight_n2", "L0_gnn_Wq", "L0_gnn_Wk",
        "L0_gnn_Wv"]
_CONV = [f"L1_gnn_l{layer}_{kind}{name}" for layer in (1, 2) for name in "qkvs" for kind in "wb"]
_REST = ["L2_gnn_basis", "L2_gnn_coeff", "L2_gnn_self_weight", "L2_gnn_bias", "L3_gnn_W_msg", "L3_gnn_b_msg",
         "L3_gnn_W_ih", "L3_gnn_W_hh", "L3_gnn_b_ih", "L3_gnn_b_hh"]


def kernel(**inputs):
    import numpy as _np
    import concourse.bacc as _bacc
    from concourse import mybir as _mybir
    from concourse.bass_utils import run_bass_kernel_spmd as _run

    nc = _bacc.Bacc("TRN2", target_bir_lowering=False, num_devices=1)
    arrays, aps = {}, {}
    for name in _INS + _CONV + _REST:
        a = _np.ascontiguousarray(inputs[name])
        arrays[f"in_{name}_dram"] = a
        aps[name] = nc.dram_tensor(f"in_{name}_dram", a.shape, _mybir.dt.from_np(a.dtype), kind="ExternalInput").ap()
    shape = inputs["x"].shape
    out = nc.dram_tensor("out_0_dram", shape, _mybir.dt.from_np(_np.dtype("float32")), kind="ExternalOutput").ap()
    conv = [[aps[f"L1_gnn_l{layer}_{kind}{name}"] for layer in (1, 2)] for name in "qkvs" for kind in "wb"]
    gnn_kernel(nc, *(aps[n] for n in _INS), *conv, *(aps[n] for n in _REST), out)
    r = _run(nc, [arrays], core_ids=[0])
    return r.results[0]["out_0_dram"]
```

```python
from contextlib import ExitStack

import concourse.bass as bass
from concourse import mybir

F32 = mybir.dt.float32
I32 = mybir.dt.int32
ALU = mybir.AluOpType
ACT = mybir.ActivationFunctionType
AX = mybir.AxisListType.X

P = 128
SLOTS = 4
GROUP = P * SLOTS
ROWS = 8
CHUNK = P * ROWS
CROWS = 4
CCHUNK = P * CROWS
BIG = 1e30
NOWHERE = 1 << 20
EPS = 1e-5
META = 8
M_SRC, M_DST, M_LAST, M_W, M_SRCF, M_DSTF, M_RDEG, M_TYPE = range(META)
UNROLL = 4
CELL_UNROLL = 8
PEEL = 2
NEWTON = 3
ROOT_STEPS = 2 + 4 * NEWTON
REFINE_STEPS = 1 + 4
RANK_CHUNK = 896
ZCOLS = 3584


def wait(eng, sem, value):
    if isinstance(value, int) and value <= 0:
        return
    eng.wait_ge(sem, value)


def pipeline(eng, items, *stages, unroll=UNROLL):
    stages = [s if isinstance(s, tuple) else (n, s) for n, s in enumerate(stages)]
    loops = items // unroll

    def step(i, u):
        for d, stage in stages:
            back = -((u - d) // unroll)
            at = i - back
            if isinstance(at, int) and not 0 <= unroll * i + u - d < items:
                continue
            stage(at, u - d + back * unroll)

    for i in range(PEEL):
        for u in range(unroll):
            step(i, u)
    with eng.Fori(PEEL, loops) as i:
        for u in range(unroll):
            step(i, u)
    for n in range(unroll * loops, items + max(d for d, _ in stages)):
        step(n // unroll, n % unroll)


class Steps:

    def __init__(self, eng, sem):
        self.eng, self.sem, self.n = eng, sem, 0

    def __call__(self, ins):
        self.n += 1
        ins.then_inc(self.sem, 1)
        self.eng.wait_ge(self.sem, self.n)


def gnn_kernel(nc, x, src, dst, attr, etype, ew, ew2, Wq0, Wk0, Wv0, wq, bq, wk, bk, wv, bv, ws, bs,
               basis, coeff, self_w, rel_bias, Wmsg, bmsg, Wih, Whh, bih, bhh, out):
    N, D = x.shape
    E = src.shape[0]
    NA = attr.shape[1]
    H0, FH = Wq0.shape[0], Wq0.shape[1]
    H1 = wq[0].shape[1] // D
    NREL, NB = coeff.shape
    HALF = NREL // 2
    NPROD = HALF // 2
    GI = 3 * D
    NG = -(-E // GROUP)
    NG += NG % 2
    EP = NG * GROUP
    EC = EP // P
    NCH = -(-N // CHUNK)
    NCH += NCH % 2
    NP = NCH * CHUNK
    NCC = NP // CCHUNK
    AW = D + 32
    EW = D + NA + 1
    PARTS, REST = E // EC, E % EC
    LAST_PARTS = (N - (NCH - 1) * CHUNK) // ROWS
    C_FULL, C_PARTS = N // CCHUNK, N % CCHUNK // CROWS
    NBC = D * D // 512
    assert (N - (NCH - 1) * CHUNK) % ROWS == 0 and 0 < LAST_PARTS <= P and N % CROWS == 0
    assert D == 64 and H0 * FH == D and H1 * D == P and NA == 16 and NCC % CELL_UNROLL and C_FULL // CELL_UNROLL == NCC // CELL_UNROLL and REST > 1
    assert N + NOWHERE < 1 << 24 and NP % (NG * P) == 0 and EP % RANK_CHUNK == 0 and NP * D % (P * ZCOLS) == 0

    ctx = ExitStack()
    with ctx:
        prep_only = ExitStack()

        def sb(name, shape, dt=F32, life=ctx):
            return life.enter_context(nc.sbuf_tensor(name, shape, dt))

        def sem(name):
            return ctx.enter_context(nc.semaphore(name))

        def pair(name, shape, dt=F32, n=2):
            return [sb(f"{name}{k}", shape, dt) for k in range(n)]

        def sems(name, n=2):
            return [sem(f"{name}{k}") for k in range(n)]

        def dram(name, shape, dt=F32):
            return nc.dram_tensor(name, shape, dt).ap()

        x1, h1, x2, x3, v1 = (dram(n, (NP, D)) for n in ("x1", "h1", "x2", "x3", "v1"))
        agg0 = dram("agg0", (NP + GROUP, D))
        agg = dram("agg", (NP, D))
        aggw = dram("aggw", (NP, AW))
        meta_d, attr_d = dram("meta_d", (EP, META)), dram("attr_d", (EP, NA))
        srec_d, satt_d, key_d = dram("srec_d", (EP, META)), dram("satt_d", (EP, NA)), dram("key_d", (EP,))
        srcf_d, low_d, high_d, same_d = (dram(n, (EP,)) for n in ("srcf_d", "low_d", "high_d", "same_d"))
        tgt_d = dram("tgt_d", (EP + 2,))
        logit_d, coef_d = dram("logit_d", (H1, EP)), dram("coef_d", (H1, EP))
        xst_d = dram("xst_d", (NG, D, GROUP))
        relw_d = dram("relw_d", (NREL, D * D))

        ident = sb("ident", [P, P])
        later = sb("later", [P, SLOTS, GROUP])
        trash = sb("trash", [P, SLOTS])
        eps_col = sb("eps_col", [P, 1])
        ones_row, ones_col = sb("ones_row", [1, P]), sb("ones_col", [P, 1])
        stops = sb("stops", [1, 2])
        zeros = sb("zeros", [P, ZCOLS])
        qkv_w = sb("qkv_w", [D, 3 * D])
        wk_t, wq_t = pair("wk_t", [P, P]), pair("wq_t", [P, P])
        wv_t = pair("wv_t", [D, P])
        bias_t = sb("bias_t", [P, 2, 3])
        head_sum = sb("head_sum", [P, H1])
        head_mean = sb("head_mean", [P, D])
        half_sum = sb("half_sum", [P, D])
        lin_w = pair("lin_w", [P, P], n=3)
        lin_b = pair("lin_b", [1, ROWS * D], n=3)
        rel_w = sb("rel_w", [P, NPROD, P])
        rel_id = sb("rel_id", [P, NPROD])
        upper = sb("upper", [P, 1])
        gate_w = pair("gate_w", [P, GI])
        gate_v = pair("gate_v", [96, 4 * D])

        roww = pair("roww", [P, SLOTS, AW], n=UNROLL)
        scan = pair("scan", [P, GROUP], n=UNROLL)
        psame, nsame, pneg, nneg = (sb(n, [P, EC]) for n in ("psame", "nsame", "pneg", "nneg"))
        ends2 = sb("ends2", [P, 4, H1])
        ends_row = sb("ends_row", [H1, 4, P])
        flag, flag_i = sb("flag", [P, 1]), sb("flag_i", [1, 1], I32)
        sc_a, sc_b, sc_c = (sb(n, [P, H1, EC]) for n in ("sc_a", "sc_b", "sc_c"))
        end_col, in_col = sb("end_col", [P, H1]), sb("in_col", [P, H1])
        end_row, in_row = sb("end_row", [H1, P]), sb("in_row", [H1, P + 1])

        def once(name, shape, dt=F32):
            return sb(name, shape, dt, prep_only)

        src_i, dst_i, next_i, type_i = (once(n, [P, EC], I32) for n in ("src_i", "dst_i", "next_i", "type_i"))
        w1_t, w2_t = once("w1_t", [P, EC]), once("w2_t", [P, EC])
        rec = once("rec", [P, EC, META])
        att = once("att", [P, EC, NA])
        colf = once("colf", [P, 6, EC])
        basis_t, relw_t = once("basis_t", [NB, D * D]), once("relw_t", [NREL, D * D])
        coeff_t, coeffT = once("coeff_t", [NREL, NB]), once("coeffT", [NB, NREL])
        raw_w = once("raw_w", [P, 4, P])
        raw_h = once("raw_h", [P, 2, D])
        turned_w = once("turned_w", [P, 2, GI])
        whhT = [once(f"whhT{r}", [D, GI]) for r in range(2)]

        s_key, s_pos, s_lt, s_eq = (once(n, [P, RANK_CHUNK]) for n in ("s_key", "s_pos", "s_lt", "s_eq"))
        s_cur, s_cnt = once("s_cur", [P, 3]), once("s_cnt", [P, 2])
        s_posc, s_rank = once("s_posc", [P, EC]), once("s_rank", [P, EC])
        s_rec, s_att, s_idx = once("s_rec", [P, META]), once("s_att", [P, NA]), once("s_idx", [P, 1], I32)
        prep_only.close()

        edge_only = ExitStack()

        def esb(name, shape, dt=F32):
            return sb(name, shape, dt, edge_only)

        def epair(name, shape, dt=F32, n=UNROLL):
            return [esb(f"{name}{k}", shape, dt) for k in range(n)]

        meta = epair("meta", [P, SLOTS, META])
        rowb = epair("rowb", [P, GROUP])
        sameb = epair("sameb", [P, GROUP])
        rows = epair("rows", [P, SLOTS, P])
        turn = epair("turn", [P, GROUP])
        fmaj = epair("fmaj", [P, GROUP], n=2)
        prod = epair("prod", [P, GROUP])
        outr = epair("outr", [P, SLOTS, AW])
        outd = epair("outd", [P, SLOTS, D])
        idx = epair("idx", [P, SLOTS], I32)
        eq = epair("eq", [P, SLOTS, GROUP])
        junk = esb("junk", [P, SLOTS, GROUP])
        cnt, gap, shift = epair("cnt", [P, SLOTS]), epair("gap", [P, SLOTS]), epair("shift", [P, SLOTS])
        q_t, qk_t, msg_t = epair("q_t", [P, SLOTS, D]), epair("qk_t", [P, SLOTS, D]), epair("msg_t", [P, SLOTS, D])
        weight, sum_row = epair("weight", [P, SLOTS]), epair("sum_row", [P, SLOTS])
        al_t, aw_t = epair("al_t", [P, SLOTS, H0]), epair("aw_t", [P, SLOTS, H0])
        logit = epair("logit", [H1, GROUP])

        edge_only.close()

        node_c, node_q = (pair(n, [P, ROWS, D], n=UNROLL) for n in ("node_c", "node_q"))
        node_s, node_v, node_i = (pair(n, [P, ROWS], n=UNROLL) for n in ("node_s", "node_v", "node_i"))
        node_e, node_w, node_z, node_j = (pair(n, [P, ROWS], n=UNROLL) for n in ("node_e", "node_w", "node_z", "node_j"))
        node_only = ExitStack()
        node_a, node_g, node_r, node_t, node_p, node_y, node_o = (
            [sb(f"{n}{k}", [P, ROWS, D], F32, node_only) for k in range(UNROLL)]
            for n in ("node_a", "node_g", "node_r", "node_t", "node_p", "node_y", "node_o"))
        node_only.close()

        cell_in = pair("cell_in", [P, CROWS, D + AW + D], n=CELL_UNROLL)
        cell_t, cell_u = pair("cell_t", [P, CROWS * P]), pair("cell_u", [96, CROWS * P])
        cell_rz = pair("cell_rz", [P, CROWS, 2 * D])
        H_AT, S_AT, E_AT, DEG_AT = D + AW, D, 2 * D, 2 * D + NA

        ps = ctx.enter_context(nc.psum_tensor("ps", [P, 8, 512], F32))

        phase_done, passed = sem("phase_done"), sem("passed")
        ends_of = {}

        def phase_end(eng, name):
            n = ends_of.setdefault(name, len(ends_of) + 1)
            eng.drain().then_inc(phase_done, 1)
            eng.wait_ge(phase_done, 5 * n)

        def steady(eng):
            eng.sem_inc(passed, 1)

        def spread(flat, parts):
            return flat.unsqueeze(0).broadcast_to([parts, flat.shape[0]])

        def group_of(flat, i, k):
            return flat[bass.ds((UNROLL * i + k) * GROUP, GROUP)]

        def to_row(t):
            return t.rearrange("f (j p) -> f p j", j=SLOTS)

        def in_order(t):
            return t.rearrange("f (p j) -> f p j", j=SLOTS)

        def slot_of(t, j):
            return t.rearrange("f (p j) -> f j p", j=SLOTS)[:, j, :]

        const_ready, in_ready, w_ready, dve_step = (sem(n) for n in ("const_ready", "in_ready", "w_ready", "dve_step"))
        raw_ready, pe_turned, act_moved, rel_stored = (
            sem(n) for n in ("raw_ready", "pe_turned", "act_moved", "rel_stored"))
        w_late = sem("w_late")
        agg0_zero, tables_zero = sem("agg0_zero"), sem("tables_zero")
        flag_sum, flag_set = sem("flag_sum"), sem("flag_set")
        sort_key, sort_in, sort_counted, sort_staged, sort_put, sort_back = (
            sem(n) for n in ("sort_key", "sort_in", "sort_counted", "sort_staged", "sort_put", "sort_back"))
        tgt_stored, tgt_in, recs_stored = sem("tgt_stored"), sem("tgt_in"), sem("recs_stored")
        end_ready, end_turned = sem("end_ready"), sem("end_turned")
        said = {}

        def consts(pool):
            g = nc.gpsimd
            n = [0]

            def const(ins):
                n[0] += 1
                ins.then_inc(const_ready, 1)
                pool.wait_ge(const_ready, n[0])

            const(g.memset(zeros[:], 0.0))
            blank = [(ident, 0.0), (later, 1.0), (ones_row, 1.0), (ones_col, 1.0), (eps_col, EPS), (upper, 0.0), (qkv_w, 0.0), (head_sum, 0.0)]
            blank += [(t, 0.0) for t in wk_t + wq_t + gate_v + lin_w + roww + scan]
            blank += [(dst_i, N), (next_i, N), (src_i, 0), (type_i, 0), (w1_t, 0.0), (w2_t, 0.0), (att, 0.0)]
            for t, v in blank:
                const(g.memset(t[:], v))
            const(g.memset(stops[0:1, 0:1], -1.0))
            const(g.memset(stops[0:1, 1:2], -2.0))
            said["blank"] = n[0]
            const(g.affine_select(out=ident[:], in_=ident[:], compare_op=ALU.not_equal, fill=1.0, base=0,
                                  pattern=[[-1, P]], channel_multiplier=1))
            const(g.affine_select(out=later[:], in_=later[:], compare_op=ALU.is_gt, fill=0.0, base=0,
                                  pattern=[[-1, SLOTS], [1, GROUP]], channel_multiplier=-SLOTS))
            const(g.memset(head_sum[0:D, 0:1], float(D) ** -0.5))
            const(g.memset(head_sum[D:P, 1:2], float(D) ** -0.5))
            const(g.iota(trash[:], pattern=[[1, SLOTS]], base=NP, channel_multiplier=SLOTS,
                         allow_small_or_imprecise_dtypes=True))
            const(g.memset(upper[D:P, :], 1.0))
            const(g.iota(rel_id[0:D, :], pattern=[[2, NPROD]], base=0, channel_multiplier=0,
                         allow_small_or_imprecise_dtypes=True))
            const(g.iota(rel_id[D:P, :], pattern=[[2, NPROD]], base=1, channel_multiplier=0,
                         allow_small_or_imprecise_dtypes=True))
            for t in roww:
                const(g.memset(t[:, :, D + NA:D + NA + 1], 1.0))
            said["const"] = n[0]

        N_LOADS = 14

        def prep_sync(sp):
            sp.wait_ge(const_ready, said["blank"])
            for t, flat, at in ((dst_i, dst, 0), (src_i, src, 0), (type_i, etype, 0), (w1_t, ew, 0),
                                (w2_t, ew2, 0), (next_i, dst, 1)):
                sp.dma_start(t[0:PARTS, :], flat[at:at + PARTS * EC].rearrange("(p c) -> p c", c=EC)) \
                  .then_inc(in_ready, 16)
                sp.dma_start(t[PARTS:PARTS + 1, 0:REST - at], flat[at + PARTS * EC:E].unsqueeze(0)) \
                  .then_inc(in_ready, 16)
            sp.dma_start(att[0:PARTS, :, :], attr[0:PARTS * EC, :].rearrange("(p c) a -> p c a", c=EC)) \
              .then_inc(in_ready, 16)
            sp.dma_start(att[PARTS:PARTS + 1, 0:REST, :], attr[PARTS * EC:E, :].unsqueeze(0)).then_inc(in_ready, 16)
            n = [0]

            def put(to, of):
                n[0] += 1
                with nc.allow_non_contiguous_dma(reason="small weights"):
                    sp.dma_start(to, of).then_inc(w_ready, 16)

            put(basis_t[:], basis.rearrange("b i o -> b (i o)"))
            put(coeff_t[:], coeff[:, :])
            for m, w in enumerate((Wq0, Wk0, Wv0)):
                for h in range(H0):
                    put(qkv_w[h * FH:(h + 1) * FH, m * D + h * FH:m * D + (h + 1) * FH], w[h])
            for r in range(2):
                put(wk_t[r][0:D, :], wk[r][:, :])
                put(wq_t[r][D:P, :], wq[r][:, :])
                put(wv_t[r][:], wv[r][:, :])
                for m, b in enumerate((bk[r], bq[r], bv[r])):
                    put(bias_t[:, r, m:m + 1], b.unsqueeze(1))
                put(gate_v[r][NA + 1:NA + 2, 0:GI], bih[r:r + 1, :])
                put(gate_v[r][NA + 2:NA + 3, 0:2 * D], bhh[r:r + 1, 0:2 * D])
                put(gate_v[r][NA + 2:NA + 3, GI:GI + D], bhh[r:r + 1, 2 * D:GI])
            for m, (w, b) in enumerate(((ws[0], bs[0]), (ws[1], bs[1]), (self_w, rel_bias))):
                put(lin_w[m][0:D, 0:D], w[:, :])
                put(lin_w[m][D:P, D:P], w[:, :])
                for c in range(ROWS):
                    put(lin_b[m][0:1, c * D:(c + 1) * D], b.unsqueeze(0))
            said["weights"] = n[0]
            for r in range(2):
                if r:
                    sp.wait_ge(pe_turned, 1)
                for to, of in ((raw_w[:, 0, :], Wih[r, 0:P, :]), (raw_w[0:GI - P, 1, :], Wih[r, P:GI, :]),
                               (raw_w[:, 2, :], Wmsg[r, 0:P, :]), (raw_w[0:NA, 3, :], Wmsg[r, P:P + NA, :]),
                               (raw_w[NA:NA + 1, 3, :], bmsg[r:r + 1, :]),
                               (raw_h[:, 0, :], Whh[r, 0:P, :]), (raw_h[0:GI - P, 1, :], Whh[r, P:GI, :])):
                    sp.dma_start(to, of).then_inc(raw_ready, 16)
            for r in range(2):
                sp.wait_ge(act_moved, 2 * r + 1)
                sp.dma_start(gate_v[r][32:96, 0:2 * D], whhT[r][:, 0:2 * D]).then_inc(w_late, 16)
                sp.dma_start(gate_v[r][32:96, GI:GI + D], whhT[r][:, 2 * D:GI]).then_inc(w_late, 16)
            sp.wait_ge(act_moved, 5 + NBC)
            sp.dma_start(relw_d[:, :], relw_t[:]).then_inc(rel_stored, 16)
            sp.wait_ge(rel_stored, 16)
            by_place = relw_d.rearrange("(t q s) (i o) -> s t i q o", t=2, s=2, o=D)
            for rows_ in range(2):
                for cols in range(2):
                    sp.dma_start(rel_w[D * rows_:D * (rows_ + 1), :, D * cols:D * (cols + 1)], by_place[rows_, cols]) \
                      .then_inc(w_late, 16)
            sp.wait_ge(w_late, 16 * 8)

        def prep_tensor(pe):
            t = nc.tensor
            pe.wait_ge(const_ready, said["const"])
            for r in range(2):
                pe.wait_ge(raw_ready, 16 * 7 * (r + 1))
                if r:
                    pe.wait_ge(act_moved, 2)
                t.transpose(ps[:, 0, 0:P], raw_w[:, 0, :], ident[:])
                t.transpose(ps[:, 0, P:GI], raw_w[0:GI - P, 1, :], ident[0:GI - P, 0:GI - P])
                t.transpose(ps[:, 1, 0:P], raw_w[:, 2, :], ident[:])
                t.transpose(ps[:, 1, P:P + NA + 1], raw_w[0:NA + 1, 3, :], ident[0:NA + 1, 0:NA + 1])
                t.transpose(ps[0:D, 2, 0:P], raw_h[:, 0, :], ident[:])
                t.transpose(ps[0:D, 2, P:GI], raw_h[0:GI - P, 1, :], ident[0:GI - P, 0:GI - P]) \
                 .then_inc(pe_turned, 1)
                pe.wait_ge(act_moved, 2 * r + 1)
                t.matmul(ps[:, 3, 0:GI], turned_w[:, 1, 0:P], turned_w[:, 0, :], start=True, stop=True)
                t.matmul(ps[0:NA + 1, 4, 0:GI], turned_w[:, 1, P:P + NA + 1], turned_w[:, 0, :],
                         start=True, stop=True).then_inc(pe_turned, 1)
            pe.wait_ge(w_ready, 16 * said["weights"])
            t.transpose(ps[0:NB, 5, 0:NREL], coeff_t[:], ident[0:NREL, 0:NREL]).then_inc(pe_turned, 1)
            pe.wait_ge(act_moved, 5)
            for c in range(NBC):
                if c >= 2:
                    pe.wait_ge(act_moved, 5 + c - 1)
                t.matmul(ps[0:NREL, 6 + c % 2, :], coeffT[:], basis_t[:, 512 * c:512 * (c + 1)],
                         start=True, stop=True).then_inc(pe_turned, 1)
            pe.wait_ge(dve_step, said["flag"])
            t.matmul(ps[0:1, 5, 0:1], flag[:], ones_col[:], start=True, stop=True).then_inc(flag_sum, 1)

        def clear(act, table, zero):
            flat = table.rearrange("(p c) d -> p (c d)", p=P)
            for c in range(flat.shape[1] // ZCOLS):
                act.dma_start(flat[:, ZCOLS * c:ZCOLS * (c + 1)], zeros[:]).then_inc(zero, 16)

        def clear_piece(act, table, i, k):
            rows_ = NP // NG
            piece = table[bass.ds((UNROLL * i + k) * rows_, rows_), :].rearrange("(p c) d -> p c d", p=P)
            steady(act)
            act.dma_start(piece, zeros[:, 0:rows_ // P * table.shape[1]].rearrange("p (c d) -> p c d", d=table.shape[1])) \
               .then_inc(tables_zero, 16)

        def prep_scalar(act):
            a = nc.scalar
            act.wait_ge(const_ready, 1)
            clear(act, agg0[0:NP, :], agg0_zero)
            act.dma_start(agg0[NP:NP + GROUP, :].rearrange("(p c) d -> p (c d)", p=P),
                          zeros[:, 0:SLOTS * D]).then_inc(agg0_zero, 16)
            for r in range(2):
                act.wait_ge(pe_turned, 2 * r + 1)
                if r:
                    act.wait_ge(pe_turned, 2)
                a.copy(turned_w[:, 0, :], ps[:, 0, 0:GI])
                a.copy(turned_w[:, 1, 0:P + NA + 1], ps[:, 1, 0:P + NA + 1])
                a.copy(whhT[r][:], ps[0:D, 2, 0:GI]).then_inc(act_moved, 1)
                act.wait_ge(pe_turned, 2 * r + 2)
                a.copy(gate_w[r][:], ps[:, 3, 0:GI])
                a.copy(gate_v[r][0:NA + 1, 0:GI], ps[0:NA + 1, 4, 0:GI]).then_inc(act_moved, 1)
            act.wait_ge(pe_turned, 5)
            a.copy(coeffT[:], ps[0:NB, 5, 0:NREL]).then_inc(act_moved, 1)
            for c in range(NBC):
                act.wait_ge(pe_turned, 6 + c)
                a.copy(relw_t[:, 512 * c:512 * (c + 1)], ps[0:NREL, 6 + c % 2, :]).then_inc(act_moved, 1)

        rec_i = rec[:].bitcast(I32)

        def prep_vector(dve, st):
            v = nc.vector
            dve.wait_ge(const_ready, said["const"])
            st(v.tensor_tensor(half_sum[:], ident[:, 0:D], ident[:, D:P], ALU.add))
            st(v.tensor_scalar(head_mean[:], half_sum[:], 1.0 / H1, None, ALU.mult))
            dve.wait_ge(in_ready, 16 * N_LOADS)
            st(v.tensor_tensor(rec[:, :, M_W], w1_t[:], w2_t[:], ALU.mult))
            st(v.tensor_copy(rec[:, :, M_SRCF], src_i[:]))
            st(v.tensor_copy(rec[:, :, M_DSTF], dst_i[:]))
            st(v.tensor_copy(rec[:, :, M_TYPE], type_i[:]))
            st(v.tensor_copy(rec_i[:, :, M_SRC], src_i[:]))
            st(v.tensor_copy(rec_i[:, :, M_DST], dst_i[:]))
            st(v.tensor_copy(rec_i[:, :, M_LAST], dst_i[:]))
            st(v.memset(rec[:, :, M_RDEG], 0.0))
            st(v.tensor_tensor(colf[:, 0, :], dst_i[:], next_i[:], ALU.is_gt))
            st(v.tensor_reduce(flag[:], colf[:, 0, :], AX, ALU.add))
            said["flag"] = st.n
            dve.wait_ge(flag_sum, 1)
            v.tensor_copy(flag_i[:], ps[0:1, 5, 0:1]).then_inc(flag_set, 1)

        def unsorted(eng):
            eng.wait_ge(flag_set, 1)
            return eng.If(eng.value_load(flag_i[0:1, 0:1]) > 0)

        def sort_sync(sp):
            with unsorted(sp):
                sp.wait_ge(sort_counted, 1)
                sp.dma_start(key_d.rearrange("(p c) -> p c", c=EC), colf[:, 1, :]).then_inc(sort_key, 16)
                sp.wait_ge(sort_key, 16)
                with sp.Fori(0, EP // RANK_CHUNK) as c:
                    sp.wait_ge(sort_counted, c + 1)
                    sp.dma_start(s_key[:], spread(key_d[bass.ds(c * RANK_CHUNK, RANK_CHUNK)], P)) \
                      .then_inc(sort_in, 16)
                sp.wait_ge(sort_put, 32 * EC)
                sp.dma_start(rec[:], srec_d.rearrange("(p c) k -> p c k", c=EC)).then_inc(sort_back, 16)
                sp.dma_start(att[:], satt_d.rearrange("(p c) k -> p c k", c=EC)).then_inc(sort_back, 16)
                sp.wait_ge(sort_back, 32)

        def sort_gpsimd(pool):
            with unsorted(pool):
                nc.gpsimd.iota(s_pos[:], pattern=[[1, RANK_CHUNK]], base=0, channel_multiplier=0,
                               allow_small_or_imprecise_dtypes=True).then_inc(sort_key2, 1)
                nc.gpsimd.iota(s_posc[:], pattern=[[1, EC]], base=0, channel_multiplier=EC,
                               allow_small_or_imprecise_dtypes=True).then_inc(sort_key2, 1)
                with pool.Fori(0, EC) as c:
                    pool.wait_ge(sort_staged, c + 1)
                    steady(pool)
                    for table, of in ((srec_d, s_rec), (satt_d, s_att)):
                        nc.gpsimd.indirect_dma_start(table[:, :], bass.IndirectOffsetOnAxis(ap=s_idx[:, 0:1], axis=0),
                                                     of[:], None).then_inc(sort_put, 16)

        sort_key2 = sem("sort_key2")

        def sort_vector(dve):
            v = nc.vector
            with unsorted(dve):
                v.memset(s_rank[:], 0.0)
                v.tensor_copy(colf[:, 1, :], dst_i[:]).then_inc(sort_counted, 1)
                dve.wait_ge(sort_key2, 2)
                with dve.Fori(0, EP // RANK_CHUNK) as c:
                    dve.wait_ge(sort_in, 16 * c + 16)
                    steady(dve)
                    with dve.Fori(0, EC) as e:
                        v.tensor_copy(s_cur[:, 0:1], colf[:, 1, bass.ds(e, 1)])
                        v.tensor_copy(s_cur[:, 1:2], s_posc[:, bass.ds(e, 1)])
                        v.tensor_copy(s_cur[:, 2:3], s_rank[:, bass.ds(e, 1)])
                        v.drain()
                        v.tensor_scalar(s_lt[:], s_key[:], s_cur[:, 0:1], s_cur[:, 2:3], ALU.is_lt, ALU.add,
                                        accum_out=s_cnt[:, 0:1])
                        v.tensor_scalar(s_eq[:], s_pos[:], s_cur[:, 1:2], None, ALU.is_lt)
                        v.drain()
                        v.scalar_tensor_tensor(s_lt[:], s_key[:], s_cur[:, 0:1], s_eq[:], ALU.is_equal, ALU.mult)
                        v.drain()
                        v.tensor_reduce(s_cnt[:, 1:2], s_lt[:], AX, ALU.add)
                        v.drain()
                        v.tensor_tensor(s_rank[:, bass.ds(e, 1)], s_cnt[:, 0:1], s_cnt[:, 1:2], ALU.add)
                        v.drain()
                    v.tensor_scalar(s_posc[:], s_posc[:], float(-RANK_CHUNK), None, ALU.add)
                    v.drain().then_inc(sort_counted, 1)
                with dve.Fori(0, EC) as e:
                    v.tensor_copy(s_rec[:], rec[:, bass.ds(e, 1), :].rearrange("p o k -> p (o k)"))
                    v.tensor_copy(s_att[:], att[:, bass.ds(e, 1), :].rearrange("p o k -> p (o k)"))
                    v.tensor_copy(s_idx[:], s_rank[:, bass.ds(e, 1)])
                    v.drain().then_inc(sort_staged, 1)
                    dve.wait_ge(sort_put, 32 * e + 32)
                dve.wait_ge(sort_back, 32)

        def seg_scan(dve, n, to, keep, of, op0, op1, start, kind, forward):
            v = nc.vector
            way = slice(None) if forward else slice(None, None, -1)
            last = EC - 1 if forward else 0

            def inside(first):
                for h in range(H1):
                    v.tensor_tensor_scan(to[:, h, way], keep[:, way], of[:, h, way],
                                         start if first else in_col[:, h:h + 1], op0, op1).then_inc(scan_step, 1)
                scan_n[0] += H1
                dve.wait_ge(scan_step, scan_n[0])

            inside(True)
            v.tensor_copy(end_col[:], to[:, :, last]).then_inc(end_ready, 1)
            dve.wait_ge(end_turned, 2 * n + 1)
            v.tensor_copy(end_row[:], ps[0:H1, 7, 0:P]).then_inc(scan_step, 1)
            v.memset(in_row[:], start).then_inc(scan_step, 1)
            scan_n[0] += 2
            dve.wait_ge(scan_step, scan_n[0])
            row = in_row[:, 1:P + 1] if forward else in_row[:, 0:P]
            v.tensor_tensor_scan(row[:, way], ends_row[:, kind, way], end_row[:, way], start, op0, op1) \
             .then_inc(end_ready, 1)
            dve.wait_ge(end_turned, 2 * n + 2)
            v.tensor_copy(in_col[:], ps[:, 6, 0:H1]).then_inc(scan_step, 1)
            scan_n[0] += 1
            dve.wait_ge(scan_step, scan_n[0])
            inside(False)

        scan_step = sem("scan_step")
        scan_n = [0]

        def seg_scan_tensor(pe, n, forward):
            pe.wait_ge(end_ready, 2 * n + 1)
            nc.tensor.transpose(ps[0:H1, 7, 0:P], end_col[:], ident[:]).then_inc(end_turned, 1)
            pe.wait_ge(end_ready, 2 * n + 2)
            row = in_row[:, 0:P] if forward else in_row[:, 1:P + 1]
            nc.tensor.transpose(ps[:, 6, 0:H1], row, ident[0:H1, 0:H1]).then_inc(end_turned, 1)

        PSAME, NSAME, PNEG, NNEG = range(4)

        def order_vector(dve, st):
            v = nc.vector
            for n, m in ((0, M_DSTF), (3, M_SRCF)):
                st(v.tensor_copy(colf[:, n, :], rec[:, :, m]))
            st(v.tensor_scalar(colf[:, 5, :], rec[:, :, M_TYPE], float(HALF), None, ALU.is_ge))
            st(v.scalar_tensor_tensor(colf[:, 4, :], colf[:, 5, :], float(-HALF), rec[:, :, M_TYPE],
                                      ALU.mult, ALU.add))
            said["flat"] = st.n
            dve.wait_ge(tgt_in, 32)
            st(v.tensor_tensor(psame[:], colf[:, 0, :], colf[:, 1, :], ALU.is_equal))
            st(v.tensor_tensor(nsame[:], colf[:, 0, :], colf[:, 2, :], ALU.is_equal))
            st(v.tensor_scalar(pneg[:], psame[:], 1.0, BIG, ALU.subtract, ALU.mult))
            st(v.tensor_scalar(nneg[:], nsame[:], 1.0, BIG, ALU.subtract, ALU.mult))
            for kind, t in ((PSAME, psame), (NSAME, nsame), (PNEG, pneg), (NNEG, nneg)):
                for h in range(H1):
                    st(v.tensor_reduce(ends2[:, kind, h:h + 1], t[:], AX, ALU.min))
            said["ends"] = st.n
            dve.wait_ge(ends_turned, 1)
            st(v.tensor_copy(ends_row[:], ps[0:H1, 0, :].rearrange("h (k p) -> h k p", k=4)))
            st(v.memset(sc_a[:], 1.0))
            seg_scan(dve, 0, sc_b, psame, sc_a, ALU.mult, ALU.add, 0.0, PSAME, True)
            st(v.reciprocal(rec[:, :, M_RDEG], sc_b[:, 0, :]))
            st(v.scalar_tensor_tensor(rec_i[:, :, M_LAST], nsame[:], float(NOWHERE), colf[:, 0, :],
                                      ALU.mult, ALU.add))
            st(v.scalar_tensor_tensor(rec_i[:, :, M_DST], colf[:, 0, :], float(N), colf[:, 0, :],
                                      ALU.is_lt, ALU.mult))
            said["records"] = st.n

        ends_turned = sem("ends_turned")

        def order_tensor(pe):
            pe.wait_ge(dve_step, said["ends"])
            for kind in range(4):
                mm = nc.tensor.transpose(ps[0:H1, 0, kind * P:(kind + 1) * P], ends2[:, kind, :], ident[:])
            mm.then_inc(ends_turned, 1)
            seg_scan_tensor(pe, 0, True)

        def order_sync(sp):
            flat = lambda t: t.rearrange("(p c) -> p c", c=EC)
            sp.wait_ge(dve_step, said["flat"])
            sp.dma_start(flat(tgt_d[1:EP + 1]), colf[:, 0, :]).then_inc(tgt_stored, 16)
            sp.dma_start(tgt_d[0:1].unsqueeze(0), stops[0:1, 0:1]).then_inc(tgt_stored, 16)
            sp.dma_start(tgt_d[EP + 1:EP + 2].unsqueeze(0), stops[0:1, 1:2]).then_inc(tgt_stored, 16)
            sp.wait_ge(tgt_stored, 48)
            sp.dma_start(colf[:, 1, :], flat(tgt_d[0:EP])).then_inc(tgt_in, 16)
            sp.dma_start(colf[:, 2, :], flat(tgt_d[2:EP + 2])).then_inc(tgt_in, 16)
            sp.dma_start(flat(srcf_d), colf[:, 3, :]).then_inc(recs_stored, 16)
            sp.dma_start(flat(low_d), colf[:, 4, :]).then_inc(recs_stored, 16)
            sp.dma_start(flat(high_d), colf[:, 5, :]).then_inc(recs_stored, 16)
            sp.dma_start(attr_d.rearrange("(p c) a -> p c a", c=EC), att[:]).then_inc(recs_stored, 16)
            sp.wait_ge(dve_step, said["records"])
            sp.dma_start(flat(same_d), psame[:]).then_inc(recs_stored, 16)
            sp.dma_start(meta_d.rearrange("(p c) k -> p c k", c=EC), rec[:]).then_inc(recs_stored, 16)
            sp.wait_ge(recs_stored, 96)

        def nth(r, i, k):
            return r * NG + UNROLL * i + k + 1

        kinds = {n: sems(n, UNROLL) for n in ("gathered", "scattered", "stored")}
        kinds.update({n: sems(n, CELL_UNROLL) for n in ("loaded", "extra", "written")})
        gathered, scattered, stored, loaded, extra, written = kinds.values()
        uses = [("e0", NG, dict(loaded=2, gathered=SLOTS, scattered=SLOTS)), ("n0", NCH, dict(loaded=2, stored=1))]
        for r in range(2):
            uses += [(f"e1{r}", NG, dict(loaded=1, gathered=2 * SLOTS, stored=1, extra=1)),
                     (f"e2{r}", NG, dict(loaded=3 + H1, scattered=SLOTS)),
                     (f"n{1 + r}", NCH, dict(loaded=2 + r, stored=1))]
        uses += [("e3", NG, dict(loaded=4, gathered=SLOTS, scattered=SLOTS)), ("n3", NCH, dict(loaded=2, stored=1))]
        for r in range(2):
            uses += [(f"e4{r}", NG, dict(loaded=3, gathered=SLOTS, scattered=SLOTS)),
                     (f"c{r}", NCC, dict(loaded=2, written=1, extra=r), CELL_UNROLL)]
        base, total = {}, {(kind, k): 0 for kind in kinds for k in range(CELL_UNROLL)}
        for phase, items, counts, *unroll in uses:
            slots = unroll[0] if unroll else UNROLL
            for kind, n in counts.items():
                for k in range(slots):
                    mine = len(range(k, items, slots))
                    base[kind, phase, k] = (total[kind, k], n, mine)
                    total[kind, k] += n * mine

        def landed(kind, phase, i, k):
            before, n, _ = base[kind, phase, k]
            return 16 * (before + n * (i + 1))

        def wait_all(eng, kind, phase):
            for k in [k for k in range(CELL_UNROLL) if (kind, phase, k) in base]:
                eng.wait_ge(kinds[kind][k], landed(kind, phase, base[kind, phase, k][2] - 1, k))

        def record(k, m):
            return lambda j: meta[k][:, j, m:m + 1].bitcast(I32)

        def rows_of(k):
            return lambda j: idx[k][:, j:j + 1]

        def gather(pool, to, table, column, done):
            steady(pool)
            for j in range(SLOTS):
                nc.gpsimd.indirect_dma_start(
                    to[:, j, 0:D] if to.shape[2] != D else to[:, j, :], None, table,
                    bass.IndirectOffsetOnAxis(ap=column(j), axis=0)).then_inc(done, 16)

        def evac(out_, in_):
            return nc.scalar.copy(out_, in_)

        e0_turned, e0_copied, e0_qkv, e0_q, e0_qk, e0_al, e0_aw, e0_msg, e0_eq, e0_cnt, e0_shift, e0_idx, e0_sum, \
            e0_out, e0_row = (sem(f"e0_{n}") for n in ("turned", "copied", "qkv", "q", "qk", "al", "aw", "msg", "eq", "cnt",
                                               "shift", "idx", "sum", "out", "row"))
        qkv_ps = [ps[:, 2 + 2 * k:4 + 2 * k, :].rearrange("p b n -> p (b n)").rearrange("p (j c) -> p j c", j=SLOTS)
                  for k in range(2)]

        def e0_sync(sp):
            def load(i, k):
                wait(sp, gathered[k], landed("gathered", "e0", i - 1, k))
                steady(sp)
                wait(sp, e0_row, nth(0, i - 1, k))
                steady(sp)
                sp.dma_start(meta[k][:], group_rec(i, k)).then_inc(loaded[k], 16)
                sp.dma_start(rowb[k][:], spread(group_of(srcf_d, i, k), P)).then_inc(loaded[k], 16)
            pipeline(sp, NG, load)

        def group_rec(i, k):
            return meta_d[bass.ds((UNROLL * i + k) * GROUP, GROUP), :].rearrange("(p j) m -> p j m", j=SLOTS)

        def e0_gpsimd(pool):
            pool.wait_ge(agg0_zero, 16 * (NP * D // (P * ZCOLS) + 1))

            def take(i, k):
                pool.wait_ge(loaded[k], landed("loaded", "e0", i, k))
                wait(pool, e0_turned, nth(0, i - 1, k))
                gather(pool, rows[k], x[:, :], record(k, M_DST), gathered[k])

            def give(i, k):
                pool.wait_ge(e0_out, nth(0, i, k))
                pool.wait_ge(e0_idx, nth(0, i, k))
                wait(pool, scattered[(k - 1) % UNROLL], landed("scattered", "e0", i if k else i - 1, (k - 1) % UNROLL))
                steady(pool)
                for j in range(SLOTS):
                    nc.gpsimd.indirect_dma_start(
                        agg0[:, :], bass.IndirectOffsetOnAxis(ap=idx[k][:, j:j + 1], axis=0),
                        outd[k][:, j, :], None, compute_op=ALU.add).then_inc(scattered[k], 16)
            pipeline(pool, NG, take, (4, give))
            wait_all(pool, "scattered", "e0")

        def e0_tensor(pe):
            t = nc.tensor

            def front(i, k):
                pe.wait_ge(gathered[k], landed("gathered", "e0", i, k))
                wait(pe, e0_copied, nth(0, i, k) - 2)
                steady(pe)
                for j in range(SLOTS):
                    mm = t.transpose(ps[0:D, k % 2, j * P:(j + 1) * P], rows[k][:, j, 0:D], ident[:])
                mm.then_inc(e0_turned, 1)

            def middle(i, k):
                pe.wait_ge(e0_copied, nth(0, i, k))
                wait(pe, e0_msg, nth(0, i, k) - 2)
                wait(pe, e0_q, nth(0, i, k) - 2)
                steady(pe)
                for j in range(SLOTS):
                    mm = t.matmul(qkv_ps[k % 2][:, j, 0:3 * D], turn[k][0:D, j * P:(j + 1) * P], qkv_w[:],
                                  start=True, stop=True)
                mm.then_inc(e0_qkv, 1)

            def back(i, k):
                pe.wait_ge(e0_msg, nth(0, i, k))
                pe.wait_ge(e0_eq, nth(0, i, k))
                wait(pe, e0_out, nth(0, i, k) - 2)
                steady(pe)
                for j in range(SLOTS):
                    for m in range(SLOTS):
                        mm = t.matmul(ps[:, 6 + k % 2, j * D:(j + 1) * D], slot_of(eq[k][:, m, :], j),
                                      msg_t[k][:, m, :], start=(m == 0), stop=(m == SLOTS - 1))
                mm.then_inc(e0_sum, 1)
            pipeline(pe, NG, front, middle, back)

        def e0_scalar(act):
            def front(i, k):
                act.wait_ge(e0_turned, nth(0, i, k))
                wait(act, e0_qkv, nth(0, i - 1, k))
                evac(turn[k][0:D, :], ps[0:D, k % 2, :]).then_inc(e0_copied, 1)

            def middle(i, k):
                act.wait_ge(e0_qkv, nth(0, i, k))
                wait(act, e0_qk, nth(0, i - 1, k))
                evac(q_t[k][:], qkv_ps[k % 2][:, :, 0:D]).then_inc(e0_q, 1)

            def back(i, k):
                act.wait_ge(e0_sum, nth(0, i, k))
                wait(act, scattered[k], landed("scattered", "e0", i - 1, k))
                evac(outd[k][:], ps[:, 6 + k % 2, 0:SLOTS * D].rearrange("p (j d) -> p j d", j=SLOTS)) \
                    .then_inc(e0_out, 1)
            pipeline(act, NG, front, middle, back, (0, lambda i, k: clear_piece(act, agg, i, k)))

        def e0_vector(dve):
            v = nc.vector

            def match(i, k):
                dve.wait_ge(loaded[k], landed("loaded", "e0", i, k))
                wait(dve, e0_sum, nth(0, i - 1, k))
                for j in range(SLOTS):
                    op = v.tensor_scalar(eq[k][:, j, :], rowb[k][:], meta[k][:, j, M_SRCF:M_SRCF + 1], None,
                                         ALU.is_equal)
                op.then_inc(e0_eq, 1)

            def count(i, k):
                dve.wait_ge(e0_eq, nth(0, i, k))
                for j in range(SLOTS):
                    v.tensor_tensor_reduce(junk[:, j, :], eq[k][:, j, :], later[:, j, :], 1.0, 0.0, ALU.mult, ALU.add,
                                           cnt[k][:, j:j + 1])
                v.tensor_copy(weight[k][:], meta[k][:, :, M_W])
                v.tensor_tensor(gap[k][:], trash[:], meta[k][:, :, M_SRCF], ALU.subtract).then_inc(e0_cnt, 1)

            def divert(i, k):
                dve.wait_ge(e0_cnt, nth(0, i, k))
                v.scalar_tensor_tensor(shift[k][:], cnt[k][:], 0.0, gap[k][:], ALU.is_gt, ALU.mult) \
                 .then_inc(e0_shift, 1)

            def row(i, k):
                dve.wait_ge(e0_shift, nth(0, i, k))
                v.tensor_tensor(sum_row[k][:], shift[k][:], meta[k][:, :, M_SRCF], ALU.add).then_inc(e0_row, 1)

            def index(i, k):
                dve.wait_ge(e0_row, nth(0, i, k))
                wait(dve, scattered[k], landed("scattered", "e0", i - 1, k))
                v.tensor_copy(idx[k][:], sum_row[k][:]).then_inc(e0_idx, 1)

            def products(i, k):
                dve.wait_ge(e0_q, nth(0, i, k))
                v.tensor_tensor(qk_t[k][:], q_t[k][:], qkv_ps[k % 2][:, :, D:2 * D], ALU.mult).then_inc(e0_qk, 1)

            def logits(i, k):
                dve.wait_ge(e0_qk, nth(0, i, k))
                v.tensor_reduce(al_t[k][:], qk_t[k][:].rearrange("p j (h f) -> p j h f", f=FH), AX, ALU.add) \
                 .then_inc(e0_al, 1)

            def weights(i, k):
                dve.wait_ge(e0_al, nth(0, i, k))
                v.scalar_tensor_tensor(aw_t[k][:], al_t[k][:], float(FH) ** -0.5,
                                       weight[k][:].unsqueeze(2).broadcast_to([P, SLOTS, H0]),
                                       ALU.mult, ALU.mult).then_inc(e0_aw, 1)

            def message(i, k):
                dve.wait_ge(e0_aw, nth(0, i, k))
                wait(dve, e0_sum, nth(0, i - 1, k))
                v.tensor_tensor(msg_t[k][:].rearrange("p j (h f) -> p j h f", f=FH),
                                qkv_ps[k % 2][:, :, 2 * D:3 * D].rearrange("p j (h f) -> p j h f", f=FH),
                                aw_t[k][:].unsqueeze(3).broadcast_to([P, SLOTS, H0, FH]), ALU.mult) \
                 .then_inc(e0_msg, 1)
            pipeline(dve, NG, (1, products), (0, match), (1, logits), (0, count), (1, weights), (0, divert),
                     (1, message), (0, row), (2, index))

        e1_turned, e1_copied, e1_qk, e1_k, e1_prod, e1_sum, e1_logit = (
            sem(f"e1_{n}") for n in ("turned", "copied", "qk", "k", "prod", "sum", "logit"))

        def e1_sync(sp, r):
            def load(i, k):
                wait(sp, gathered[k], landed("gathered", f"e1{r}", i - 1, k))
                steady(sp)
                sp.dma_start(meta[k][:], group_rec(i, k)).then_inc(loaded[k], 16)
            pipeline(sp, NG, load)

        def e1_gpsimd(pool, r, table):
            def take(i, k):
                pool.wait_ge(loaded[k], landed("loaded", f"e1{r}", i, k))
                wait(pool, e1_turned, nth(r, i - 1, k))
                for at, m in ((0, M_SRC), (D, M_DST)):
                    gather(pool, rows[k][:, :, at:at + D], table, record(k, m), gathered[k])
            pipeline(pool, NG, take)

        def e1_tensor(pe, r):
            t = nc.tensor

            def front(i, k):
                pe.wait_ge(gathered[k], landed("gathered", f"e1{r}", i, k))
                wait(pe, e1_copied, nth(r, i, k) - 2)
                steady(pe)
                for j in range(SLOTS):
                    mm = t.transpose(ps[:, k % 2, j * P:(j + 1) * P], rows[k][:, j, :], ident[:])
                mm.then_inc(e1_turned, 1)

            def middle(i, k):
                pe.wait_ge(e1_copied, nth(r, i, k))
                wait(pe, e1_prod, nth(r, i, k) - 2)
                t.matmul(ps[:, 2 + k % 2, :], wk_t[r][:], turn[k][:], start=True, stop=True)
                t.matmul(ps[:, 4 + k % 2, :], wq_t[r][:], turn[k][:], start=True, stop=True).then_inc(e1_qk, 1)

            def back(i, k):
                pe.wait_ge(e1_prod, nth(r, i, k))
                wait(pe, e1_logit, nth(r, i, k) - 2)
                t.matmul(ps[0:H1, 6 + k % 2, :], head_sum[:], prod[k][:], start=True, stop=True).then_inc(e1_sum, 1)
            pipeline(pe, NG, front, middle, back)

        def e1_scalar(act, r):
            def front(i, k):
                act.wait_ge(e1_turned, nth(r, i, k))
                wait(act, e1_qk, nth(r, i - 1, k))
                wait(act, stored[k], landed("stored", f"e1{r}", i - 1, k))
                evac(in_order(turn[k][:]), to_row(ps[:, k % 2, :])).then_inc(e1_copied, 1)
                act.wait_ge(e1_copied, nth(r, i, k))
                steady(act)
                act.dma_start(xst_d[bass.ds(UNROLL * i + k, 1), :, :].rearrange("o d c -> (o d) c"), turn[k][0:D, :]) \
                   .then_inc(stored[k], 16)

            def middle(i, k):
                act.wait_ge(e1_qk, nth(r, i, k))
                wait(act, e1_prod, nth(r, i, k) - 2)
                nc.scalar.activation(fmaj[k % 2][:], ps[:, 2 + k % 2, :], ACT.Identity, bias=bias_t[:, r, 0:1]) \
                  .then_inc(e1_k, 1)

            def back(i, k):
                act.wait_ge(e1_sum, nth(r, i, k))
                wait(act, extra[k], landed("extra", f"e1{r}", i - 1, k))
                evac(logit[k][:], ps[0:H1, 6 + k % 2, :]).then_inc(e1_logit, 1)
                act.wait_ge(e1_logit, nth(r, i, k))
                steady(act)
                act.dma_start(logit_d[:, bass.ds((UNROLL * i + k) * GROUP, GROUP)], logit[k][:]).then_inc(extra[k], 16)
            pipeline(act, NG, front, middle, (3, back),
                     *([(0, lambda i, k: clear_piece(act, aggw, i, k))] if r == 0 else []))
            wait_all(act, "stored", f"e1{r}")
            wait_all(act, "extra", f"e1{r}")

        def e1_vector(dve, r):
            def times(i, k):
                dve.wait_ge(e1_k, nth(r, i, k))
                wait(dve, e1_sum, nth(r, i - 1, k))
                nc.vector.scalar_tensor_tensor(prod[k][:], ps[:, 4 + k % 2, :], bias_t[:, r, 1:2], fmaj[k % 2][:],
                                               ALU.add, ALU.mult).then_inc(e1_prod, 1)
            pipeline(dve, NG, times)

        sm_loaded, sm_exp, sm_stored = sem("sm_loaded"), sem("sm_exp"), sem("sm_stored")
        by_head = lambda t: t.rearrange("h (p c) -> p h c", c=EC)

        def softmax_sync(sp, r):
            sp.dma_start(sc_a[:], by_head(logit_d)).then_inc(sm_loaded, 16)
            sp.wait_ge(dve_step, said["coef", r])
            steady(sp)
            sp.dma_start(by_head(coef_d), sc_c[:]).then_inc(sm_stored, 16)
            sp.wait_ge(sm_stored, 16 * (r + 1))

        def softmax_scalar(act, r):
            act.wait_ge(dve_step, said["shifted", r])
            nc.scalar.activation(sc_c[:], sc_a[:], ACT.Exp).then_inc(sm_exp, 1)

        def softmax_tensor(pe, r):
            for n, forward in enumerate((True, False, True, False)):
                seg_scan_tensor(pe, 1 + 4 * r + n, forward)

        def softmax_vector(dve, st, r):
            v = nc.vector
            n = 1 + 4 * r
            dve.wait_ge(sm_loaded, 16 * (r + 1))
            seg_scan(dve, n, sc_b, pneg, sc_a, ALU.add, ALU.max, -BIG, PNEG, True)
            seg_scan(dve, n + 1, sc_c, nneg, sc_b, ALU.add, ALU.max, -BIG, NNEG, False)
            st(v.tensor_tensor(sc_a[:], sc_a[:], sc_c[:], ALU.subtract))
            said["shifted", r] = st.n
            dve.wait_ge(sm_exp, r + 1)
            seg_scan(dve, n + 2, sc_b, psame, sc_c, ALU.mult, ALU.add, 0.0, PSAME, True)
            for h in range(H1):
                st(v.tensor_scalar(sc_a[:, h, :], nsame[:], -1.0, 1.0, ALU.mult, ALU.add))
            st(v.tensor_tensor(sc_b[:], sc_b[:], sc_a[:], ALU.mult))
            seg_scan(dve, n + 3, sc_a, nsame, sc_b, ALU.mult, ALU.add, 0.0, NSAME, False)
            st(v.tensor_scalar(sc_a[:], sc_a[:], 1e-16, None, ALU.add))
            st(v.reciprocal(sc_b[:], sc_a[:]))
            st(v.tensor_tensor(sc_c[:], sc_c[:], sc_b[:], ALU.mult))
            said["coef", r] = st.n

        e2_v, e2_prod, e2_scan, e2_sum, e2_out, e2_idx = (
            sem(f"e2_{n}") for n in ("v", "prod", "scan", "sum", "out", "idx"))

        def give_rows(pool, table, of, column, done):
            steady(pool)
            for j in range(SLOTS):
                nc.gpsimd.indirect_dma_start(
                    table, bass.IndirectOffsetOnAxis(ap=column(j), axis=0), of[:, j, :], None,
                    bounds_check=N - 1, oob_is_err=False).then_inc(done, 16)

        def e2_sync(sp, r):
            def load(i, k):
                wait(sp, e2_idx, nth(r, i - 1, k))
                steady(sp)
                wait(sp, e2_scan, nth(r, i - 1, k))
                steady(sp)
                sp.dma_start(turn[k][0:D, :], xst_d[bass.ds(UNROLL * i + k, 1), :, :].rearrange("o d c -> (o d) c")) \
                  .then_inc(loaded[k], 16)
                for h in range(H1):
                    sp.dma_start(rowb[k][h * D:(h + 1) * D, :], spread(group_of(coef_d[h], i, k), D)) \
                      .then_inc(loaded[k], 16)
                sp.dma_start(sameb[k][:], spread(group_of(same_d, i, k), P)).then_inc(loaded[k], 16)
                sp.dma_start(meta[k][:], group_rec(i, k)).then_inc(loaded[k], 16)
            pipeline(sp, NG, load)

        def e2_tensor(pe, r):
            t = nc.tensor

            def front(i, k):
                pe.wait_ge(loaded[k], landed("loaded", f"e2{r}", i, k))
                wait(pe, e2_prod, nth(r, i, k) - 2)
                t.matmul(ps[:, k % 2, :], wv_t[r][:], turn[k][0:D, :], start=True, stop=True).then_inc(e2_v, 1)

            def back(i, k):
                pe.wait_ge(e2_scan, nth(r, i, k))
                wait(pe, e2_out, nth(r, i, k) - 2)
                steady(pe)
                for j in range(SLOTS):
                    mm = t.matmul(ps[:, 2 + k % 2, j * D:(j + 1) * D], slot_of(scan[k][:], j), head_mean[:],
                                  start=True, stop=True)
                mm.then_inc(e2_sum, 1)
            pipeline(pe, NG, front, back)

        def run_scan(dve, i, k, rows_, of, done, r):
            dve.wait_ge(done, nth(r, i, k) - 1) if not (isinstance(i, int) and nth(r, i, k) == 1) else None
            nc.vector.tensor_tensor_scan(scan[k][0:rows_, :], sameb[k][0:rows_, :], of,
                                         scan[k - 1][0:rows_, GROUP - 1:GROUP], ALU.mult, ALU.add) \
              .then_inc(done, 1)

        def e2_vector(dve, r):
            def weigh(i, k):
                dve.wait_ge(e2_v, nth(r, i, k))
                nc.vector.scalar_tensor_tensor(prod[k][:], ps[:, k % 2, :], bias_t[:, r, 2:3], rowb[k][:],
                                               ALU.add, ALU.mult).then_inc(e2_prod, 1)
                dve.wait_ge(e2_prod, nth(r, i, k))
                wait(dve, e2_sum, nth(r, i - 1, k))
                run_scan(dve, i, k, P, prod[k][:], e2_scan, r)
                wait(dve, scattered[k], landed("scattered", f"e2{r}", i - 1, k))
                nc.vector.tensor_copy(idx[k][:], meta[k][:, :, M_LAST].bitcast(I32)).then_inc(e2_idx, 1)
            pipeline(dve, NG, weigh)

        def e2_scalar(act, r):
            def back(i, k):
                act.wait_ge(e2_sum, nth(r, i, k))
                wait(act, scattered[k], landed("scattered", f"e2{r}", i - 1, k))
                evac(outd[k][:], ps[:, 2 + k % 2, 0:SLOTS * D].rearrange("p (j d) -> p j d", j=SLOTS)) \
                    .then_inc(e2_out, 1)
            pipeline(act, NG, back)

        def e2_gpsimd(pool, r):
            def give(i, k):
                pool.wait_ge(e2_out, nth(r, i, k))
                pool.wait_ge(e2_idx, nth(r, i, k))
                give_rows(pool, agg[:, :], outd[k], rows_of(k), scattered[k])
            pipeline(pool, NG, give)
            wait_all(pool, "scattered", f"e2{r}")

        masked = [t[:] for t in prod] + [t[:, 2, :] for t in eq]
        assert len(masked) == NPROD
        e3_twice, e3_turned, e3_copied, e3_masked, e3_used, e3_msg, e3_scan, e3_sum, e3_out, e3_idx, e3_deg = (
            sem(f"e3_{n}") for n in ("twice", "turned", "copied", "masked", "used", "msg", "scan", "sum", "out", "idx",
                                    "deg"))

        def e3_sync(sp):
            def load(i, k):
                wait(sp, gathered[k], landed("gathered", "e3", i - 1, k))
                steady(sp)
                wait(sp, e3_scan, nth(0, i - 1, k))
                steady(sp)
                wait(sp, e3_idx, nth(0, i - 1, k))
                steady(sp)
                sp.dma_start(meta[k][:], group_rec(i, k)).then_inc(loaded[k], 16)
                sp.dma_start(rowb[k][:], spread(group_of(low_d, i, k), P)).then_inc(loaded[k], 16)
                sp.dma_start(eq[k][:, 0, :], spread(group_of(high_d, i, k), P)).then_inc(loaded[k], 16)
                sp.dma_start(sameb[k][:], spread(group_of(same_d, i, k), P)).then_inc(loaded[k], 16)
            pipeline(sp, NG, load)

        def e3_gpsimd(pool):
            def take(i, k):
                pool.wait_ge(loaded[k], landed("loaded", "e3", i, k))
                wait(pool, e3_turned, nth(0, i - 1, k))
                gather(pool, rows[k], x2[:, :], record(k, M_SRC), gathered[k])

            def give(i, k):
                pool.wait_ge(e3_out, nth(0, i, k))
                pool.wait_ge(e3_idx, nth(0, i, k))
                give_rows(pool, agg[:, :], outd[k], rows_of(k), scattered[k])
            pipeline(pool, NG, take, (4, give))
            wait_all(pool, "scattered", "e3")

        def e3_tensor(pe):
            t = nc.tensor

            def front(i, k):
                pe.wait_ge(e3_twice, nth(0, i, k))
                wait(pe, e3_copied, nth(0, i, k) - 2)
                steady(pe)
                for j in range(SLOTS):
                    mm = t.transpose(ps[:, k % 2, j * P:(j + 1) * P], rows[k][:, j, :], ident[:])
                mm.then_inc(e3_turned, 1)

            def middle(i, k):
                wait(pe, e3_msg, nth(0, i, k) - 2)
                for m in range(NPROD):
                    pe.wait_ge(e3_masked, (nth(0, i, k) - 1) * NPROD + m + 1)
                    mm = t.matmul(ps[:, 2 + k % 2, :], rel_w[:, m, :], masked[m],
                                  start=(m == 0), stop=(m == NPROD - 1))
                    mm.then_inc(e3_used, 1)

            def back(i, k):
                pe.wait_ge(e3_scan, nth(0, i, k))
                wait(pe, e3_out, nth(0, i, k) - 2)
                steady(pe)
                for j in range(SLOTS):
                    mm = t.matmul(ps[:, 4 + k % 2, j * D:(j + 1) * D], slot_of(scan[k][:], j), half_sum[:],
                                  start=True, stop=True)
                mm.then_inc(e3_sum, 1)
            pipeline(pe, NG, (0, front), (1, middle), (2, back))

        def e3_scalar(act):
            def front(i, k):
                act.wait_ge(gathered[k], landed("gathered", "e3", i, k))
                evac(rows[k][:, :, D:P], rows[k][:, :, 0:D]).then_inc(e3_twice, 1)
                act.wait_ge(e3_turned, nth(0, i, k))
                wait(act, e3_used, NPROD * nth(0, i - 1, k))
                evac(in_order(turn[k][:]), to_row(ps[:, k % 2, :])).then_inc(e3_copied, 1)

            def back(i, k):
                act.wait_ge(e3_sum, nth(0, i, k))
                act.wait_ge(e3_deg, nth(0, i, k))
                wait(act, scattered[k], landed("scattered", "e3", i - 1, k))
                for j in range(SLOTS):
                    ins = nc.scalar.activation(outd[k][:, j, :], ps[:, 4 + k % 2, j * D:(j + 1) * D], ACT.Copy,
                                               scale=gap[k][:, j:j + 1])
                ins.then_inc(e3_out, 1)
            pipeline(act, NG, front, (3, back))

        def e3_vector(dve):
            v = nc.vector

            def mask(i, k):
                dve.wait_ge(e3_copied, nth(0, i, k))
                dve.wait_ge(loaded[k], landed("loaded", "e3", i, k))
                for m in range(NPROD):
                    wait(dve, e3_used, (nth(0, i, k) - 2) * NPROD + m + 1)
                    v.scalar_tensor_tensor(masked[m], rowb[k][:], rel_id[:, m:m + 1], turn[k][:],
                                           ALU.is_equal, ALU.mult).then_inc(e3_masked, 1)

            def add(i, k):
                dve.wait_ge(e3_used, NPROD * nth(0, i, k))
                v.scalar_tensor_tensor(eq[k][:, 1, :], eq[k][:, 0, :], upper[:, 0:1], ps[:, 2 + k % 2, :],
                                       ALU.is_equal, ALU.mult).then_inc(e3_msg, 1)
                wait(dve, e3_out, nth(0, i - 1, k))
                v.tensor_copy(gap[k][:], meta[k][:, :, M_RDEG]).then_inc(e3_deg, 1)
                wait(dve, scattered[k], landed("scattered", "e3", i - 1, k))
                v.tensor_copy(idx[k][:], meta[k][:, :, M_LAST].bitcast(I32)).then_inc(e3_idx, 1)
                dve.wait_ge(e3_msg, nth(0, i, k))
                wait(dve, e3_sum, nth(0, i - 1, k))
                run_scan(dve, i, k, P, eq[k][:, 1, :], e3_scan, 0)

            pipeline(dve, NG, (1, mask), (2, add))

        e4_turned, e4_copied, e4_scan, e4_sum, e4_out, e4_idx = (
            sem(f"e4_{n}") for n in ("turned", "copied", "scan", "sum", "out", "idx"))

        def e4_sync(sp, r):
            def load(i, k):
                wait(sp, e4_turned, nth(r, i - 1, k))
                steady(sp)
                wait(sp, e4_idx, nth(r, i - 1, k))
                steady(sp)
                wait(sp, gathered[k], landed("gathered", f"e4{r}", i - 1, k))
                steady(sp)
                wait(sp, e4_scan, nth(r, i - 1, k))
                steady(sp)
                sp.dma_start(meta[k][:], group_rec(i, k)).then_inc(loaded[k], 16)
                sp.dma_start(roww[k][:, :, D:D + NA], attr_d[bass.ds((UNROLL * i + k) * GROUP, GROUP), :]
                             .rearrange("(p j) a -> p j a", j=SLOTS)).then_inc(loaded[k], 16)
                sp.dma_start(sameb[k][0:AW, :], spread(group_of(same_d, i, k), AW)).then_inc(loaded[k], 16)
            pipeline(sp, NG, load)

        def e4_gpsimd(pool, r, table):
            def take(i, k):
                pool.wait_ge(loaded[k], landed("loaded", f"e4{r}", i, k))
                wait(pool, e4_turned, nth(r, i - 1, k))
                gather(pool, roww[k], table, record(k, M_SRC), gathered[k])

            def give(i, k):
                pool.wait_ge(e4_out, nth(r, i, k))
                pool.wait_ge(e4_idx, nth(r, i, k))
                give_rows(pool, aggw[:, :], outr[k], rows_of(k), scattered[k])
            pipeline(pool, NG, take, (2, give))
            wait_all(pool, "scattered", f"e4{r}")

        def e4_tensor(pe, r):
            t = nc.tensor

            def front(i, k):
                pe.wait_ge(gathered[k], landed("gathered", f"e4{r}", i, k))
                wait(pe, e4_copied, nth(r, i, k) - 2)
                steady(pe)
                for j in range(SLOTS):
                    mm = t.transpose(ps[0:AW, k % 2, j * P:(j + 1) * P], roww[k][:, j, :], ident[:])
                mm.then_inc(e4_turned, 1)

            def back(i, k):
                pe.wait_ge(e4_scan, nth(r, i, k))
                wait(pe, e4_out, nth(r, i, k) - 2)
                steady(pe)
                for j in range(SLOTS):
                    mm = t.transpose(ps[:, 2 + k % 2, j * AW:(j + 1) * AW], slot_of(scan[k][0:AW, :], j),
                                     ident[0:AW, 0:AW])
                mm.then_inc(e4_sum, 1)
            pipeline(pe, NG, front, back)

        def e4_scalar(act, r):
            def front(i, k):
                act.wait_ge(e4_turned, nth(r, i, k))
                wait(act, e4_scan, nth(r, i - 1, k))
                evac(in_order(turn[k][0:AW, :]), to_row(ps[0:AW, k % 2, :])).then_inc(e4_copied, 1)

            def back(i, k):
                act.wait_ge(e4_sum, nth(r, i, k))
                wait(act, scattered[k], landed("scattered", f"e4{r}", i - 1, k))
                evac(outr[k][:], ps[:, 2 + k % 2, 0:SLOTS * AW].rearrange("p (j d) -> p j d", j=SLOTS)) \
                    .then_inc(e4_out, 1)
            pipeline(act, NG, front, back)

        def e4_vector(dve, r):
            def add(i, k):
                dve.wait_ge(e4_copied, nth(r, i, k))
                dve.wait_ge(loaded[k], landed("loaded", f"e4{r}", i, k))
                wait(dve, e4_sum, nth(r, i - 1, k))
                run_scan(dve, i, k, AW, turn[k][0:AW, :], e4_scan, r)
                wait(dve, scattered[k], landed("scattered", f"e4{r}", i - 1, k))
                nc.vector.tensor_copy(idx[k][:], meta[k][:, :, M_LAST].bitcast(I32)).then_inc(e4_idx, 1)
            pipeline(dve, NG, add)

        HAS_LINEAR, HAS_NORM = (0, 1, 1, 1), (1, 0, 1, 1)
        nd_turned, nd_copied, nd_mm, nd_part, nd_y, nd_s, nd_c, nd_q, nd_v, nd_i, nd_o, nd_e, nd_j = (
            sem(f"nd_{n}") for n in ("turned", "copied", "mm", "part", "y", "s", "c", "q", "v", "i", "o", "e",
                                    "j"))

        nd_w = sem("nd_w")

        def nd(r, i, k):
            return r * NCH + UNROLL * i + k + 1

        def nd_lin(r, i, k):
            return sum(HAS_LINEAR[:r]) * NCH + UNROLL * i + k + 1

        def nd_nrm(r, i, k):
            return sum(HAS_NORM[:r]) * NCH + UNROLL * i + k + 1

        def chunk_of(table, i, k, parts=P):
            return table[bass.ds((UNROLL * i + k) * CHUNK, parts * ROWS), :].rearrange("(p c) d -> p c d", c=ROWS)

        def node_sync(sp, r, a, g, res):
            def load(i, k):
                wait(sp, nd_y, nd(r, i - 1, k))
                last = r == 0 and isinstance(i, int) and UNROLL * i + k == NCH - 1
                parts = LAST_PARTS if last else P
                for t, of in ((node_a[k], a), (node_g[k], g), (node_r[k], res)):
                    if of is not None:
                        n = parts if of is x else P
                        sp.dma_start(t[0:n], chunk_of(of, i, k, n)).then_inc(loaded[k], 16)
            pipeline(sp, NCH, load)

        def node_tensor(pe, r):
            t = nc.tensor
            w, b = lin_w[r - 1], lin_b[r - 1]

            def front(i, k):
                pe.wait_ge(loaded[k], landed("loaded", f"n{r}", i, k))
                wait(pe, nd_copied, nd_lin(r, i, k) - 2)
                for c in range(0, ROWS, 2):
                    mm = t.transpose(ps[:, k % 2, c * D:(c + 2) * D], node_a[k][:, c:c + 2, :].rearrange("p c d -> p (c d)"),
                                     ident[:])
                mm.then_inc(nd_turned, 1)

            def back(i, k):
                pe.wait_ge(nd_copied, nd_lin(r, i, k))
                wait(pe, nd_y, nd(r, i, k) - 2)
                t.matmul(ps[:, 2 + k % 2, :], ones_row[:], b[:], start=True, stop=False, skip_group_check=True)
                for c in range(0, ROWS, 2):
                    mm = t.matmul(ps[:, 2 + k % 2, c * D:(c + 2) * D], node_t[k][:, c:c + 2, :].rearrange("p c d -> p (c d)"),
                                  w[:], start=False, stop=True, skip_group_check=True)
                mm.then_inc(nd_mm, 1)
            pipeline(pe, NCH, front, back)

        def node_scalar(act, r, to):
            def front(i, k):
                act.wait_ge(nd_turned, nd_lin(r, i, k))
                wait(act, nd_mm, nd_lin(r, i - 1, k))
                evac(node_t[k][:].rearrange("p c d -> p (c d)"), ps[:, k % 2, :]).then_inc(nd_copied, 1)

            def square(i, k):
                act.wait_ge(nd_c, nd_nrm(r, i, k))
                wait(act, nd_v, nd_nrm(r, i - 1, k))
                nc.scalar.activation(node_q[k][:], node_c[k][:], ACT.Square).then_inc(nd_q, 1)

            def root(i, k):
                act.wait_ge(nd_v, nd_nrm(r, i, k))
                wait(act, nd_j, nd_nrm(r, i - 1, k))
                nc.scalar.activation(node_e[k][:], node_v[k][:], ACT.Sqrt, bias=eps_col[:, 0:1], scale=1.0 / D) \
                  .then_inc(nd_e, 1)

            def store(i, k):
                if HAS_NORM[r]:
                    act.wait_ge(nd_o, nd_nrm(r, i, k))
                else:
                    act.wait_ge(nd_y, nd(r, i, k))
                steady(act)
                act.dma_start(chunk_of(to, i, k), node_o[k][:]).then_inc(stored[k], 16)
            pipeline(act, NCH, *([(3, root)] if HAS_NORM[r] else []), *([(0, front)] if HAS_LINEAR[r] else []),
                     *([(2, square), (5, store)] if HAS_NORM[r] else [(2, store)]))
            wait_all(act, "stored", f"n{r}")

        def node_vector(dve, r):
            v = nc.vector

            def add(i, k):
                y = node_y[k] if HAS_NORM[r] else node_o[k]
                mm = ps[:, 2 + k % 2, :].rearrange("p (c d) -> p c d", d=D)
                dve.wait_ge(nd_mm, nd_lin(r, i, k))
                if r == 1:
                    dve.wait_ge(loaded[k], landed("loaded", "n1", i, k))
                    wait(dve, stored[k], landed("stored", "n1", i - 1, k))
                    v.tensor_tensor(y[:], mm, node_g[k][:], ALU.add).then_inc(nd_y, 1)
                else:
                    dve.wait_ge(nd_part, (r - 2) * NCH + UNROLL * i + k + 1)
                    v.tensor_tensor(y[:], mm, node_p[k][:], ALU.add).then_inc(nd_y, 1)

            def mean(i, k):
                row_sums(dve, k, node_y[k], nd_y, nd(r, i, k))

            def less_mean(i, k):
                center(dve, k, node_y[k], nd_nrm(r, i, k))

            def spread_of(i, k):
                variance(dve, k, ROWS, nd_nrm(r, i, k))

            def scale(i, k):
                wait(dve, stored[k], landed("stored", f"n{r}", i - 1, k))
                dve.wait_ge(nd_i, nd_nrm(r, i, k))
                norm(dve, k, node_o[k], 1.0)

            def invert(i, k):
                dve.wait_ge(nd_e, nd_nrm(r, i, k))
                wait(dve, nd_i, nd_nrm(r, i - 1, k))
                v.reciprocal(node_j[k][:], node_e[k][:]).then_inc(nd_j, 1)
            if HAS_NORM[r]:
                pipeline(dve, NCH, (3, invert), *([(1, add)] if HAS_LINEAR[r] else []), (4, scale), (1, mean),
                         (2, spread_of), (1, less_mean))
            else:
                pipeline(dve, NCH, (1, add))

        def row_sums(dve, k, y, y_ready, ready, at=0):
            dve.wait_ge(y_ready, ready)
            nc.vector.tensor_reduce(node_s[k][:, at:at + y.shape[1]], y[:], AX, ALU.add).then_inc(nd_s, 1)

        def center(dve, k, y, n, at=0):
            to = slice(at, at + y.shape[1])
            dve.wait_ge(nd_s, n)
            nc.vector.scalar_tensor_tensor(
                node_c[k][:, to, :], node_s[k][:, to].unsqueeze(2).broadcast_to([P, y.shape[1], D]),
                -1.0 / D, y[:], ALU.mult, ALU.add).then_inc(nd_c, 1)

        def variance(dve, k, rows_, n, at=0):
            dve.wait_ge(nd_q, n)
            nc.vector.tensor_reduce(node_v[k][:, at:at + rows_], node_q[k][:, at:at + rows_, :], AX, ALU.add).then_inc(nd_v, 1)

        def pool_steps(pool, before):
            done = [before]

            def step(ins):
                done[0] = done[0] + 1
                ins.then_inc(nd_w, 1)
                pool.wait_ge(nd_w, done[0])
                steady(pool)
            return step

        def newton(step, to, root_, work, var):
            g = nc.gpsimd
            step(g.tensor_tensor(work, root_, root_, ALU.mult))
            step(g.tensor_tensor(work, work, var, ALU.mult))
            step(g.tensor_scalar(work, work, -0.5, 1.5, ALU.mult, ALU.add))
            step(g.tensor_tensor(to, root_, work, ALU.mult))

        def refine_root(pool, k, n):
            step = pool_steps(pool, (n - 1) * REFINE_STEPS)
            pool.wait_ge(nd_v, n)
            steady(pool)
            step(nc.gpsimd.tensor_scalar(node_z[k][:], node_v[k][:], 1.0 / D, EPS, ALU.mult, ALU.add))
            pool.wait_ge(nd_j, n)
            steady(pool)
            newton(step, node_i[k][:], node_j[k][:], node_w[k][:], node_z[k][:])
            nc.gpsimd.engine_nop().then_inc(nd_i, 1)

        def inverse_root(pool, q, p, n):
            g = nc.gpsimd
            var, root_, work = (t[q][:] for t in (node_z, node_i, node_w))
            step = pool_steps(pool, sum(HAS_NORM) * NCH * REFINE_STEPS + p * ROOT_STEPS)
            pool.wait_ge(nd_v, n)
            steady(pool)
            step(g.tensor_scalar(var, node_v[q][:], D * EPS, None, ALU.add))
            step(g.tensor_scalar(root_.bitcast(I32), var.bitcast(I32), -0.5, float(0x5f3759df), ALU.mult, ALU.add))
            for _ in range(NEWTON):
                newton(step, root_, root_, work, var)
            g.engine_nop().then_inc(gc_root, 1)

        def norm(dve, k, to, factor, at=0):
            of = slice(at, at + to.shape[1])
            nc.vector.scalar_tensor_tensor(to[:], node_c[k][:, of, :], factor,
                                           node_i[k][:, of].unsqueeze(2).broadcast_to([P, to.shape[1], D]),
                                           ALU.mult, ALU.mult).then_inc(nd_o, 1)

        def node_gpsimd(pool, r, rest):
            def partial(i, k):
                pool.wait_ge(loaded[k], landed("loaded", f"n{r}", i, k))
                if r == 0:
                    wait(pool, nd_c, nd_nrm(r, i - 1, k))
                else:
                    wait(pool, nd_y, nd(r, i - 1, k))
                steady(pool)
                nc.gpsimd.tensor_tensor((node_y if r == 0 else node_p)[k][:], rest[k][:], node_g[k][:], ALU.add) \
                  .then_inc(nd_y if r == 0 else nd_part, 1)

            def refine(i, k):
                wait(pool, nd_o, nd_nrm(r, i - 1, k))
                refine_root(pool, k, nd_nrm(r, i, k))
            if HAS_NORM[r]:
                pipeline(pool, NCH, partial, (3, refine))

        gc_dh, gc_turned, gc_copied, gc_mm, gc_rz, gc_rn, gc_pre, gc_n, gc_d, gc_zd, gc_h, gc_y = (
            sem(f"gc_{n}") for n in ("dh", "turned", "copied", "mm", "rz", "rn", "pre", "n", "d", "zd", "h", "y"))
        gc_blank, gc_root = sem("gc_blank"), sem("gc_root")
        PAIRS = CELL_UNROLL // 2

        def half(u):
            return u % 2 * CROWS
        cell_n, cell_p, cell_d, cell_z = (pair(n, [P, CROWS, D]) for n in ("cell_n", "cell_p", "cell_d", "cell_z"))
        cell_q, cell_h, cell_y = (pair(n, [P, CROWS, D]) for n in ("cell_q", "cell_h", "cell_y"))
        cell_o = pair("cell_o", [P, CROWS, D], n=CELL_UNROLL)
        cell_r = pair("cell_r", [P, CROWS, D], n=CELL_UNROLL)
        gate_ps = [ps[:, 4 + 2 * k:6 + 2 * k, :].rearrange("p b n -> p (b n)").rearrange("p (c n) -> p c n", c=CROWS)
                   for k in range(2)]

        def gc(r, i, u):
            return r * NCC + CELL_UNROLL * i + u + 1

        def cell_chunk(table, i, u, parts=P):
            return table[bass.ds((CELL_UNROLL * i + u) * CCHUNK, parts * CROWS), :].rearrange("(p c) d -> p c d", c=CROWS)

        def cell_blank(pool, r):
            n = 2 * CELL_UNROLL * r
            for t in cell_in:
                for at, to, value in ((DEG_AT + 1, DEG_AT + 3, 1.0), (DEG_AT + 3, H_AT, 0.0)):
                    n += 1
                    nc.gpsimd.memset(t[:, :, at:to], value).then_inc(gc_blank, 1)
                    pool.wait_ge(gc_blank, n)

        def cell_sync(sp, r, h):
            sp.wait_ge(gc_blank, 2 * CELL_UNROLL * (r + 1))

            def load(i, u):
                wait(sp, gc_h, gc(r, i, u) - CELL_UNROLL)
                steady(sp)
                sp.dma_start(cell_in[u][:, :, H_AT:H_AT + D], cell_chunk(h, i, u)).then_inc(loaded[u], 16)
                sp.dma_start(cell_in[u][:, :, S_AT:S_AT + EW], aggw[bass.ds((CELL_UNROLL * i + u) * CCHUNK, CCHUNK), 0:EW]
                             .rearrange("(p c) d -> p c d", c=CROWS)).then_inc(loaded[u], 16)
                if r == 1:
                    wait(sp, gc_y, CELL_UNROLL * i + u + 1 - CELL_UNROLL)
                    steady(sp)
                    sp.dma_start(cell_r[u][:], cell_chunk(x3, i, u)).then_inc(extra[u], 16)
            pipeline(sp, NCC, load, unroll=CELL_UNROLL)

        def cell_tensor(pe, r):
            t = nc.tensor

            def turn_in(i, u):
                k = u % 2
                pe.wait_ge(gc_dh, gc(r, i, u))
                wait(pe, gc_copied, gc(r, i, u) - 2)
                for c in range(CROWS):
                    t.transpose(ps[:, k % 2, c * P:(c + 1) * P], cell_in[u][:, c, 0:P], ident[:])
                    mm = t.transpose(ps[0:96, 2 + k % 2, c * P:(c + 1) * P], cell_in[u][:, c, P:P + 96], ident[:])
                mm.then_inc(gc_turned, 1)

            def gates(i, u):
                k = u % 2
                pe.wait_ge(gc_copied, gc(r, i, u))
                wait(pe, gc_pre, gc(r, i, u) - 2)
                for c in range(CROWS):
                    t.matmul(gate_ps[k][:, c, :], cell_u[k][:, c * P:(c + 1) * P], gate_v[r][:],
                             start=True, stop=False, skip_group_check=True)
                    mm = t.matmul(gate_ps[k][:, c, 0:GI], cell_t[k][:, c * P:(c + 1) * P], gate_w[r][:],
                                  start=False, stop=True, skip_group_check=True)
                mm.then_inc(gc_mm, 1)
            pipeline(pe, NCC, turn_in, gates, unroll=CELL_UNROLL)

        def cell_scalar(act, r):
            a = nc.scalar

            def copy(i, u):
                k = u % 2
                act.wait_ge(gc_turned, gc(r, i, u))
                wait(act, gc_mm, gc(r, i, u) - 2)
                evac(cell_t[k][:], ps[:, k % 2, :])
                evac(cell_u[k][:], ps[0:96, 2 + k % 2, :]).then_inc(gc_copied, 1)

            def gates(i, u):
                k = u % 2
                act.wait_ge(gc_mm, gc(r, i, u))
                wait(act, gc_zd, gc(r, i, u) - 2)
                a.activation(cell_rz[k][:], gate_ps[k][:, :, 0:2 * D], ACT.Sigmoid).then_inc(gc_rz, 1)

            def new(i, u):
                k = u % 2
                act.wait_ge(gc_pre, gc(r, i, u))
                wait(act, gc_h, gc(r, i, u) - 2)
                a.activation(cell_n[k][:], cell_p[k][:], ACT.Tanh).then_inc(gc_n, 1)

            def square(i, u):
                q, to = u // 2, slice(half(u), half(u) + CROWS)
                act.wait_ge(nd_c, sum(HAS_NORM) * NCH + CELL_UNROLL * i + u + 1)
                wait(act, nd_v, sum(HAS_NORM) * NCH + CELL_UNROLL * (i - 1) + u + 1)
                a.activation(node_q[q][:, to, :], node_c[q][:, to, :], ACT.Square).then_inc(nd_q, 1)
            pipeline(act, NCC, copy, gates, new, *([(5, square)] if r == 1 else []), unroll=CELL_UNROLL)

        def cell_vector(dve, r):
            v = nc.vector

            def scale_in(i, u):
                dve.wait_ge(loaded[u], landed("loaded", f"c{r}", i, u))
                v.tensor_tensor(cell_in[u][:, :, 0:D], cell_in[u][:, :, H_AT:H_AT + D],
                                cell_in[u][:, :, DEG_AT:DEG_AT + 1].broadcast_to([P, CROWS, D]), ALU.mult) \
                 .then_inc(gc_dh, 1)

            def reset(i, u):
                k = u % 2
                dve.wait_ge(gc_rz, gc(r, i, u))
                v.tensor_tensor(cell_q[k][:], cell_rz[k][:, :, 0:D], gate_ps[k][:, :, GI:GI + D], ALU.mult) \
                 .then_inc(gc_rn, 1)

            def new_in(i, u):
                k = u % 2
                dve.wait_ge(gc_rn, gc(r, i, u))
                wait(dve, gc_n, gc(r, i, u) - 2)
                v.tensor_tensor(cell_p[k][:], cell_q[k][:], gate_ps[k][:, :, 2 * D:GI], ALU.add).then_inc(gc_pre, 1)

            def difference(i, u):
                k = u % 2
                dve.wait_ge(gc_n, gc(r, i, u))
                v.tensor_tensor(cell_d[k][:], cell_in[u][:, :, H_AT:H_AT + D], cell_n[k][:], ALU.subtract) \
                 .then_inc(gc_d, 1)

            def update(i, u):
                k = u % 2
                dve.wait_ge(gc_d, gc(r, i, u))
                v.tensor_tensor(cell_z[k][:], cell_rz[k][:, :, D:2 * D], cell_d[k][:], ALU.mult).then_inc(gc_zd, 1)

            def state(i, u):
                k = u % 2
                to = cell_o[u] if r == 0 else cell_h[k]
                dve.wait_ge(gc_zd, gc(r, i, u))
                if r == 0:
                    wait(dve, written[u], landed("written", "c0", i - 1, u))
                v.tensor_tensor(to[:], cell_n[k][:], cell_z[k][:], ALU.add).then_inc(gc_h, 1)

            def residual(i, u):
                k = u % 2
                dve.wait_ge(gc_h, gc(r, i, u))
                dve.wait_ge(extra[u], landed("extra", "c1", i, u))
                v.tensor_tensor(cell_y[k][:], cell_h[k][:], cell_r[u][:], ALU.add).then_inc(gc_y, 1)

            def chunk(i, u):
                return sum(HAS_NORM) * NCH + CELL_UNROLL * i + u + 1

            def mean(i, u):
                row_sums(dve, u // 2, cell_y[u % 2], gc_y, CELL_UNROLL * i + u + 1, half(u))

            def less_mean(i, u):
                center(dve, u // 2, cell_y[u % 2], chunk(i, u), half(u))

            def scale(i, u):
                wait(dve, written[u], landed("written", "c1", i - 1, u))
                dve.wait_ge(gc_root, PAIRS * i + u // 2 + 1)
                norm(dve, u // 2, cell_o[u], float(D) ** 0.5, half(u))

            def spread_of(i, u):
                variance(dve, u // 2, CROWS, sum(HAS_NORM) * NCH + CELL_UNROLL * i + u + 1, half(u))
            if r == 0:
                pipeline(dve, NCC, (0, scale_in), (2, reset), (3, difference), (2, new_in), (3, update), (3, state),
                         unroll=CELL_UNROLL)
            else:
                pipeline(dve, NCC, (0, scale_in), (2, reset), (3, difference), (4, mean), (2, new_in), (3, update),
                         (4, less_mean), (3, state), (6, spread_of), (3, residual), (9, scale), unroll=CELL_UNROLL)

        def cell_gpsimd(pool, r, to):
            cell_blank(pool, r)

            def store(i, u):
                if r == 0:
                    pool.wait_ge(gc_h, gc(r, i, u))
                    steady(pool)
                    pool.dma_start(cell_chunk(to, i, u), cell_o[u][:]).then_inc(written[u], 16)
                    return
                pool.wait_ge(nd_o, sum(HAS_NORM) * NCH + CELL_UNROLL * i + u + 1)
                n = CELL_UNROLL * i + u if isinstance(i, int) else 0
                parts = P if n < C_FULL else C_PARTS if n == C_FULL else 0
                if parts:
                    pool.dma_start(cell_chunk(to, i, u, parts), cell_o[u][0:parts]).then_inc(written[u], 16)

            def root(i, u):
                if u % 2:
                    chunk = sum(HAS_NORM) * NCH + CELL_UNROLL * i + u + 1
                    wait(pool, nd_o, chunk - CELL_UNROLL)
                    inverse_root(pool, u // 2, PAIRS * i + u // 2, chunk)

            pipeline(pool, NCC, *([store] if r == 0 else [(0, root), (3, store)]), unroll=CELL_UNROLL)
            wait_all(pool, "written", f"c{r}")

        conv_in = (x1, h1)
        block = ctx.enter_context(nc.Block())

        @block.gpsimd
        def _(pool):
            consts(pool)
            sort_gpsimd(pool)
            phase_end(pool, "prepare")
            e0_gpsimd(pool)
            phase_end(pool, "edges 0")
            node_gpsimd(pool, 0, node_r)
            phase_end(pool, "nodes 0")
            for r in range(2):
                e1_gpsimd(pool, r, conv_in[r][:, :])
                phase_end(pool, f"logits {r}")
                phase_end(pool, f"softmax {r}")
                e2_gpsimd(pool, r)
                phase_end(pool, f"values {r}")
                node_gpsimd(pool, 1 + r, (None, node_r)[r])
                phase_end(pool, f"nodes {1 + r}")
            e3_gpsimd(pool)
            phase_end(pool, "relations")
            node_gpsimd(pool, 3, node_a)
            phase_end(pool, "nodes 3")
            for r in range(2):
                e4_gpsimd(pool, r, (x3, v1)[r][:, :])
                phase_end(pool, f"messages {r}")
                cell_gpsimd(pool, r, (v1, out)[r])
                phase_end(pool, f"cell {r}")

        @block.vector
        def _(dve):
            st = Steps(dve, dve_step)
            prep_vector(dve, st)
            sort_vector(dve)
            order_vector(dve, st)
            phase_end(dve, "prepare")
            e0_vector(dve)
            phase_end(dve, "edges 0")
            node_vector(dve, 0)
            phase_end(dve, "nodes 0")
            for r in range(2):
                e1_vector(dve, r)
                phase_end(dve, f"logits {r}")
                softmax_vector(dve, st, r)
                phase_end(dve, f"softmax {r}")
                e2_vector(dve, r)
                phase_end(dve, f"values {r}")
                node_vector(dve, 1 + r)
                phase_end(dve, f"nodes {1 + r}")
            e3_vector(dve)
            phase_end(dve, "relations")
            node_vector(dve, 3)
            phase_end(dve, "nodes 3")
            for r in range(2):
                e4_vector(dve, r)
                phase_end(dve, f"messages {r}")
                cell_vector(dve, r)
                phase_end(dve, f"cell {r}")

        @block.sync
        def _(sp):
            prep_sync(sp)
            sort_sync(sp)
            order_sync(sp)
            phase_end(sp, "prepare")
            e0_sync(sp)
            phase_end(sp, "edges 0")
            node_sync(sp, 0, None, agg0, x)
            phase_end(sp, "nodes 0")
            for r in range(2):
                e1_sync(sp, r)
                phase_end(sp, f"logits {r}")
                softmax_sync(sp, r)
                phase_end(sp, f"softmax {r}")
                e2_sync(sp, r)
                phase_end(sp, f"values {r}")
                node_sync(sp, 1 + r, conv_in[r], agg, (None, x1)[r])
                phase_end(sp, f"nodes {1 + r}")
            e3_sync(sp)
            phase_end(sp, "relations")
            node_sync(sp, 3, x2, agg, None)
            phase_end(sp, "nodes 3")
            for r in range(2):
                e4_sync(sp, r)
                phase_end(sp, f"messages {r}")
                cell_sync(sp, r, (x3, v1)[r])
                phase_end(sp, f"cell {r}")

        @block.tensor
        def _(pe):
            prep_tensor(pe)
            order_tensor(pe)
            phase_end(pe, "prepare")
            e0_tensor(pe)
            phase_end(pe, "edges 0")
            phase_end(pe, "nodes 0")
            for r in range(2):
                e1_tensor(pe, r)
                phase_end(pe, f"logits {r}")
                softmax_tensor(pe, r)
                phase_end(pe, f"softmax {r}")
                e2_tensor(pe, r)
                phase_end(pe, f"values {r}")
                node_tensor(pe, 1 + r)
                phase_end(pe, f"nodes {1 + r}")
            e3_tensor(pe)
            phase_end(pe, "relations")
            node_tensor(pe, 3)
            phase_end(pe, "nodes 3")
            for r in range(2):
                e4_tensor(pe, r)
                phase_end(pe, f"messages {r}")
                cell_tensor(pe, r)
                phase_end(pe, f"cell {r}")

        @block.scalar
        def _(act):
            prep_scalar(act)
            act.wait_ge(agg0_zero, 16 * (NP * D // (P * ZCOLS) + 1))
            phase_end(act, "prepare")
            e0_scalar(act)
            act.wait_ge(tables_zero, 16 * NG)
            phase_end(act, "edges 0")
            node_scalar(act, 0, x1)
            phase_end(act, "nodes 0")
            for r in range(2):
                e1_scalar(act, r)
                act.wait_ge(tables_zero, 16 * 2 * NG)
                phase_end(act, f"logits {r}")
                softmax_scalar(act, r)
                phase_end(act, f"softmax {r}")
                e2_scalar(act, r)
                phase_end(act, f"values {r}")
                node_scalar(act, 1 + r, (h1, x2)[r])
                phase_end(act, f"nodes {1 + r}")
            e3_scalar(act)
            phase_end(act, "relations")
            node_scalar(act, 3, x3)
            phase_end(act, "nodes 3")
            for r in range(2):
                e4_scalar(act, r)
                phase_end(act, f"messages {r}")
                cell_scalar(act, r)
                phase_end(act, f"cell {r}")


_INS = ["x", "src", "dst", "edge_attr_16", "edge_type_32", "edge_weight", "edge_weight_n2", "L0_gnn_Wq", "L0_gnn_Wk",
        "L0_gnn_Wv"]
_CONV = [f"L1_gnn_l{layer}_{kind}{name}" for layer in (1, 2) for name in "qkvs" for kind in "wb"]
_REST = ["L2_gnn_basis", "L2_gnn_coeff", "L2_gnn_self_weight", "L2_gnn_bias", "L3_gnn_W_msg", "L3_gnn_b_msg",
         "L3_gnn_W_ih", "L3_gnn_W_hh", "L3_gnn_b_ih", "L3_gnn_b_hh"]


def kernel(**inputs):
    import numpy as _np
    import concourse.bacc as _bacc
    from concourse import mybir as _mybir
    from concourse.bass_utils import run_bass_kernel_spmd as _run

    nc = _bacc.Bacc("TRN2", target_bir_lowering=False, num_devices=1)
    arrays, aps = {}, {}
    for name in _INS + _CONV + _REST:
        a = _np.ascontiguousarray(inputs[name])
        arrays[f"in_{name}_dram"] = a
        aps[name] = nc.dram_tensor(f"in_{name}_dram", a.shape, _mybir.dt.from_np(a.dtype), kind="ExternalInput").ap()
    shape = inputs["x"].shape
    out = nc.dram_tensor("out_0_dram", shape, _mybir.dt.from_np(_np.dtype("float32")), kind="ExternalOutput").ap()
    conv = [[aps[f"L1_gnn_l{layer}_{kind}{name}"] for layer in (1, 2)] for name in "qkvs" for kind in "wb"]
    gnn_kernel(nc, *(aps[n] for n in _INS), *conv, *(aps[n] for n in _REST), out)
    r = _run(nc, [arrays], core_ids=[0])
    return r.results[0]["out_0_dram"]
```
